# Optimizing a Trainium2 kernel written in Bass

```python
import numpy as np
import jax
import jax.numpy as jnp

def _softmax(x, axis=-1):
    return jax.nn.softmax(x, axis=axis)

def _gelu(x):
    return jax.nn.gelu(x, approximate=True)

def _silu(x):
    return jax.nn.silu(x)

def _sigmoid(x):
    return jax.nn.sigmoid(x)

def _layernorm(x, axis=-1, eps=1e-05):
    m = jnp.mean(x, axis=axis, keepdims=True)
    v = jnp.var(x, axis=axis, keepdims=True)
    return (x - m) / jnp.sqrt(v + eps)

def _scatter_add(tgt, idx, src, axis=0):
    return tgt.at[idx].add(src)

def _segment_sum(src, seg, n):
    return jax.ops.segment_sum(src, seg, n)
kernel_name = 'mk_macaron_d2_jaxref_r8_653c23'

def setup_inputs(seed: int=0):
    np.random.seed(seed)
    _w = jnp.asarray

    def _L0_attn_setup():
        import jax, jax.numpy as jnp
        import numpy as np
        B, T, E, H = (4, 256, 128, 16)
        S = E // H
        key = jax.random.key(seed)
        ks = jax.random.split(key, 4)
        x = jax.random.normal(ks[0], (B, T, E), dtype=jnp.float32)
        Wk = jax.random.normal(ks[1], (E, E), dtype=jnp.float32) * E ** (-0.5)
        Wq = jax.random.normal(ks[2], (E, E), dtype=jnp.float32) * E ** (-0.5)
        Wo = jax.random.normal(ks[3], (E, E), dtype=jnp.float32) * E ** (-0.5)
        bo = jnp.zeros((E,), dtype=jnp.float32)
        return {'x': x, 'Wk': Wk, 'Wq': Wq, 'Wo': Wo, 'bo': bo}
    _L0_attn_in = _L0_attn_setup()

    def _L0_ffn_setup():
        import jax, jax.numpy as jnp
        import numpy as np
        key = jax.random.key(seed)
        ks = jax.random.split(key, 4)
        B, T, M, E, F = (4, 256, 128, 8, 512)
        hidden_states = jax.random.normal(ks[0], (B, T, M), dtype=jnp.float32)
        wg = jax.random.normal(ks[1], (M, E), dtype=jnp.float32) * (1.0 / np.sqrt(M))
        w1 = jax.random.normal(ks[2], (E, M, F), dtype=jnp.float32) * (1.0 / np.sqrt(M))
        b1 = jnp.zeros((E, F), dtype=jnp.float32)
        w2 = jax.random.normal(ks[3], (E, F, M), dtype=jnp.float32) * (1.0 / np.sqrt(F))
        b2 = jnp.zeros((E, M), dtype=jnp.float32)
        return {'hidden_states': hidden_states, 'wg': wg, 'w1': w1, 'b1': b1, 'w2': w2, 'b2': b2}
    _L0_ffn_in = _L0_ffn_setup()

    def _L1_attn_setup():
        import jax, jax.numpy as jnp
        import numpy as np
        HEAD_SIZE = 64
        key = jax.random.key(seed)
        ks = jax.random.split(key, 5)
        B, N, D, H, E, O = (2, 256, 128, 16, HEAD_SIZE, 128)
        return {'query': jax.random.normal(ks[0], (B, N, D), dtype=jnp.float32), 'Wq': jax.random.normal(ks[1], (H, D, E), dtype=jnp.float32) / np.sqrt(D), 'Wk': jax.random.normal(ks[2], (H, D, E), dtype=jnp.float32) / np.sqrt(D), 'Wv': jax.random.normal(ks[3], (H, D, E), dtype=jnp.float32) / np.sqrt(D), 'Wp': jax.random.normal(ks[4], (H * E, O), dtype=jnp.float32) / np.sqrt(H * E), 'bp': jnp.zeros((O,), dtype=jnp.float32)}
    _L1_attn_in = _L1_attn_setup()

    def _L1_ffn_setup():
        import jax, jax.numpy as jnp
        import numpy as np
        TOP_K = 2
        key = jax.random.key(seed)
        k1, k2, k3, k4 = jax.random.split(key, 4)
        B, T, C = (4, 256, 128)
        E, D_FF = (8, 128)
        x = jax.random.normal(k1, (B, T, C), dtype=jnp.float32)
        router_w = jax.random.normal(k2, (E, C), dtype=jnp.float32) * 0.02
        w1 = jax.random.normal(k3, (E, C, D_FF), dtype=jnp.float32) * 0.02
        w2 = jax.random.normal(k4, (E, D_FF, C), dtype=jnp.float32) * 0.02
        return {'x': x, 'router_w': router_w, 'w1': w1, 'w2': w2}
    _L1_ffn_in = _L1_ffn_setup()
    _d = {'L0_attn_x': _L0_attn_in['x'], 'L0_attn_Wk': _L0_attn_in['Wk'], 'L0_attn_Wq': _L0_attn_in['Wq'], 'L0_attn_Wo': _L0_attn_in['Wo'], 'L0_attn_bo': _L0_attn_in['bo'], 'L0_ffn_wg': _L0_ffn_in['wg'], 'L0_ffn_w1': _L0_ffn_in['w1'], 'L0_ffn_b1': _L0_ffn_in['b1'], 'L0_ffn_w2': _L0_ffn_in['w2'], 'L0_ffn_b2': _L0_ffn_in['b2'], 'L1_attn_Wq': _L1_attn_in['Wq'], 'L1_attn_Wk': _L1_attn_in['Wk'], 'L1_attn_Wv': _L1_attn_in['Wv'], 'L1_attn_Wp': _L1_attn_in['Wp'], 'L1_attn_bp': _L1_attn_in['bp'], 'L1_ffn_router_w': _L1_ffn_in['router_w'], 'L1_ffn_w1': _L1_ffn_in['w1'], 'L1_ffn_w2': _L1_ffn_in['w2']}
    _x0 = _d['L0_attn_x']
    _d['L0_attn_x'] = jax.random.normal(jax.random.fold_in(jax.random.key(seed), 1), (1, 2048, 128), dtype=_x0.dtype)
    del _x0
    return _d

def reference(L0_attn_x, L0_attn_Wk, L0_attn_Wq, L0_attn_Wo, L0_attn_bo, L0_ffn_wg, L0_ffn_w1, L0_ffn_b1, L0_ffn_w2, L0_ffn_b2, L1_attn_Wq, L1_attn_Wk, L1_attn_Wv, L1_attn_Wp, L1_attn_bp, L1_ffn_router_w, L1_ffn_w1, L1_ffn_w2):

    def _L0_attn_ref(x, Wk, Wq, Wo, bo):
        import jax, jax.numpy as jnp
        import numpy as np
        B, T, E, H = (4, 256, 128, 16)
        S = E // H
        b, t, e = x.shape
        h, s = (H, E // H)
        scale = e ** (-0.25)
        k = (x @ Wk).reshape(b, t, h, s).transpose(0, 2, 1, 3)
        q = (x @ Wq).reshape(b, t, h, s).transpose(0, 2, 1, 3)
        v = (x @ Wk).reshape(b, t, h, s).transpose(0, 2, 1, 3)
        dot = jnp.einsum('bhqd,bhkd->bhqk', q * scale, k * scale)
        attn = jax.nn.softmax(dot, axis=-1)
        out = jnp.einsum('bhqk,bhkd->bhqd', attn, v)
        out = out.transpose(0, 2, 1, 3).reshape(b, t, e)
        return out @ Wo + bo

    def _L0_ffn_ref(hidden_states, wg, w1, b1, w2, b2):
        import jax, jax.numpy as jnp
        import numpy as np
        B, T, M = hidden_states.shape
        E = wg.shape[1]
        S = B * T
        MIN_CAPACITY = 4
        C = max((S + E - 1) // E, MIN_CAPACITY)
        x = hidden_states.reshape(S, M)
        logits = x @ wg
        gates = jax.nn.softmax(logits, axis=-1)
        idx = jnp.argmax(gates, axis=-1)
        mask1 = jax.nn.one_hot(idx, E, dtype=gates.dtype)
        l_aux = jnp.sum(gates.mean(0) * mask1.mean(0)) * E
        locations1 = jnp.cumsum(mask1, axis=0) - 1.0
        mask1 = mask1 * (locations1 < C)
        gates1_s = jnp.sum(gates * mask1, axis=1)
        loc_s = jnp.sum(locations1 * mask1, axis=1).astype(jnp.int32)
        loc_sc = jax.nn.one_hot(loc_s, C, dtype=gates.dtype)
        combine_weights = jnp.einsum('se,sc->sec', gates1_s[:, None] * mask1, loc_sc)
        dispatch_mask = (combine_weights > 0).astype(x.dtype)
        dispatched = jnp.einsum('sec,sm->ecm', dispatch_mask, x)
        h = jax.nn.gelu(jnp.einsum('ecm,emf->ecf', dispatched, w1) + b1[:, None, :])
        expert_out = jnp.einsum('ecf,efm->ecm', h, w2) + b2[:, None, :]
        out = jnp.einsum('sec,ecm->sm', combine_weights, expert_out)
        return out.reshape(B, T, M)

    def _L1_attn_ref(query, Wq, Wk, Wv, Wp, bp):
        import jax, jax.numpy as jnp
        import numpy as np
        HEAD_SIZE = 64
        B, N, D = query.shape
        H, _, E = Wq.shape
        scale = 1.0 / jnp.sqrt(jnp.asarray(E, query.dtype))
        q = jnp.einsum('bnd,hde->bhne', query, Wq) * scale
        k = jnp.einsum('bmd,hde->bhme', query, Wk)
        v = jnp.einsum('bmd,hde->bhme', query, Wv)
        logits = jnp.einsum('bhne,bhme->bhnm', q, k)
        attn = jax.nn.softmax(logits, axis=-1)
        out = jnp.einsum('bhnm,bhme->bnhe', attn, v)
        out = jnp.swapaxes(out, -1, -2).reshape(B, N, E * H)
        return jnp.dot(out, Wp) + bp

    def _L1_ffn_ref(x, router_w, w1, w2):
        import jax, jax.numpy as jnp
        import numpy as np
        TOP_K = 2
        B, T, C = x.shape
        x_flat = x.reshape(-1, C)
        logits = x_flat @ router_w.T
        probs = jax.nn.softmax(logits, axis=-1)
        weights, indices = jax.lax.top_k(probs, TOP_K)
        hidden = jax.nn.relu(jnp.einsum('nc,ecf->nef', x_flat, w1))
        out_all = jnp.einsum('nef,efc->nec', hidden, w2)
        sel = jnp.take_along_axis(out_all, indices[:, :, None], axis=1)
        out = jnp.sum(sel * weights[:, :, None], axis=1)
        return out.reshape(B, T, C)
    x = L0_attn_x
    x = x + 0.5 * _L0_ffn_ref(_layernorm(x, axis=-1), L0_ffn_wg, L0_ffn_w1, L0_ffn_b1, L0_ffn_w2, L0_ffn_b2)
    x = x + _L0_attn_ref(_layernorm(x, axis=-1), L0_attn_Wk, L0_attn_Wq, L0_attn_Wo, L0_attn_bo)
    x = x + 0.5 * _L0_ffn_ref(_layernorm(x, axis=-1), L0_ffn_wg, L0_ffn_w1, L0_ffn_b1, L0_ffn_w2, L0_ffn_b2)
    x = x + 0.5 * _L1_ffn_ref(_layernorm(x, axis=-1), L1_ffn_router_w, L1_ffn_w1, L1_ffn_w2)
    x = x + _L1_attn_ref(_layernorm(x, axis=-1), L1_attn_Wq, L1_attn_Wk, L1_attn_Wv, L1_attn_Wp, L1_attn_bp)
    x = x + 0.5 * _L1_ffn_ref(_layernorm(x, axis=-1), L1_ffn_router_w, L1_ffn_w1, L1_ffn_w2)
    return x

_drawn_inputs = setup_inputs


def setup_inputs(seed=0):
    import zlib

    import numpy as np

    out = dict(_drawn_inputs(seed))
    spreads = {'L0_attn_bo': (0.0, 0.1),
     'L0_ffn_b1': (0.0, 0.299),
     'L0_ffn_b2': (0.0, 0.1),
     'L1_attn_bp': (0.0, 0.1)}
    factors = {'L1_ffn_router_w': 8.0, 'L1_ffn_w1': 8.0, 'L1_ffn_w2': 7.307}
    for name, (base, spread) in spreads.items():
        noise = np.random.default_rng([zlib.crc32(name.encode()), seed]).standard_normal(out[name].shape)
        drawn = base * np.exp(spread * noise) if base else spread * noise
        out[name] = jnp.asarray(drawn.astype(out[name].dtype))
    for name, factor in factors.items():
        out[name] = (out[name] * factor).astype(out[name].dtype)
    return out
```

```python
from contextlib import ExitStack

import concourse.bass as bass
from concourse import mybir

ALU = mybir.AluOpType
ACT = mybir.ActivationFunctionType
X_AXIS = mybir.AxisListType.X
F32 = mybir.dt.float32
F32R = mybir.dt.float32r
BF16 = mybir.dt.bfloat16
I32 = mybir.dt.int32
RMAX = bass.bass_isa.ReduceOp.max
RADD = bass.bass_isa.ReduceOp.add

P = 128
S = 2048
M = 128
NT = S // P
CH = 512
NCH = S // CH
TPC = CH // P
E = 8
F0 = 512
FT = F0 // P
CAP = S // E
EPS = 1e-5
SAFE_ARGUMENT = 60.0


def broadcast_last(ap, n):
    return ap.unsqueeze(2).to_broadcast([ap.shape[0], ap.shape[1], n])


class Kernel:

    def __init__(self, nc, ctx, dram):
        self.nc, self.dram = nc, dram

        def sb(name, shape, dt=F32):
            return ctx.enter_context(nc.sbuf_tensor(name, shape, dt))

        self.ps = ctx.enter_context(nc.psum_tensor("banks", [P, 8, CH], F32))
        self.x = sb("x_tokens", [P, NT, M])
        self.xnT = sb("xn_transposed", [M, S])
        self.ident = sb("ident", [P, P])
        self.ones = sb("ones", [P, P])
        self.ones_r = sb("ones_r", [P, P], F32R)
        self.ones_b = sb("ones_b", [P, P], BF16)
        self.earlier = sb("earlier_tokens", [P, P], BF16)
        self.rank = sb("expert_rank", [P, NT, E])
        self.base_slot = sb("base_slot", [P, E, NT])
        self.scan_keep = sb("scan_keep", [P, E, NT + 1])
        self.slot_of_row = sb("slot_of_row", [P, NT])
        self.eps = sb("eps", [P, 1])


def constants(k):
    nc = k.nc
    with ExitStack() as ctx:
        x_loaded = nc.alloc_semaphore("x_loaded")
        filled = nc.alloc_semaphore("const_filled")
        block = ctx.enter_context(nc.Block())

        @block.sync
        def _(sp):
            sp.dma_start(k.x[:], k.dram["x"].rearrange("b (t p) m -> p (b t) m", p=P)).then_inc(x_loaded, 16)
            sp.wait_ge(x_loaded, 16)

        @block.vector
        def _(dve):
            nc.vector.memset(k.ones_r[:].bitcast(F32), 1.0)
            nc.vector.memset(k.ones_b[:], 1.0)
            for e in range(E):
                nc.vector.memset(k.rank[:, :, e], float(E - e))
                nc.vector.memset(k.base_slot[:, e, :], float(e * CAP))
            nc.vector.memset(k.eps[:], EPS)

        @block.gpsimd
        def _(pool):
            nc.gpsimd.memset(k.ident[:], 0.0).then_inc(filled, 1)
            nc.gpsimd.memset(k.ones[:], 1.0).then_inc(filled, 1)
            nc.gpsimd.memset(k.scan_keep[:], 1.0).then_inc(filled, 1)
            nc.gpsimd.iota(k.slot_of_row[:], [[P, NT]], base=0, channel_multiplier=1,
                           allow_small_or_imprecise_dtypes=True)
            pool.wait_ge(filled, 3)
            nc.gpsimd.affine_select(out=k.ident[:], in_=k.ident[:], compare_op=ALU.not_equal, fill=1.0,
                                    base=0, pattern=[[-1, P]], channel_multiplier=1)
            nc.gpsimd.affine_select(out=k.earlier[:], in_=k.ones[:], compare_op=ALU.is_gt, fill=0.0,
                                    base=0, pattern=[[1, P]], channel_multiplier=-1)
            nc.gpsimd.memset(k.scan_keep[:, :, 0], 0.0)


def layernorm(k, xn, tag):
    nc, ps = k.nc, k.ps
    with ExitStack() as ctx:
        def sb(name, shape, dt=F32):
            return ctx.enter_context(nc.sbuf_tensor(f"s_{name}_{tag}", shape, dt))

        def sem(name):
            return nc.alloc_semaphore(f"{name}_{tag}")

        stats = sb("ln_stats", [P, NT, 6])
        mv = sb("ln_mean_var", [P, NT, 2])
        var = sb("ln_var", [P, NT])
        std = sb("ln_std", [P, NT])
        rstd = sb("ln_rstd", [P, NT])
        newton = sb("ln_newton", [P, NT])
        dve_step, var_ready, std_ready = sem("ln_dve_step"), sem("ln_var_ready"), sem("ln_std_ready")
        xn_ready, transposed = sem("ln_xn_ready"), sem("ln_transposed")
        block = ctx.enter_context(nc.Block())

        @block.vector
        def _(dve):
            done = [0]

            def link(ins):
                done[0] += 1
                ins.then_inc(dve_step, 1)
                dve.wait_ge(dve_step, done[0])

            for t in range(NT):
                last = nc.vector.bn_stats(stats[:, t, :], k.x[:, t, :])
            link(last)
            for t in range(NT):
                last = nc.vector.bn_aggr(mv[:, t, :], stats[:, t, :])
            link(last)
            nc.vector.tensor_scalar(var[:], mv[:, :, 1], EPS, None, ALU.add).then_inc(var_ready, 1)
            dve.wait_ge(std_ready, 1)
            link(nc.vector.reciprocal(rstd[:], std[:]))
            link(nc.vector.tensor_tensor(newton[:], rstd[:], rstd[:], ALU.mult))
            link(nc.vector.tensor_tensor(newton[:], newton[:], var[:], ALU.mult))
            link(nc.vector.tensor_scalar(newton[:], newton[:], -0.5, 1.5, ALU.mult, ALU.add))
            link(nc.vector.tensor_tensor(rstd[:], rstd[:], newton[:], ALU.mult))
            for t in range(NT):
                nc.vector.tensor_scalar(xn[:, t, :], k.x[:, t, :], mv[:, t, 0:1], rstd[:, t:t + 1],
                                        ALU.subtract, ALU.mult).then_inc(xn_ready, 1)

        @block.scalar
        def _(act):
            act.wait_ge(var_ready, 1)
            nc.scalar.activation(std[:], var[:], ACT.Sqrt).then_inc(std_ready, 1)
            for c in range(NCH):
                act.wait_ge(transposed, c + 1)
                nc.scalar.activation(k.xnT[:, c * CH:(c + 1) * CH], ps[:, c, :], ACT.Copy)

        @block.tensor
        def _(pe):
            for t in range(NT):
                pe.wait_ge(xn_ready, t + 1)
                ins = nc.tensor.transpose(ps[:, t // TPC, (t % TPC) * P:(t % TPC + 1) * P], xn[:, t, :], k.ident[:])
                if t % TPC == TPC - 1:
                    ins.then_inc(transposed, 1)


def moe_top1(k, tag):
    nc, ps, d = k.nc, k.ps, k.dram
    with ExitStack() as ctx:
        def sb(name, shape, dt=F32):
            return ctx.enter_context(nc.sbuf_tensor(f"s_{name}_{tag}", shape, dt))

        def sem(name):
            return nc.alloc_semaphore(f"{name}_{tag}")

        xn = sb("t1_xn", [P, NT, M])
        layernorm(k, xn, tag)

        w1 = sb("t1_w1", [M, E, F0])
        w2 = sb("t1_w2", [P, E, FT, M])
        b1 = sb("t1_b1", [P, E, FT])
        b2 = sb("t1_b2", [1, E, M])
        wg = sb("t1_wg", [M, E])
        xn_hi = sb("t1_xn_hi", [P, NT, M], F32R)
        xn_lo = sb("t1_xn_lo", [P, NT, M], F32R)
        shifted = sb("t1_shifted", [P, NT, E])
        ex = sb("t1_ex", [P, NT, E])
        score = sb("t1_score", [P, NT, E])
        stat = sb("t1_stat", [P, 12, NT])
        mask = sb("t1_mask", [P, E, NT + 1], BF16)
        before = sb("t1_before", [P, E, NT + 1], BF16)
        own = sb("t1_own", [P, E, NT])
        own_base = sb("t1_own_base", [P, E, NT])
        slot_diag = sb("t1_slot_diag", [P, NT, P], F32R)
        slot_row = sb("t1_slot_row", [P, S])
        slot_iota = sb("t1_slot_iota", [P, S])
        onehot = sb("t1_onehot", [P, 2, S], F32R)
        xdT = sb("t1_dispatched", [M, S])
        hT = sb("t1_hidden", [P, 2, FT, CAP])
        eo_hi = sb("t1_expert_hi", [P, NT, M], F32R)
        eo_lo = sb("t1_expert_lo", [P, NT, M], F32R)
        (row_max, row_sum, best_ex, r_sum, gate, best_rank, cnt_own, base_own, keep, slot, slot_kept,
         half_gate) = [stat[:, i, :] for i in range(12)]

        w_loaded, w1_loaded, w2_loaded = sem("t1_w_loaded"), sem("t1_w1_loaded"), sem("t1_w2_loaded")
        dve_step, mask_zero, iota_ready = sem("t1_dve_step"), sem("t1_mask_zero"), sem("t1_iota_ready")
        logits_ready, shift_ready, ex_ready = sem("t1_logits_ready"), sem("t1_shift_ready"), sem("t1_ex_ready")
        mask_ready, counts_ready, diag_ready = sem("t1_mask_ready"), sem("t1_counts_ready"), sem("t1_diag_ready")
        row_in_psum, row_ready = sem("t1_row_in_psum"), sem("t1_row_ready")
        hi_ready, lo_ready = sem("t1_hi_ready"), sem("t1_lo_ready")
        onehot_ready, onehot_used = sem("t1_onehot_ready"), sem("t1_onehot_used")
        gathered, xd_ready = sem("t1_gathered"), sem("t1_xd_ready")
        up_done, hidden_ready, down_done = sem("t1_up_done"), sem("t1_hidden_ready"), sem("t1_down_done")
        eo_ready, back, back_ready, tokens_back = (sem("t1_eo_ready"), sem("t1_back"), sem("t1_back_ready"),
                                                   sem("t1_tokens_back"))
        block = ctx.enter_context(nc.Block())

        @block.sync
        def _(sp):
            sp.dma_start(wg[:], d["t1_wg"]).then_inc(w_loaded, 16)
            sp.dma_start(w1[:], d["t1_w1"].rearrange("e m f -> m e f")).then_inc(w1_loaded, 16)
            sp.dma_start(w2[:], d["t1_w2"].rearrange("e (t f) m -> f e t m", f=P)).then_inc(w2_loaded, 16)
            with nc.allow_non_contiguous_dma(reason="the biases, one per hidden unit's partition"):
                sp.dma_start(b1[:], d["t1_b1"].rearrange("e (t f) -> f e t", f=P)).then_inc(w2_loaded, 16)
            sp.dma_start(b2[:], d["t1_b2"].rearrange("(a e) m -> a e m", a=1)).then_inc(w2_loaded, 16)

        @block.gpsimd
        def _(pool):
            nc.gpsimd.memset(mask[:, :, 0], 0.0).then_inc(mask_zero, 1)
            nc.gpsimd.iota(slot_iota[:], [[1, S]], base=0, channel_multiplier=0,
                           allow_small_or_imprecise_dtypes=True).then_inc(iota_ready, 1)
            pool.wait_ge(hi_ready, 1)
            nc.gpsimd.tensor_tensor(xn_lo[:], xn[:], xn_hi[:].bitcast(F32), ALU.subtract).then_inc(lo_ready, 1)

        @block.scalar
        def _(act):
            nc.scalar.activation(xn_hi[:], xn[:], ACT.Copy).then_inc(hi_ready, 1)
            act.wait_ge(shift_ready, 1)
            nc.scalar.activation(ex[:], shifted[:], ACT.Exp).then_inc(ex_ready, 1)
            for c in range(NCH):
                act.wait_ge(row_in_psum, c + 1)
                nc.scalar.activation(slot_row[:, c * CH:(c + 1) * CH], ps[:, c, :], ACT.Copy).then_inc(row_ready, 1)
            for c in range(NCH):
                act.wait_ge(gathered, c + 1)
                nc.scalar.activation(xdT[:, c * CH:(c + 1) * CH], ps[:, 4 + c, :], ACT.Copy).then_inc(xd_ready, 1)
            act.wait_ge(w2_loaded, 48)
            for e in range(E):
                if e >= 2:
                    act.wait_ge(down_done, e - 1)
                for f in range(FT):
                    act.wait_ge(up_done, e * 2 + f // 2 + 1)
                    bank = (e % 2) * 2 + f // 2
                    nc.scalar.activation(hT[:, e % 2, f, :], ps[:, bank, (f % 2) * CAP:(f % 2 + 1) * CAP],
                                         ACT.Gelu_apprx_tanh, bias=b1[:, e, f:f + 1]).then_inc(hidden_ready, 1)
            for c in range(NCH):
                act.wait_ge(back, c + 1)
                nc.scalar.activation(xdT[:, c * CH:(c + 1) * CH], ps[:, c, :], ACT.Copy).then_inc(back_ready, 1)

        @block.vector
        def _(dve):
            done = [0]

            def link(ins):
                done[0] += 1
                ins.then_inc(dve_step, 1)
                dve.wait_ge(dve_step, done[0])

            logits = ps[:, 0, 0:NT * E].rearrange("p (t e) -> p t e", e=E)
            dve.wait_ge(logits_ready, 1)
            link(nc.vector.tensor_reduce(row_max, logits, X_AXIS, ALU.max))
            nc.vector.tensor_tensor(shifted[:], logits, broadcast_last(row_max, E), ALU.subtract)\
                .then_inc(shift_ready, 1)
            dve.wait_ge(ex_ready, 1)
            nc.vector.tensor_reduce(row_sum, ex[:], X_AXIS, ALU.add)
            link(nc.vector.tensor_reduce(best_ex, ex[:], X_AXIS, ALU.max))
            nc.vector.reciprocal(r_sum, row_sum)
            link(nc.vector.tensor_tensor(score[:], ex[:], broadcast_last(best_ex, E), ALU.is_equal))
            nc.vector.tensor_tensor(gate, best_ex, r_sum, ALU.mult)
            link(nc.vector.tensor_tensor(score[:], score[:], k.rank[:], ALU.mult))
            link(nc.vector.tensor_reduce(best_rank, score[:], X_AXIS, ALU.max))
            nc.vector.tensor_scalar(half_gate, gate, 0.5, None, ALU.mult)
            dve.wait_ge(mask_zero, 1)
            link(nc.vector.tensor_tensor(mask[:, :, 1:NT + 1].rearrange("p e t -> p t e"), score[:],
                                         broadcast_last(best_rank, E), ALU.is_equal))
            nc.vector.tensor_tensor_scan(before[:].rearrange("p e t -> p (e t)"),
                                         k.scan_keep[:].rearrange("p e t -> p (e t)"),
                                         mask[:].rearrange("p e t -> p (e t)"), 0.0, ALU.mult, ALU.add)\
                .then_inc(mask_ready, 1)
            counts = ps[:, 1, 0:E * NT].rearrange("p (e t) -> p e t", e=E)
            nc.vector.tensor_tensor(own_base[:], k.base_slot[:], mask[:, :, 1:NT + 1], ALU.mult)
            dve.wait_ge(counts_ready, 1)
            link(nc.vector.tensor_tensor(own[:], counts, mask[:, :, 1:NT + 1], ALU.mult))
            nc.vector.tensor_reduce(base_own, own_base[:].rearrange("p e t -> p t e"), X_AXIS, ALU.add)
            link(nc.vector.tensor_reduce(cnt_own, own[:].rearrange("p e t -> p t e"), X_AXIS, ALU.add))
            nc.vector.tensor_scalar(keep, cnt_own, float(CAP), None, ALU.is_lt)
            link(nc.vector.tensor_tensor(slot, cnt_own, base_own, ALU.add))
            link(nc.vector.scalar_tensor_tensor(out=slot, in0=slot, scalar=1.0, in1=keep, op0=ALU.add, op1=ALU.mult))
            link(nc.vector.tensor_scalar(slot_kept, slot, -1.0, None, ALU.add))
            nc.vector.tensor_tensor(slot_diag[:], k.ident[:].unsqueeze(1).to_broadcast([P, NT, P]),
                                    broadcast_last(slot_kept, P), ALU.mult).then_inc(diag_ready, 1)
            dve.wait_ge(iota_ready, 1)
            for t in range(NT):
                if t >= 2:
                    dve.wait_ge(onehot_used, t - 1)
                nc.vector.tensor_scalar(onehot[:, t % 2, :], slot_iota[:], slot_kept[:, t:t + 1], None,
                                        ALU.is_equal).then_inc(onehot_ready, 1)

            def expert_out(e):
                dve.wait_ge(down_done, e + 1)
                rows = ps[:, 4 + e % 4, 0:2 * M].rearrange("p (t m) -> p t m", m=M)
                link(nc.vector.tensor_copy(eo_hi[:, 2 * e:2 * e + 2, :], rows))
                nc.vector.tensor_tensor(eo_lo[:, 2 * e:2 * e + 2, :], rows,
                                        eo_hi[:, 2 * e:2 * e + 2, :].bitcast(F32), ALU.subtract).then_inc(eo_ready, 1)

            def onehot_back(j):
                if j == 1:
                    dve.wait_ge(gathered, NCH)
                else:
                    dve.wait_ge(onehot_used, NT - 1 if j == 0 else NT - 1 + j - 1)
                nc.vector.tensor_scalar(onehot[:, j % 2, :], slot_row[:], k.slot_of_row[:, j:j + 1], None,
                                        ALU.is_equal).then_inc(onehot_ready, 1)

            dve.wait_ge(row_ready, NCH)
            onehot_back(0)
            onehot_back(1)
            for e in range(E):
                expert_out(e)
            for j in range(2, NT):
                onehot_back(j)
            for t in range(NT):
                dve.wait_ge(tokens_back, t // TPC + 1)
                nc.vector.scalar_tensor_tensor(out=k.x[:, t, :], in0=ps[:, 4 + t // TPC, (t % TPC) * P:(t % TPC + 1) * P],
                                               scalar=half_gate[:, t:t + 1], in1=k.x[:, t, :],
                                               op0=ALU.mult, op1=ALU.add)

        @block.tensor
        def _(pe):
            pe.wait_ge(w_loaded, 16)
            for t in range(NT):
                last = nc.tensor.matmul(ps[:, 0, t * E:(t + 1) * E], k.xnT[:, t * P:(t + 1) * P], wg[:],
                                        start=True, stop=True)
            last.then_inc(logits_ready, 1)
            pe.wait_ge(mask_ready, 1)
            counts = ps[:, 1, 0:E * NT]
            nc.tensor.matmul(counts, k.earlier[:], mask[:, :, 1:NT + 1], start=True, stop=False)
            nc.tensor.matmul(counts, k.ones_b[:], before[:, :, 0:NT], start=False, stop=True)\
                .then_inc(counts_ready, 1)
            pe.wait_ge(diag_ready, 1)
            for c in range(NCH):
                nc.tensor.matmul(ps[:, c, :], k.ones_r[:], slot_diag[:, c * TPC:(c + 1) * TPC, :],
                                 start=True, stop=True).then_inc(row_in_psum, 1)
            pe.wait_ge(lo_ready, 1)
            for t in range(NT):
                pe.wait_ge(onehot_ready, t + 1)
                for part, rows in enumerate((xn_hi, xn_lo)):
                    for c in range(NCH):
                        last = nc.tensor.matmul(ps[:, 4 + c, :], rows[:, t, :], onehot[:, t % 2, c * CH:(c + 1) * CH],
                                                start=(t == 0 and part == 0), stop=(t == NT - 1 and part == 1))
                        if t == NT - 1 and part == 1:
                            last.then_inc(gathered, 1)
                if t < NT - 1:
                    last.then_inc(onehot_used, 1)
            pe.wait_ge(w1_loaded, 16)
            pe.wait_ge(w2_loaded, 48)
            pe.wait_ge(row_ready, NCH)

            def up(e):
                if e % 2 == 0:
                    pe.wait_ge(xd_ready, e // 2 + 1)
                if e >= 2:
                    pe.wait_ge(hidden_ready, (e - 1) * FT)
                for f in range(FT):
                    bank = (e % 2) * 2 + f // 2
                    last = nc.tensor.matmul(ps[:, bank, (f % 2) * CAP:(f % 2 + 1) * CAP],
                                            w1[:, e, f * P:(f + 1) * P], xdT[:, e * CAP:(e + 1) * CAP],
                                            start=True, stop=True)
                    if f % 2:
                        last.then_inc(up_done, 1)

            def down(e):
                pe.wait_ge(hidden_ready, (e + 1) * FT)
                if e < 4:
                    pe.wait_ge(xd_ready, NCH)
                else:
                    pe.wait_ge(eo_ready, e - 3)
                for half in range(2):
                    out = ps[:, 4 + e % 4, half * M:(half + 1) * M]
                    for f in range(FT):
                        nc.tensor.matmul(out, hT[:, e % 2, f, half * P:(half + 1) * P], w2[:, e, f, :],
                                         start=(f == 0), stop=False)
                    last = nc.tensor.matmul(out, k.ones[0:1, :], b2[:, e, :], start=False, stop=True)
                last.then_inc(down_done, 1)

            up(0)
            for e in range(E):
                if e + 1 < E:
                    up(e + 1)
                down(e)
            pe.wait_ge(hidden_ready, E * FT)
            for j in range(NT):
                pe.wait_ge(onehot_ready, NT + j + 1)
                pe.wait_ge(eo_ready, j // 2 + 1)
                for part, rows in enumerate((eo_hi, eo_lo)):
                    for c in range(NCH):
                        last = nc.tensor.matmul(ps[:, c, :], rows[:, j, :], onehot[:, j % 2, c * CH:(c + 1) * CH],
                                                start=(j == 0 and part == 0), stop=(j == NT - 1 and part == 1))
                        if j == NT - 1 and part == 1:
                            last.then_inc(back, 1)
                if j < NT - 1:
                    last.then_inc(onehot_used, 1)
            for t in range(NT):
                pe.wait_ge(back_ready, t // TPC + 1)
                if t == 0:
                    pe.wait_ge(eo_ready, E)
                last = nc.tensor.transpose(ps[:, 4 + t // TPC, (t % TPC) * P:(t % TPC + 1) * P],
                                           xdT[:, t * P:(t + 1) * P], k.ident[:])
                if t % TPC == TPC - 1:
                    last.then_inc(tokens_back, 1)


def moe_top2(k, tag):
    nc, ps, d = k.nc, k.ps, k.dram
    with ExitStack() as ctx:
        def sb(name, shape, dt=F32):
            return ctx.enter_context(nc.sbuf_tensor(f"s_{name}_{tag}", shape, dt))

        def sem(name):
            return nc.alloc_semaphore(f"{name}_{tag}")

        xn = sb("t2_xn", [P, NT, M])
        layernorm(k, xn, tag)

        w1 = sb("t2_w1", [M, E, P])
        w2 = sb("t2_w2", [P, E, M])
        wr = sb("t2_router", [M, E])
        shifted = sb("t2_shifted", [P, NT, E])
        ex = sb("t2_ex", [P, NT, E])
        rest = sb("t2_rest", [P, NT, E])
        score = sb("t2_score", [P, NT, E])
        first = sb("t2_first", [P, NT, E])
        second = sb("t2_second", [P, NT, E])
        weight = sb("t2_weight", [P, NT, E])
        stat = sb("t2_stat", [P, 8, NT])
        hidden = sb("t2_hidden", [P, 4, CH])
        row_max, row_sum, best_ex, r_sum, best_rank, next_ex, next_rank, half = [stat[:, i, :] for i in range(8)]

        w_loaded, dve_step = sem("t2_w_loaded"), sem("t2_dve_step")
        logits_ready, shift_ready, ex_ready = sem("t2_logits_ready"), sem("t2_shift_ready"), sem("t2_ex_ready")
        up_done, hidden_ready, down_done, added = (sem("t2_up_done"), sem("t2_hidden_ready"), sem("t2_down_done"),
                                                   sem("t2_added"))
        block = ctx.enter_context(nc.Block())
        steps = [(c, e) for c in range(NCH) for e in range(E)]

        @block.sync
        def _(sp):
            sp.dma_start(wr[:], d["t2_router"]).then_inc(w_loaded, 16)
            sp.dma_start(w1[:], d["t2_w1"].rearrange("e m f -> m e f")).then_inc(w_loaded, 16)
            sp.dma_start(w2[:], d["t2_w2"].rearrange("e f m -> f e m")).then_inc(w_loaded, 16)

        @block.scalar
        def _(act):
            act.wait_ge(shift_ready, 1)
            nc.scalar.activation(ex[:], shifted[:], ACT.Exp).then_inc(ex_ready, 1)
            for n in range(len(steps)):
                act.wait_ge(up_done, n + 1)
                if n >= 4:
                    act.wait_ge(down_done, n - 3)
                nc.scalar.activation(hidden[:, n % 4, :], ps[:, n % 4, :], ACT.Relu).then_inc(hidden_ready, 1)

        @block.vector
        def _(dve):
            done = [0]

            def link(ins):
                done[0] += 1
                ins.then_inc(dve_step, 1)
                dve.wait_ge(dve_step, done[0])

            logits = ps[:, 7, 0:NT * E].rearrange("p (t e) -> p t e", e=E)
            dve.wait_ge(logits_ready, 1)
            link(nc.vector.tensor_reduce(row_max, logits, X_AXIS, ALU.max))
            nc.vector.tensor_tensor(shifted[:], logits, broadcast_last(row_max, E), ALU.subtract)\
                .then_inc(shift_ready, 1)
            dve.wait_ge(ex_ready, 1)
            nc.vector.tensor_reduce(row_sum, ex[:], X_AXIS, ALU.add)
            link(nc.vector.tensor_reduce(best_ex, ex[:], X_AXIS, ALU.max))
            nc.vector.reciprocal(r_sum, row_sum)
            link(nc.vector.tensor_tensor(score[:], ex[:], broadcast_last(best_ex, E), ALU.is_equal))
            link(nc.vector.tensor_tensor(score[:], score[:], k.rank[:], ALU.mult))
            link(nc.vector.tensor_reduce(best_rank, score[:], X_AXIS, ALU.max))
            link(nc.vector.tensor_tensor(first[:], score[:], broadcast_last(best_rank, E), ALU.is_equal))
            link(nc.vector.tensor_tensor(rest[:], ex[:], first[:], ALU.mult))
            link(nc.vector.tensor_tensor(rest[:], ex[:], rest[:], ALU.subtract))
            link(nc.vector.tensor_tensor(rest[:], rest[:], first[:], ALU.subtract))
            link(nc.vector.tensor_reduce(next_ex, rest[:], X_AXIS, ALU.max))
            link(nc.vector.tensor_tensor(score[:], rest[:], broadcast_last(next_ex, E), ALU.is_equal))
            link(nc.vector.tensor_tensor(score[:], score[:], k.rank[:], ALU.mult))
            link(nc.vector.tensor_reduce(next_rank, score[:], X_AXIS, ALU.max))
            nc.vector.tensor_scalar(half, r_sum, 0.5, None, ALU.mult)
            link(nc.vector.tensor_tensor(second[:], score[:], broadcast_last(next_rank, E), ALU.is_equal))
            link(nc.vector.tensor_tensor(first[:], first[:], second[:], ALU.add))
            link(nc.vector.tensor_tensor(weight[:], first[:], ex[:], ALU.mult))
            link(nc.vector.tensor_tensor(weight[:], weight[:], broadcast_last(half, E), ALU.mult))
            for n, (c, e) in enumerate(steps):
                dve.wait_ge(down_done, n + 1)
                if n >= 1:
                    dve.wait_ge(added, n)
                for i in range(TPC):
                    t = c * TPC + i
                    last = nc.vector.scalar_tensor_tensor(
                        out=k.x[:, t, :], in0=ps[:, 4 + n % 3, i * P:(i + 1) * P], scalar=weight[:, t, e:e + 1],
                        in1=k.x[:, t, :], op0=ALU.mult, op1=ALU.add)
                last.then_inc(added, 1)

        @block.tensor
        def _(pe):
            pe.wait_ge(w_loaded, 48)
            for t in range(NT):
                last = nc.tensor.matmul(ps[:, 7, t * E:(t + 1) * E], k.xnT[:, t * P:(t + 1) * P], wr[:],
                                        start=True, stop=True)
            last.then_inc(logits_ready, 1)

            def up(n):
                c, e = steps[n]
                if n >= 4:
                    pe.wait_ge(hidden_ready, n - 3)
                nc.tensor.matmul(ps[:, n % 4, :], w1[:, e, :], k.xnT[:, c * CH:(c + 1) * CH],
                                 start=True, stop=True).then_inc(up_done, 1)

            def down(n):
                c, e = steps[n]
                pe.wait_ge(hidden_ready, n + 1)
                if n >= 3:
                    pe.wait_ge(added, n - 2)
                for i in range(TPC):
                    last = nc.tensor.matmul(ps[:, 4 + n % 3, i * P:(i + 1) * P], hidden[:, n % 4, i * P:(i + 1) * P],
                                            w2[:, e, :], start=True, stop=True)
                last.then_inc(down_done, 1)

            up(0)
            up(1)
            for n in range(len(steps)):
                if n + 2 < len(steps):
                    up(n + 2)
                down(n)


def store(k):
    nc = k.nc
    with ExitStack() as ctx:
        stored = nc.alloc_semaphore("stored")
        block = ctx.enter_context(nc.Block())

        @block.sync
        def _(sp):
            sp.dma_start(k.dram["out"].rearrange("b (t p) m -> p (b t) m", p=P), k.x[:]).then_inc(stored, 16)
            sp.wait_ge(stored, 16)


def attention_small(k):
    nc, ps, d = k.nc, k.ps, k.dram
    H, D, G = 16, 8, 4
    NG = H // G
    PARTS = 3
    ROWS = PARTS * PARTS * D
    SCALE = float(M) ** -0.5
    W = P // G
    JT = NT * G // 2
    NI = NG * NCH
    RING, PROBS = 3, 4
    TURNS = 2
    ACC, EPI = 6, 7
    q_dram = nc.dram_tensor("a0_q_parts", (H, PARTS, D, S), BF16, kind="Internal").ap()
    k_dram = nc.dram_tensor("a0_k_parts", (H, PARTS, D, S), BF16, kind="Internal").ap()

    with ExitStack() as ctx:
        def sb(name, shape, dt=F32):
            return ctx.enter_context(nc.sbuf_tensor(f"s_a0_{name}", shape, dt))

        def sem(name):
            return nc.alloc_semaphore(f"a0_{name}")

        safe = sb("safe", [H, 1], I32)
        values = sb("values", [P, NT, M])
        v_strip = sb("v_strip", [P, 2, NT, G, W])
        wo = sb("wo_strips", [P, NG, M])
        sum_row = sb("sum_row", [P, P])

        with ExitStack() as prep:
            def psb(name, shape, dt=F32):
                return prep.enter_context(nc.sbuf_tensor(f"s_a0_{name}", shape, dt))

            def psem(name):
                return sem(name)

            xn = psb("xn", [P, NT, M])
            layernorm(k, xn, "a0")
            wq, wk = psb("wq", [M, M]), psb("wk", [M, M])
            bo = psb("bo", [P, M])
            qk = psb("qk", [P, 2, S])
            part = psb("part", [P, 2, PARTS, S], BF16)
            square = psb("square", [P, 2 * NCH, CH], BF16)
            head_rows = psb("head_rows", [P, H], BF16)
            norm = psb("norm", [H, 2 * NCH])
            most = psb("most", [H, 4])
            w_loaded, bo_loaded = psem("w_loaded"), psem("bo_loaded")
            wo_zero, wo_loaded, filled = psem("wo_zero"), psem("wo_loaded"), psem("filled")
            projected, copied, squared = psem("projected"), psem("copied"), psem("squared")
            v_projected, normed, norm_read = psem("v_projected"), psem("normed"), psem("norm_read")
            split, stored, dve_step, product, reduced = (psem("split"), psem("stored"), psem("dve_step"),
                                                         psem("product"), psem("reduced"))
            block = prep.enter_context(nc.Block())

            @block.sync
            def _(sp):
                sp.dma_start(wq[:], d["a0_wq"]).then_inc(w_loaded, 16)
                sp.dma_start(wk[:], d["a0_wk"]).then_inc(w_loaded, 16)
                sp.dma_start(bo[:], d["a0_bo"].partition_broadcast(P)).then_inc(bo_loaded, 16)
                sp.wait_ge(wo_zero, 1)
                for h in range(G):
                    sp.dma_start(wo[W * h:W * h + D, :, :],
                                 d["a0_wo"].rearrange("(g h d) n -> h d g n", g=NG, h=G)[h]).then_inc(wo_loaded, 16)
                for side, dram in enumerate((q_dram, k_dram)):
                    for i in range(PARTS):
                        sp.wait_ge(split, side * PARTS + i + 1)
                        sp.dma_start(dram[:, i, :, :], part[:, side, i, :]).then_inc(stored, 16)
                sp.wait_ge(stored, 2 * PARTS * 16)
                sp.wait_ge(wo_loaded, G * 16)

            @block.gpsimd
            def _(pool):
                nc.gpsimd.memset(wo[:], 0.0).then_inc(wo_zero, 1)
                nc.gpsimd.memset(head_rows[:], 1.0).then_inc(filled, 1)
                nc.gpsimd.memset(sum_row[:], 0.0).then_inc(filled, 1)
                nc.gpsimd.memset(v_strip[:], 0.0).then_inc(filled, 1)
                pool.wait_ge(filled, 3)
                nc.gpsimd.affine_select(out=head_rows[:], in_=head_rows[:], compare_op=ALU.is_ge, fill=0.0,
                                        base=0, pattern=[[-D, H]], channel_multiplier=1).then_inc(filled, 1)
                pool.wait_ge(filled, 4)
                nc.gpsimd.affine_select(out=head_rows[:], in_=head_rows[:], compare_op=ALU.is_ge, fill=0.0,
                                        base=D - 1, pattern=[[D, H]], channel_multiplier=-1).then_inc(filled, 1)
                nc.gpsimd.affine_select(out=sum_row[:], in_=sum_row[:], compare_op=ALU.not_equal, fill=1.0,
                                        base=-D, pattern=[[-W, G], [0, W]], channel_multiplier=1)
                nc.gpsimd.memset(v_strip[:, :, :, :, D], 1.0)
                pool.wait_ge(bo_loaded, 16)
                nc.gpsimd.tensor_tensor(k.x[:], k.x[:], bo[:].unsqueeze(1).to_broadcast([P, NT, M]), ALU.add)
                pool.wait_ge(product, 1)
                nc.gpsimd.partition_all_reduce(most[:, 3:4], most[:, 2:3], H, RMAX).then_inc(reduced, 1)

            @block.scalar
            def _(act):
                for n in range(2 * NCH):
                    act.wait_ge(projected, n + 1)
                    nc.scalar.activation(qk[:, n // NCH, (n % NCH) * CH:(n % NCH + 1) * CH], ps[:, n, :],
                                         ACT.Copy).then_inc(copied, 1)
                    nc.scalar.activation(square[:, n, :], ps[:, n, :], ACT.Square).then_inc(squared, 1)
                for c in range(NCH):
                    act.wait_ge(v_projected, c + 1)
                    nc.scalar.activation(values[:, c * TPC:(c + 1) * TPC, :], ps[:, c, :], ACT.Copy)

            @block.vector
            def _(dve):
                done = [0]

                def link(ins):
                    done[0] += 1
                    ins.then_inc(dve_step, 1)
                    dve.wait_ge(dve_step, done[0])

                for side in range(2):
                    dve.wait_ge(copied, (side + 1) * NCH)
                    for i in range(PARTS):
                        nc.vector.tensor_copy(part[:, side, i, :], qk[:, side, :]).then_inc(split, 1)
                        dve.wait_ge(split, side * PARTS + i + 1)
                        if i < PARTS - 1:
                            link(nc.vector.tensor_tensor(qk[:, side, :], qk[:, side, :], part[:, side, i, :],
                                                         ALU.subtract))
                for n in range(2 * NCH):
                    dve.wait_ge(normed, n + 1)
                    nc.vector.tensor_reduce(norm[:, n:n + 1], ps[0:H, 4 + n % 4, :], X_AXIS, ALU.max)\
                        .then_inc(norm_read, 1)
                dve.wait_ge(norm_read, 2 * NCH)
                link(nc.vector.tensor_reduce(most[:, 0:2], norm[:].rearrange("h (s c) -> h s c", s=2), X_AXIS, ALU.max))
                nc.vector.tensor_tensor(most[:, 2:3], most[:, 0:1], most[:, 1:2], ALU.mult).then_inc(product, 1)
                dve.wait_ge(reduced, 1)
                nc.vector.tensor_scalar(safe[:], most[:, 3:4], 1.0625 * SCALE * SCALE, SAFE_ARGUMENT ** 2,
                                        ALU.mult, ALU.is_le)

            @block.tensor
            def _(pe):
                pe.wait_ge(w_loaded, 32)
                for n in range(2 * NCH):
                    c = n % NCH
                    nc.tensor.matmul(ps[:, n, :], (wq, wk)[n // NCH][:], k.xnT[:, c * CH:(c + 1) * CH],
                                     start=True, stop=True).then_inc(projected, 1)
                for t in range(NT):
                    pe.wait_ge(squared, t // TPC + 1)
                    last = nc.tensor.matmul(ps[:, t // TPC, (t % TPC) * P:(t % TPC + 1) * P],
                                            k.xnT[:, t * P:(t + 1) * P], wk[:], start=True, stop=True)
                    if t % TPC == TPC - 1:
                        last.then_inc(v_projected, 1)
                pe.wait_ge(squared, 2 * NCH)
                pe.wait_ge(filled, 5)
                for n in range(2 * NCH):
                    if n >= 4:
                        pe.wait_ge(norm_read, n - 3)
                    nc.tensor.matmul(ps[0:H, 4 + n % 4, :], head_rows[:], square[:, n, :], start=True, stop=True)\
                        .then_inc(normed, 1)

        k_rows = sb("k_rows", [ROWS, 2, G, S], BF16)
        q_rows = sb("q_rows", [ROWS, 2, G, S], BF16)
        probs = sb("probs", [P, PROBS, 2, CH])
        weighted = sb("weighted", [P, CH])
        inverse = sb("inverse", [P, CH])
        attended = sb("attended", [P, CH])
        running_max = sb("running_max", [P, CH])
        minus_max = sb("minus_max", [P, TPC])
        shift = sb("shift", [P, G, TPC, P])

        loaded = sem("loaded")
        v_ready, score_done, exp_done, pv_done = sem("v_ready"), sem("score_done"), sem("exp_done"), sem("pv_done")
        acc_copied, sums_done, inverse_ready, attended_ready, out_done, x_added = (
            sem("acc_copied"), sem("sums_done"), sem("inverse_ready"), sem("attended_ready"), sem("out_done"),
            sem("x_added"))
        max_score, max_taken, max_turned, max_read, shift_ready = (
            sem("max_score"), sem("max_taken"), sem("max_turned"), sem("max_read"), sem("shift_ready"))
        LOADS = PARTS * PARTS + PARTS
        block = ctx.enter_context(nc.Block())

        @block.sync
        def _(sp):
            for g in range(NG):
                if g >= 1:
                    sp.wait_ge(loaded, g * (LOADS * 16))
                if g >= 2:
                    sp.wait_ge(pv_done, NCH * (g - 1) * JT + PROBS)
                for b in range(PARTS):
                    for a in range(PARTS):
                        r = (b * PARTS + a) * D
                        sp.dma_start(k_rows[r:r + D, g % 2, :, :],
                                     k_dram[g * G:(g + 1) * G, b].rearrange("h d t -> d h t"))\
                            .then_inc(loaded, 16)
                    r = b * PARTS * D
                    sp.dma_start(q_rows[r:r + PARTS * D, g % 2, :, :],
                                 q_dram[g * G:(g + 1) * G].rearrange("h a d t -> (a d) h t"))\
                        .then_inc(loaded, 16)

        @block.scalar
        def _(act):
            act.sem_inc(exp_done, RING)
            with act.Fori(0, NG) as g:
                for n in range(NCH * JT):
                    act.wait_ge(score_done, g * (NCH * JT) + (n + 1))
                    act.wait_ge(pv_done, g * (NCH * JT) + (n + 1))
                    bank = 2 * (n % JT % RING)
                    nc.scalar.activation(probs[:, n % PROBS, :, :], ps[:, bank:bank + 2, :],
                                         ACT.Exp, scale=SCALE).then_inc(exp_done, 1)

        def dve_program(dve, guarded):
            def strip_values(g, slot):
                nc.vector.tensor_copy(v_strip[:, slot, :, :, 0:D],
                                      values[:, :, bass.ds(g * (G * D), G * D)].rearrange("p t (h d) -> p t h d", d=D))\
                    .then_inc(v_ready, 1)

            def row_maxima(it):
                for n in range(G * NT):
                    h, kt = n // NT, n % NT
                    dve.wait_ge(max_score, it * (G * NT) + (n + 1))
                    if kt == 0:
                        ins = nc.vector.tensor_copy(running_max[:], ps[:, n % 2, :])
                    else:
                        ins = nc.vector.tensor_tensor(running_max[:], ps[:, n % 2, :], running_max[:], ALU.max)
                    ins.then_inc(max_taken, 1)
                    dve.wait_ge(max_taken, it * (G * NT) + (n + 1 + TURNS))
                    if kt == NT - 1:
                        dve.wait_ge(max_turned, it * G + (h + 1))
                        nc.vector.tensor_reduce(minus_max[:], ps[:, 2, :].rearrange("p (i k) -> p i k", i=TPC),
                                                X_AXIS, ALU.max, negate=True).then_inc(max_read, 1)
                        dve.wait_ge(max_read, it * G + (h + 2))
                        for i in range(TPC):
                            ins = nc.vector.tensor_scalar(shift[:, h, i, :], k.ident[:], minus_max[:, i:i + 1], None,
                                                          ALU.mult)
                        ins.then_inc(shift_ready, 1)

            def epilogue(it, qc):
                dve.wait_ge(pv_done, (it + 1) * JT + PROBS)
                nc.vector.tensor_copy(weighted[:], ps[:, ACC, :]).then_inc(acc_copied, 1)
                dve.wait_ge(sums_done, it + 1)
                nc.vector.reciprocal(inverse[:], ps[:, EPI, :]).then_inc(inverse_ready, 1)
                dve.wait_ge(inverse_ready, it + 1)
                nc.vector.tensor_tensor(attended[:], weighted[:], inverse[:], ALU.mult).then_inc(attended_ready, 1)
                dve.wait_ge(out_done, it + 1)
                rows = k.x[:, bass.ds(qc * TPC, TPC), :]
                nc.vector.tensor_tensor(rows, rows, ps[:, EPI, :].rearrange("p (i m) -> p i m", m=M), ALU.add)\
                    .then_inc(x_added, 1)

            strip_values(0, 0)
            with dve.Fori(0, NG // 2) as gg:
                for par in range(2):
                    g = gg * 2 + par
                    strip_values((g + 1) % NG, 1 - par)
                    with dve.Fori(0, NCH) as qc:
                        if guarded:
                            row_maxima(g * NCH + qc)
                        epilogue(g * NCH + qc, qc)

        @block.vector
        def _(dve):
            dve.sem_inc(max_taken, TURNS)
            is_safe = dve.value_load(safe[0:1, 0:1], min_val=0, max_val=1)
            with dve.If(is_safe == 1):
                dve_program(dve, guarded=False)
            with dve.Else():
                dve_program(dve, guarded=True)

        def pe_program(pe, guarded):
            def score(out, slot, h, kt, q0, last):
                k_flat = k_rows[:].rearrange("r b h t -> r (b h t)")
                q_flat = q_rows[:].rearrange("r b h t -> r (b h t)")
                return nc.tensor.matmul(out, k_flat[:, bass.ds(slot * (G * S) + (h * S + kt * P), P)],
                                        q_flat[:, bass.ds(slot * (G * S) + (h * S + q0), CH)], start=True, stop=last)

            def scores(it, par, qc, j):
                kt, pair = j // 2, j % 2
                before = j - RING if j >= RING else max(t for t in range(JT) if t % RING == j) - JT
                pe.wait_ge(exp_done, it * JT + (before + 1 + RING))
                for hh in range(2):
                    bank = 2 * (j % RING) + hh
                    ins = score(ps[:, bank, :], par, 2 * pair + hh, kt, qc * CH, not guarded)
                    if guarded:
                        ins = nc.tensor.matmul(ps[:, bank, :], k.ones[:], shift[:, 2 * pair + hh, :, :],
                                               start=False, stop=True)
                ins.then_inc(score_done, 1)

            def weigh(it, par, j):
                kt, pair = j // 2, j % 2
                pe.wait_ge(exp_done, it * JT + (j + 1 + RING))
                if j == 0:
                    pe.wait_ge(acc_copied, it + 1)
                for hh in range(2):
                    h = 2 * pair + hh
                    last = nc.tensor.matmul(ps[W * h:W * (h + 1), ACC, :], v_strip[:, par, kt, h, :],
                                            probs[:, j % PROBS, hh, :], start=(kt == 0), stop=(kt == NT - 1))
                last.then_inc(pv_done, 1)

            def sums(n):
                pe.wait_ge(acc_copied, n + 1)
                pe.wait_ge(x_added, n)
                nc.tensor.matmul(ps[:, EPI, :], sum_row[:], weighted[:], start=True, stop=True).then_inc(sums_done, 1)

            def project(n, g):
                pe.wait_ge(attended_ready, n)
                for i in range(TPC):
                    last = nc.tensor.matmul(ps[:, EPI, i * P:(i + 1) * P], attended[:, i * P:(i + 1) * P],
                                            wo[:, :, :].rearrange("p g m -> p (g m)")[:, bass.ds(g * M, M)],
                                            start=True, stop=True)
                last.then_inc(out_done, 1)

            def row_maxima(it, par, qc):
                pe.wait_ge(exp_done, it * JT + RING)
                for n in range(G * NT):
                    h, kt = n // NT, n % NT
                    pe.wait_ge(max_taken, it * (G * NT) + (n + 1))
                    score(ps[:, n % 2, :], par, h, kt, qc * CH, True).then_inc(max_score, 1)
                    if kt == NT - 1:
                        pe.wait_ge(max_taken, it * (G * NT) + (n + 1 + TURNS))
                        pe.wait_ge(max_read, it * G + (h + 1))
                        for i in range(TPC):
                            last = nc.tensor.transpose(ps[:, 2, i * P:(i + 1) * P], running_max[:, i * P:(i + 1) * P],
                                                       k.ident[:])
                        last.then_inc(max_turned, 1)
                pe.wait_ge(shift_ready, it * G + G)

            if not guarded:
                pe.wait_ge(loaded, LOADS * 16)
                for j in range(RING):
                    scores(0, 0, 0, j)
            with pe.Fori(0, NG // 2) as gg:
                for par in range(2):
                    g = gg * 2 + par
                    with pe.Fori(0, NCH) as qc:
                        pe.wait_ge(v_ready, g + 1)
                        it = g * NCH + qc
                        if guarded:
                            pe.wait_ge(loaded, (g + 1) * (LOADS * 16))
                            row_maxima(it, par, qc)
                            for j in range(RING):
                                scores(it, par, qc, j)
                        for j in range(JT):
                            if j + RING < JT:
                                scores(it, par, qc, j + RING)
                            weigh(it, par, j)
                            if not guarded and j + RING >= JT:
                                group = (it + 1) // NCH % NG
                                if j + RING == JT:
                                    pe.wait_ge(loaded, (group + 1) * (LOADS * 16))
                                scores(it + 1, group % 2, (qc + 1) % NCH, j + RING - JT)
                            if not guarded and j == 4:
                                with pe.If(it > 0):
                                    sums(it)
                            if not guarded and j == 10:
                                with pe.If(it > 0):
                                    project(it, (it + NI - 1) // NCH % NG)
                        if guarded:
                            sums(it + 1)
                            project(it + 1, g)
            if not guarded:
                sums(NI)
                project(NI, NG - 1)

        @block.tensor
        def _(pe):
            pe.sem_inc(pv_done, PROBS)
            pe.sem_inc(x_added, 1)
            pe.sem_inc(acc_copied, 1)
            pe.sem_inc(max_read, 1)
            is_safe = pe.value_load(safe[0:1, 0:1], min_val=0, max_val=1)
            with pe.If(is_safe == 1):
                pe_program(pe, guarded=False)
            with pe.Else():
                pe_program(pe, guarded=True)


def attention_wide(k):
    nc, ps, d = k.nc, k.ps, k.dram
    H, D = 16, 64
    NP = H // 2
    SCALE = float(D) ** -0.5
    NI = NP * NCH
    RING, PROBS = 2, 8
    ACC, EPI, QV, KB = 4, 5, 6, 7
    ADDS = NT - 2

    with ExitStack() as ctx:
        def sb(name, shape, dt=F32):
            return ctx.enter_context(nc.sbuf_tensor(f"s_a1_{name}", shape, dt))

        def sem(name):
            return nc.alloc_semaphore(f"a1_{name}")

        safe = sb("safe", [H, 1], I32)
        w_all = sb("w_all", [M, 3, H, D])
        wp = sb("wp", [P, NP, M])

        with ExitStack() as prep:
            def psb(name, shape, dt=F32):
                return prep.enter_context(nc.sbuf_tensor(f"s_a1_{name}", shape, dt))

            def psem(name):
                return sem(name)

            xn = psb("xn", [P, NT, M])
            layernorm(k, xn, "a1")
            bp = psb("bp", [P, M])
            x_hi = psb("x_hi", [M, S], F32R)
            w_hi = psb("w_hi", [M, 2, NP, P], F32R)
            w_square = psb("w_square", [M, 2, H * D], BF16)
            square = psb("square", [P, 4, CH], BF16)
            head_rows = psb("head_rows", [P, NP, H], BF16)
            norm = psb("norm", [H, 2 * NCH])
            norm2 = psb("norm2", [H, 8])
            w_norm = psb("w_norm", [P, 4])
            w_loaded, wp_loaded, bp_loaded = psem("w_loaded"), psem("wp_loaded"), psem("bp_loaded")
            filled, hi_ready, w_squared, w_reduced = psem("filled"), psem("hi_ready"), psem("w_squared"), psem("w_reduced")
            projected, squared, normed, norm_read = psem("projected"), psem("squared"), psem("normed"), psem("norm_read")
            dve_step, most_ready, reduced = psem("dve_step"), psem("most_ready"), psem("reduced")
            steps = [(side, c, p) for side in range(2) for c in range(NCH) for p in range(NP)]
            block = prep.enter_context(nc.Block())

            @block.sync
            def _(sp):
                for i, name in enumerate(("a1_wq", "a1_wk", "a1_wv")):
                    sp.dma_start(w_all[:, i, :, :], d[name].rearrange("h m e -> m h e")).then_inc(w_loaded, 16)
                sp.dma_start(bp[:], d["a1_bp"].partition_broadcast(P)).then_inc(bp_loaded, 16)
                for s in range(2):
                    sp.dma_start(wp[D * s:D * (s + 1), :, :],
                                 d["a1_wp"].rearrange("(e p s) o -> s e p o", p=NP, s=2)[s]).then_inc(wp_loaded, 16)
                sp.wait_ge(wp_loaded, 32)

            @block.gpsimd
            def _(pool):
                nc.gpsimd.memset(head_rows[:], 0.0).then_inc(filled, 1)
                pool.wait_ge(filled, 1)
                for s in range(2):
                    half = head_rows[D * s:D * (s + 1), :, :]
                    nc.gpsimd.affine_select(out=half, in_=half, compare_op=ALU.not_equal, fill=1.0,
                                            base=-s, pattern=[[-2, NP], [1, H]], channel_multiplier=0)\
                        .then_inc(filled, 1)
                pool.wait_ge(filled, 3)
                pool.wait_ge(bp_loaded, 16)
                nc.gpsimd.tensor_tensor(k.x[:], k.x[:], bp[:].unsqueeze(1).to_broadcast([P, NT, M]), ALU.add)
                pool.wait_ge(w_squared, 2)
                nc.gpsimd.partition_all_reduce(w_norm[:, 2:4], w_norm[:, 0:2], P, RADD).then_inc(w_reduced, 1)
                pool.wait_ge(most_ready, 1)
                nc.gpsimd.partition_all_reduce(norm2[:, 2:4], norm2[:, 0:2], H, RMAX).then_inc(reduced, 1)

            @block.scalar
            def _(act):
                act.wait_ge(w_loaded, 48)
                for side in range(2):
                    nc.scalar.activation(w_square[:, side, :], w_all[:, side, :, :].rearrange("m h e -> m (h e)"),
                                         ACT.Square, accum_out=w_norm[:, side:side + 1]).then_inc(w_squared, 1)
                for n in range(len(steps)):
                    act.wait_ge(projected, n + 1)
                    if n >= 4:
                        act.wait_ge(normed, n - 3)
                    nc.scalar.activation(square[:, n % 4, :], ps[:, n % 4, :], ACT.Square).then_inc(squared, 1)

            @block.vector
            def _(dve):
                done = [0]

                def link(ins):
                    done[0] += 1
                    ins.then_inc(dve_step, 1)
                    dve.wait_ge(dve_step, done[0])

                nc.vector.tensor_copy(x_hi[:], k.xnT[:])
                dve.wait_ge(w_loaded, 48)
                nc.vector.tensor_copy(w_hi[:].rearrange("m s p r -> m s (p r)"),
                                      w_all[:, 0:2, :, :].rearrange("m s h e -> m s (h e)")).then_inc(hi_ready, 1)
                for n in range(2 * NCH):
                    dve.wait_ge(normed, (n + 1) * NP)
                    nc.vector.tensor_reduce(norm[:, n:n + 1], ps[0:H, 4 + n % 4, :], X_AXIS, ALU.max)\
                        .then_inc(norm_read, 1)
                dve.wait_ge(norm_read, 2 * NCH)
                nc.vector.tensor_reduce(norm2[:, 0:2], norm[:].rearrange("h (s c) -> h s c", s=2), X_AXIS, ALU.max)\
                    .then_inc(most_ready, 1)
                dve.wait_ge(reduced, 1)
                dve.wait_ge(w_reduced, 1)
                link(nc.vector.tensor_scalar(norm2[:, 4:6], norm2[:, 2:4], 1.07, None, ALU.mult))
                link(nc.vector.scalar_tensor_tensor(out=norm2[:, 4:6], in0=w_norm[0:H, 2:4],
                                                    scalar=18.0 * M * 2.0 ** -22, in1=norm2[:, 4:6],
                                                    op0=ALU.mult, op1=ALU.add))
                link(nc.vector.tensor_tensor(norm2[:, 6:7], norm2[:, 4:5], norm2[:, 5:6], ALU.mult))
                nc.vector.tensor_scalar(safe[:], norm2[:, 6:7], SCALE * SCALE, SAFE_ARGUMENT ** 2,
                                        ALU.mult, ALU.is_le)

            @block.tensor
            def _(pe):
                def head_norms(n):
                    side, c, p = steps[n]
                    group = side * NCH + c
                    pe.wait_ge(squared, n + 1)
                    if group >= 4 and p == 0:
                        pe.wait_ge(norm_read, group - 3)
                    nc.tensor.matmul(ps[0:H, 4 + group % 4, :], head_rows[:, p, :], square[:, n % 4, :],
                                     start=(p == 0), stop=(p == NP - 1)).then_inc(normed, 1)

                pe.wait_ge(hi_ready, 1)
                pe.wait_ge(filled, 3)
                for n, (side, c, p) in enumerate(steps):
                    if n >= 4:
                        pe.wait_ge(squared, n - 3)
                    nc.tensor.matmul(ps[:, n % 4, :], w_hi[:, side, p, :], x_hi[:, c * CH:(c + 1) * CH],
                                     start=True, stop=True).then_inc(projected, 1)
                    if n >= 2:
                        head_norms(n - 2)
                head_norms(len(steps) - 2)
                head_norms(len(steps) - 1)

        k_rows = sb("k_rows", [P, 2, 2, S], F32R)
        q_rows = sb("q_rows", [P, 2, 2, 2, CH], F32R)
        values = sb("values", [P, 2, NT, P])
        probs = sb("probs", [P, PROBS, 2, CH])
        part_sum = sb("part_sum", [P, 2, 2, CH])
        weight_sum = sb("weight_sum", [P, 2, CH])
        wq_now, wk_now, wv_now = sb("wq_now", [M, P]), sb("wk_now", [M, P]), sb("wv_now", [M, P])
        x_now = sb("x_now", [M, CH])
        weighted = sb("weighted", [P, CH])
        inverse = sb("inverse", [P, CH])
        attended = sb("attended", [P, CH])
        running_max = sb("running_max", [P, CH])
        minus_max = sb("minus_max", [P, TPC])
        shift = sb("shift", [P, 2, TPC, P])

        def hi_halves(rows, source, order):
            out = []
            for s in range(2):
                half = s ^ order
                out.append((rows(s, order)[D * half:D * (half + 1)], source[D * s:D * (s + 1)]))
            return out

        def lo_halves(rows, source, order):
            out = []
            for s in range(2):
                half = s ^ order
                out.append((rows(s, order)[D * (1 - half):D * (2 - half)], source[D * s:D * (s + 1)],
                            rows(s, 0)[D * s:D * (s + 1)]))
            return out

        def q_at(slot):
            flat = q_rows[:].rearrange("p i s o c -> p (i s o c)")
            return lambda s, order: flat[:, bass.ds(slot * (4 * CH) + (2 * s + order) * CH, CH)]

        def k_at(par, c0):
            return lambda s, order: k_rows[:, par, s, bass.ds(c0, CH)]

        with ExitStack() as first:
            def fsem(name):
                return sem(name)

            k_proj, q_proj, v_proj = fsem("first_k_proj"), fsem("first_q_proj"), fsem("first_v_proj")
            hi_done, lo_done = fsem("first_hi_done"), fsem("first_lo_done")
            v_done = fsem("first_v_done")
            block = first.enter_context(nc.Block())

            def halves(fn):
                out = [(c, fn(k_at(0, c * CH), ps[:, c, :], 0)) for c in range(NCH)]
                out.append((NCH, fn(q_at(0), ps[:, NCH, :], 0) + fn(q_at(0), ps[:, NCH, :], 1)))
                return out

            @block.tensor
            def _(pe):
                for c in range(NCH):
                    nc.tensor.matmul(ps[:, c, :], w_all[:, 1, 0:2, :], k.xnT[:, c * CH:(c + 1) * CH],
                                     start=True, stop=True).then_inc(k_proj, 1)
                nc.tensor.matmul(ps[:, NCH, :], w_all[:, 0, 0:2, :], k.xnT[:, 0:CH],
                                 start=True, stop=True).then_inc(k_proj, 1)
                for t in range(NT):
                    bank = 5 + (t // TPC) % 3
                    if t == 3 * TPC:
                        pe.wait_ge(v_done, 1)
                    last = nc.tensor.matmul(ps[:, bank, (t % TPC) * P:(t % TPC + 1) * P], k.xnT[:, t * P:(t + 1) * P],
                                            w_all[:, 2, 0:2, :], start=True, stop=True)
                    if t % TPC == TPC - 1:
                        last.then_inc(v_proj, 1)

            @block.scalar
            def _(act):
                for n, (bank, ops) in enumerate(halves(hi_halves)):
                    act.wait_ge(k_proj, n + 1)
                    for dst, src in ops:
                        last = nc.scalar.activation(dst, src, ACT.Copy)
                    last.then_inc(hi_done, 1)
                for c in range(NCH):
                    act.wait_ge(v_proj, c + 1)
                    nc.scalar.activation(values[:, 0, c * TPC:(c + 1) * TPC, :], ps[:, 5 + c % 3, :], ACT.Copy)\
                        .then_inc(v_done, 1)

            @block.vector
            def _(dve):
                for n, (bank, ops) in enumerate(halves(lo_halves)):
                    dve.wait_ge(hi_done, n + 1)
                    for dst, src, hi in ops:
                        nc.vector.tensor_tensor(dst, src, hi.bitcast(F32), ALU.subtract)

        v_out, q_hi, k_hi, q_lo, k_lo = sem("v_out"), sem("q_hi"), sem("k_hi"), sem("q_lo"), sem("k_lo")
        q_proj, k_proj, v_proj, staged = sem("q_proj"), sem("k_proj"), sem("v_proj"), sem("staged")
        score_done, exp_done, pv_done, summed = sem("score_done"), sem("exp_done"), sem("pv_done"), sem("summed")
        total_ready, acc_copied, sums_done, inverse_ready = (sem("total_ready"), sem("acc_copied"), sem("sums_done"),
                                                             sem("inverse_ready"))
        attended_ready, out_done, x_added = sem("attended_ready"), sem("out_done"), sem("x_added")
        max_score, max_taken, max_turned, max_read, shift_ready = (
            sem("max_score"), sem("max_taken"), sem("max_turned"), sem("max_read"), sem("shift_ready"))
        block = ctx.enter_context(nc.Block())

        def pairs(eng):
            with eng.Fori(0, NP // 2) as pp:
                for par in range(2):
                    with eng.Fori(0, NCH) as qc:
                        pair = pp * 2 + par
                        yield pair, par, qc, pair * NCH + qc

        def additions_over(t):
            return t + 1 if t < 2 else t - 1

        @block.gpsimd
        def _(pool):
            for pair, par, qc, it in pairs(pool):
                pool.wait_ge(v_proj, it + 1)
                flat = w_all[:].rearrange("m w h e -> m w (h e)")
                nc.gpsimd.tensor_copy(wq_now[:], flat[:, 0, bass.ds((it + 1) // NCH % NP * P, P)])
                nc.gpsimd.tensor_copy(wk_now[:], flat[:, 1, bass.ds((pair + 1) % NP * P, P)])
                nc.gpsimd.tensor_copy(wv_now[:], flat[:, 2, bass.ds((pair + 1) % NP * P, P)])
                nc.gpsimd.tensor_copy(x_now[:], k.xnT[:, bass.ds(qc * CH, CH)]).then_inc(staged, 1)

        @block.scalar
        def _(act):
            act.sem_inc(exp_done, RING)
            for pair, par, qc, it in pairs(act):
                for j in range(NT):
                    act.wait_ge(score_done, it * NT + (j + 1))
                    act.wait_ge(pv_done, it * NT + (j + 1))
                    taken = additions_over(j - PROBS) + ADDS if j >= PROBS else additions_over(NT + j - PROBS)
                    act.wait_ge(summed, it * ADDS + taken)
                    nc.scalar.activation(probs[:, j % PROBS, :, :], ps[:, 2 * (j % RING):2 * (j % RING) + 2, :],
                                         ACT.Exp, scale=SCALE).then_inc(exp_done, 1)
                    if j in (3, 4):
                        if j == 3:
                            act.wait_ge(q_proj, it + 1)
                        for dst, src in hi_halves(q_at((it + 1) % 2), ps[:, QV, :], j - 3):
                            nc.scalar.activation(dst, src, ACT.Copy).then_inc(q_hi, 1)
                    if j in (6, 7):
                        if j == 6:
                            act.wait_ge(k_proj, it + 1)
                        dst, src = hi_halves(k_at(1 - par, qc * CH), ps[:, KB, :], 0)[j - 6]
                        nc.scalar.activation(dst, src, ACT.Copy).then_inc(k_hi, 1)
                    if j == 12:
                        act.wait_ge(v_proj, it + 2)
                        nc.scalar.activation(values[:, 1 - par, bass.ds(qc * TPC, TPC), :], ps[:, QV, :], ACT.Copy)\
                            .then_inc(v_out, 1)

        def dve_program(dve, guarded):
            def row_maxima(it):
                for n in range(2 * NT):
                    s, kt = n // NT, n % NT
                    dve.wait_ge(max_score, it * (2 * NT) + (n + 1))
                    if kt == 0:
                        ins = nc.vector.tensor_copy(running_max[:], ps[:, n % 2, :])
                    else:
                        ins = nc.vector.tensor_tensor(running_max[:], ps[:, n % 2, :], running_max[:], ALU.max)
                    ins.then_inc(max_taken, 1)
                    dve.wait_ge(max_taken, it * (2 * NT) + (n + 1 + RING))
                    if kt == NT - 1:
                        dve.wait_ge(max_turned, it * 2 + (s + 1))
                        nc.vector.tensor_reduce(minus_max[:], ps[:, 2, :].rearrange("p (i k) -> p i k", i=TPC),
                                                X_AXIS, ALU.max, negate=True).then_inc(max_read, 1)
                        dve.wait_ge(max_read, it * 2 + (s + 2))
                        for i in range(TPC):
                            ins = nc.vector.tensor_scalar(shift[:, s, i, :], k.ident[:], minus_max[:, i:i + 1], None,
                                                          ALU.mult)
                        ins.then_inc(shift_ready, 1)

            def take_weighted(n):
                dve.wait_ge(pv_done, n * NT + PROBS)
                nc.vector.tensor_copy(weighted[:], ps[:, ACC, :]).then_inc(acc_copied, 1)

            def divide(n):
                dve.wait_ge(sums_done, n)
                nc.vector.reciprocal(inverse[:], ps[:, EPI, :]).then_inc(inverse_ready, 1)
                dve.wait_ge(inverse_ready, n)
                nc.vector.tensor_tensor(attended[:], weighted[:], inverse[:], ALU.mult).then_inc(attended_ready, 1)

            def add_to_x(n, qc):
                dve.wait_ge(out_done, n)
                rows = k.x[:, bass.ds(qc * TPC, TPC), :]
                nc.vector.tensor_tensor(rows, rows, ps[:, EPI, :].rearrange("p (i m) -> p i m", m=M), ALU.add)\
                    .then_inc(x_added, 1)

            for pair, par, qc, it in pairs(dve):
                if guarded:
                    row_maxima(it)
                else:
                    with dve.If(it > 0):
                        take_weighted(it)
                dve.wait_ge(total_ready, it + 1)
                for j in range(2, NT):
                    dve.wait_ge(exp_done, it * NT + (j + 1 + RING))
                    if j < 4:
                        other = probs[:, (j - 2) % PROBS, :, :]
                    else:
                        dve.wait_ge(summed, it * ADDS + (ADDS + j - 3))
                        other = part_sum[:, j % 2, :, :]
                    nc.vector.tensor_tensor(part_sum[:, j % 2, :, :], probs[:, j % PROBS, :, :], other, ALU.add)\
                        .then_inc(summed, 1)
                    if j == 3 and not guarded:
                        with dve.If(it > 0):
                            divide(it)
                    if j in (5, 6):
                        dve.wait_ge(q_hi, it * 4 + (2 * j - 8))
                        for dst, src, hi in lo_halves(q_at((it + 1) % 2), ps[:, QV, :], j - 5):
                            last = nc.vector.tensor_tensor(dst, src, hi.bitcast(F32), ALU.subtract)
                        if j == 6:
                            last.then_inc(q_lo, 1)
                    if j in (8, 9):
                        dve.wait_ge(k_hi, it * 2 + (j - 7))
                        dst, src, hi = lo_halves(k_at(1 - par, qc * CH), ps[:, KB, :], 0)[j - 8]
                        last = nc.vector.tensor_tensor(dst, src, hi.bitcast(F32), ALU.subtract)
                        if j == 9:
                            last.then_inc(k_lo, 1)
                    if j == 12 and not guarded:
                        with dve.If(it > 0):
                            add_to_x(it, (qc + NCH - 1) % NCH)
                dve.wait_ge(summed, it * ADDS + 2 * ADDS)
                nc.vector.tensor_tensor(weight_sum[:], part_sum[:, 0, :, :], part_sum[:, 1, :, :], ALU.add)\
                    .then_inc(total_ready, 1)
                if guarded:
                    take_weighted(it + 1)
                    divide(it + 1)
                    add_to_x(it + 1, qc)
            if not guarded:
                take_weighted(NI)
                divide(NI)
                add_to_x(NI, NCH - 1)

        @block.vector
        def _(dve):
            dve.sem_inc(max_taken, RING)
            dve.sem_inc(summed, ADDS)
            dve.sem_inc(total_ready, 1)
            is_safe = dve.value_load(safe[0:1, 0:1], min_val=0, max_val=1)
            with dve.If(is_safe == 1):
                dve_program(dve, guarded=False)
            with dve.Else():
                dve_program(dve, guarded=True)

        def pe_program(pe, guarded):
            def score(out, par, s, kt, it, last):
                for order in range(2):
                    ins = nc.tensor.matmul(out, k_rows[:, par, s, kt * P:(kt + 1) * P], q_at(it % 2)(s, order),
                                           start=(order == 0), stop=(order == 1 and last))
                return ins

            def scores(it, par, j):
                pe.wait_ge(exp_done, it * NT + (j + 1))
                for s in range(2):
                    bank = 2 * (j % RING) + s
                    ins = score(ps[:, bank, :], par, s, j, it, not guarded)
                    if guarded:
                        ins = nc.tensor.matmul(ps[:, bank, :], k.ones[:], shift[:, s, :, :], start=False, stop=True)
                ins.then_inc(score_done, 1)

            def weigh(it, par, j):
                pe.wait_ge(exp_done, it * NT + (j + 1 + RING))
                if j == 0:
                    pe.wait_ge(acc_copied, it + 1)
                for s in range(2):
                    last = nc.tensor.matmul(ps[D * s:D * (s + 1), ACC, :], values[:, par, j, D * s:D * (s + 1)],
                                            probs[:, j % PROBS, s, :], start=(j == 0), stop=(j == NT - 1))
                last.then_inc(pv_done, 1)

            def sums(n):
                pe.wait_ge(total_ready, n + 1)
                pe.wait_ge(x_added, n)
                for s in range(2):
                    last = nc.tensor.matmul(ps[D * s:D * (s + 1), EPI, :], k.ones[:, 0:D], weight_sum[:, s, :],
                                            start=True, stop=True)
                last.then_inc(sums_done, 1)

            def project(n, pair):
                pe.wait_ge(attended_ready, n)
                for i in range(TPC):
                    last = nc.tensor.matmul(ps[:, EPI, i * P:(i + 1) * P], attended[:, i * P:(i + 1) * P],
                                            wp[:].rearrange("p g m -> p (g m)")[:, bass.ds(pair * M, M)],
                                            start=True, stop=True)
                last.then_inc(out_done, 1)

            def row_maxima(it, par):
                pe.wait_ge(exp_done, it * NT + RING)
                for n in range(2 * NT):
                    s, kt = n // NT, n % NT
                    pe.wait_ge(max_taken, it * (2 * NT) + (n + 1))
                    score(ps[:, n % 2, :], par, s, kt, it, True).then_inc(max_score, 1)
                    if kt == NT - 1:
                        pe.wait_ge(max_taken, it * (2 * NT) + (n + 1 + RING))
                        pe.wait_ge(max_read, it * 2 + (s + 1))
                        for i in range(TPC):
                            last = nc.tensor.transpose(ps[:, 2, i * P:(i + 1) * P], running_max[:, i * P:(i + 1) * P],
                                                       k.ident[:])
                        last.then_inc(max_turned, 1)
                pe.wait_ge(shift_ready, it * 2 + 2)

            def operands_ready(it):
                pe.wait_ge(q_lo, it + 1)
                pe.wait_ge(k_lo, it + 1)

            if not guarded:
                operands_ready(0)
                for j in range(RING):
                    scores(0, 0, j)
            for pair, par, qc, it in pairs(pe):
                pe.wait_ge(v_out, it + 1)
                if guarded:
                    operands_ready(it)
                    row_maxima(it, par)
                    for j in range(RING):
                        scores(it, par, j)
                for j in range(NT):
                    if j + RING < NT:
                        scores(it, par, j + RING)
                    if j + RING == NT and not guarded:
                        operands_ready(it + 1)
                        with pe.If(qc < NCH - 1):
                            for first in range(RING):
                                scores(it + 1, par, first)
                        with pe.Else():
                            for first in range(RING):
                                scores(it + 1, 1 - par, first)
                    weigh(it, par, j)
                    if j == 1:
                        pe.wait_ge(staged, it + 1)
                        nc.tensor.matmul(ps[:, QV, :], wq_now[:], k.xnT[:, bass.ds((qc + 1) % NCH * CH, CH)],
                                         start=True, stop=True).then_inc(q_proj, 1)
                    if j == 3 and not guarded:
                        with pe.If(it > 0):
                            sums(it)
                    if j == 4:
                        nc.tensor.matmul(ps[:, KB, :], wk_now[:], x_now[:], start=True, stop=True).then_inc(k_proj, 1)
                    if j == 9 and not guarded:
                        with pe.If(it > 0):
                            project(it, (it + NI - 1) // NCH % NP)
                    if j == 10:
                        pe.wait_ge(q_lo, it + 2)
                        for i in range(TPC):
                            last = nc.tensor.matmul(ps[:, QV, i * P:(i + 1) * P], x_now[:, i * P:(i + 1) * P],
                                                    wv_now[:], start=True, stop=True)
                        last.then_inc(v_proj, 1)
                if guarded:
                    sums(it + 1)
                    project(it + 1, pair)
            if not guarded:
                sums(NI)
                project(NI, NP - 1)

        @block.tensor
        def _(pe):
            pe.sem_inc(pv_done, PROBS)
            for ahead in (x_added, acc_copied, max_read, v_proj, q_lo, k_lo, v_out):
                pe.sem_inc(ahead, 1)
            is_safe = pe.value_load(safe[0:1, 0:1], min_val=0, max_val=1)
            with pe.If(is_safe == 1):
                pe_program(pe, guarded=False)
            with pe.Else():
                pe_program(pe, guarded=True)


def macaron(nc, dram):
    with ExitStack() as ctx:
        k = Kernel(nc, ctx, dram)
        for stage in (constants, lambda k: moe_top1(k, "a"), attention_small, lambda k: moe_top1(k, "b"),
                      lambda k: moe_top2(k, "c"), attention_wide, lambda k: moe_top2(k, "d"), store):
            with nc.cleanup_on_exit():
                stage(k)


INPUTS = {
    "x": "L0_attn_x",
    "t1_wg": "L0_ffn_wg", "t1_w1": "L0_ffn_w1", "t1_b1": "L0_ffn_b1", "t1_w2": "L0_ffn_w2", "t1_b2": "L0_ffn_b2",
    "a0_wk": "L0_attn_Wk", "a0_wq": "L0_attn_Wq", "a0_wo": "L0_attn_Wo", "a0_bo": "L0_attn_bo",
    "t2_router": "L1_ffn_router_w", "t2_w1": "L1_ffn_w1", "t2_w2": "L1_ffn_w2",
    "a1_wq": "L1_attn_Wq", "a1_wk": "L1_attn_Wk", "a1_wv": "L1_attn_Wv", "a1_wp": "L1_attn_Wp", "a1_bp": "L1_attn_bp",
}


def kernel(**inputs):
    import numpy as np
    import concourse.bacc as bacc
    from concourse.bass_utils import run_bass_kernel_spmd

    nc = bacc.Bacc("TRN2", target_bir_lowering=False, num_devices=1)
    arrays, dram = {}, {}
    for short, name in INPUTS.items():
        a = np.asarray(inputs[name])
        a = np.ascontiguousarray(a.T if short == "t2_router" else a)
        arrays[f"in_{name}_dram"] = a
        dram[short] = nc.dram_tensor(f"in_{name}_dram", a.shape, mybir.dt.from_np(a.dtype), kind="ExternalInput").ap()
    dram["out"] = nc.dram_tensor("out_0_dram", (1, S, M), F32, kind="ExternalOutput").ap()
    macaron(nc, dram)
    r = run_bass_kernel_spmd(nc, [arrays], core_ids=[0])
    return r.results[0]["out_0_dram"]
```

```python
from contextlib import ExitStack

import concourse.bass as bass
from concourse import mybir

ALU = mybir.AluOpType
ACT = mybir.ActivationFunctionType
X_AXIS = mybir.AxisListType.X
F32 = mybir.dt.float32
F32R = mybir.dt.float32r
BF16 = mybir.dt.bfloat16
I32 = mybir.dt.int32
RMAX = bass.bass_isa.ReduceOp.max
RADD = bass.bass_isa.ReduceOp.add

P = 128
S = 2048
M = 128
NT = S // P
CH = 512
NCH = S // CH
TPC = CH // P
E = 8
GATE = 7
F0 = 512
FT = F0 // P
CAP = S // E
EPS = 1e-5
SAFE_ARGUMENT = 60.0


def broadcast_last(ap, n):
    return ap.unsqueeze(2).to_broadcast([ap.shape[0], ap.shape[1], n])


class Kernel:

    def __init__(self, nc, ctx, dram):
        self.nc, self.dram = nc, dram

        def sb(name, shape, dt=F32):
            return ctx.enter_context(nc.sbuf_tensor(name, shape, dt))

        self.ps = ctx.enter_context(nc.psum_tensor("banks", [P, 8, CH], F32))
        self.x = sb("x_tokens", [P, NT, M])
        self.xnT = sb("xn_transposed", [M, S])
        self.ident = sb("ident", [P, P])
        self.ones = sb("ones", [P, P])
        self.ones_r = sb("ones_r", [P, P], F32R)
        self.ones_b = sb("ones_b", [P, P], BF16)
        self.earlier = sb("earlier_tokens", [P, P], BF16)
        self.rank = sb("expert_rank", [P, NT, E])
        self.base_slot = sb("base_slot", [P, E, NT])
        self.scan_keep = sb("scan_keep", [P, E, NT + 1])
        self.slot_of_row = sb("slot_of_row", [P, NT])
        self.t1_wg = sb("t1_wg_all", [M, E])
        self.a0_wq, self.a0_wk = sb("a0_wq_all", [M, M]), sb("a0_wk_all", [M, M])
        self.a0_bo = sb("a0_bo_all", [P, M])
        self.t2_router = sb("t2_router_all", [M, E])
        self.t2_w1 = sb("t2_w1_all", [M, E, P])
        self.t2_w2 = sb("t2_w2_all", [P, E, M])
        self.a1_w = sb("a1_w_all", [M, 3, 16, 64])
        self.a1_wp = sb("a1_wp_all", [P, 8, M])
        self.a1_bp = sb("a1_bp_all", [P, M])
        self.top1_weights = ctx.enter_context(ExitStack())
        self.t1_w1 = self.top1_weights.enter_context(nc.sbuf_tensor("t1_w1_all", [M, E, F0], F32))
        self.t1_w2 = self.top1_weights.enter_context(nc.sbuf_tensor("t1_w2_all", [P, E, FT, M], F32))
        self.t1_b1 = self.top1_weights.enter_context(nc.sbuf_tensor("t1_b1_all", [P, E, FT], F32))
        self.t1_b2 = self.top1_weights.enter_context(nc.sbuf_tensor("t1_b2_all", [P, E, M], F32))
        self.gate_loaded = nc.alloc_semaphore("gate_weights_loaded")
        self.t1_loaded = nc.alloc_semaphore("t1_weights_loaded")
        self.a0_loaded = nc.alloc_semaphore("a0_weights_loaded")
        self.t2_loaded = nc.alloc_semaphore("t2_weights_loaded")
        self.a1_loaded = nc.alloc_semaphore("a1_weights_loaded")


def constants(k):
    nc = k.nc
    with ExitStack() as ctx:
        x_loaded = nc.alloc_semaphore("x_loaded")
        filled = nc.alloc_semaphore("const_filled")
        block = ctx.enter_context(nc.Block())

        @block.sync
        def _(sp):
            sp.dma_start(k.x[:], k.dram["x"].rearrange("b (t p) m -> p (b t) m", p=P)).then_inc(x_loaded, 16)
            sp.dma_start(k.t1_wg[:], k.dram["t1_wg"]).then_inc(k.gate_loaded, 16)
            sp.wait_ge(x_loaded, 16)

        @block.vector
        def _(dve):
            nc.vector.memset(k.ones_r[:].bitcast(F32), 1.0)
            nc.vector.memset(k.ones_b[:], 1.0)
            for e in range(E):
                nc.vector.memset(k.rank[:, :, e], float(E - e))
                nc.vector.memset(k.base_slot[:, e, :], float(e * CAP))

        @block.gpsimd
        def _(pool):
            nc.gpsimd.memset(k.ident[:], 0.0).then_inc(filled, 1)
            nc.gpsimd.memset(k.ones[:], 1.0).then_inc(filled, 1)
            nc.gpsimd.memset(k.scan_keep[:], 1.0).then_inc(filled, 1)
            nc.gpsimd.iota(k.slot_of_row[:], [[P, NT]], base=0, channel_multiplier=1,
                           allow_small_or_imprecise_dtypes=True)
            pool.wait_ge(filled, 3)
            nc.gpsimd.affine_select(out=k.ident[:], in_=k.ident[:], compare_op=ALU.not_equal, fill=1.0,
                                    base=0, pattern=[[-1, P]], channel_multiplier=1)
            nc.gpsimd.affine_select(out=k.earlier[:], in_=k.ones[:], compare_op=ALU.is_gt, fill=0.0,
                                    base=0, pattern=[[1, P]], channel_multiplier=-1)
            nc.gpsimd.memset(k.scan_keep[:, :, 0], 0.0)


def load_weights(k, sp):
    nc, d = k.nc, k.dram
    sp.dma_start(k.t1_w1[:], d["t1_w1"].rearrange("e m f -> m e f")).then_inc(k.t1_loaded, 16)
    sp.dma_start(k.t1_w2[:], d["t1_w2"].rearrange("e (t f) m -> f e t m", f=P)).then_inc(k.t1_loaded, 16)
    with nc.allow_non_contiguous_dma(reason="the biases, one per hidden unit's partition"):
        sp.dma_start(k.t1_b1[:], d["t1_b1"].rearrange("e (t f) -> f e t", f=P)).then_inc(k.t1_loaded, 16)
    sp.dma_start(k.t1_b2[:], d["t1_b2"].partition_broadcast(P)).then_inc(k.t1_loaded, 16)
    sp.dma_start(k.a0_wq[:], d["a0_wq"]).then_inc(k.a0_loaded, 16)
    sp.dma_start(k.a0_wk[:], d["a0_wk"]).then_inc(k.a0_loaded, 16)
    sp.dma_start(k.a0_bo[:], d["a0_bo"].partition_broadcast(P)).then_inc(k.a0_loaded, 16)
    sp.dma_start(k.t2_router[:], d["t2_router"]).then_inc(k.t2_loaded, 16)
    sp.dma_start(k.t2_w1[:], d["t2_w1"].rearrange("e m f -> m e f")).then_inc(k.t2_loaded, 16)
    sp.dma_start(k.t2_w2[:], d["t2_w2"].rearrange("e f m -> f e m")).then_inc(k.t2_loaded, 16)
    for i, name in enumerate(("a1_wq", "a1_wk", "a1_wv")):
        sp.dma_start(k.a1_w[:, i, :, :], d[name].rearrange("h m e -> m h e")).then_inc(k.a1_loaded, 16)
    for s in range(2):
        sp.dma_start(k.a1_wp[64 * s:64 * (s + 1), :, :],
                     d["a1_wp"].rearrange("(e p s) o -> s e p o", p=8, s=2)[s]).then_inc(k.a1_loaded, 16)
    sp.dma_start(k.a1_bp[:], d["a1_bp"].partition_broadcast(P)).then_inc(k.a1_loaded, 16)


def layernorm(k, xn, tag, gate=None, gate_loaded=None, loads=None):
    nc, ps = k.nc, k.ps
    with ExitStack() as ctx:
        def sb(name, shape, dt=F32):
            return ctx.enter_context(nc.sbuf_tensor(f"s_{name}_{tag}", shape, dt))

        def sem(name):
            return nc.alloc_semaphore(f"{name}_{tag}")

        stats = sb("ln_stats", [P, NT, 6])
        mv = sb("ln_mean_var", [P, NT, 2])
        var = sb("ln_var", [P, NT])
        std = sb("ln_std", [P, NT])
        rstd = sb("ln_rstd", [P, NT])
        newton = sb("ln_newton", [P, NT])
        shift = sb("ln_shift", [P, NT])
        dve_step, scale_ready = sem("ln_dve_step"), sem("ln_scale_ready")
        var_ready, std_ready = sem("ln_var_ready"), sem("ln_std_ready")
        even_ready, odd_ready, transposed = sem("ln_even_ready"), sem("ln_odd_ready"), sem("ln_transposed")
        turned = [sem("ln_even_chunks_turned"), sem("ln_odd_chunks_turned")]
        block = ctx.enter_context(nc.Block())

        if loads:
            @block.sync
            def _(sp):
                loads(k, sp)

        @block.vector
        def _(dve):
            done = [0]

            def link(ins):
                done[0] += 1
                ins.then_inc(dve_step, 1)
                dve.wait_ge(dve_step, done[0])

            for t in range(NT):
                last = nc.vector.bn_stats(stats[:, t, :], k.x[:, t, :])
            link(last)
            for t in range(NT):
                last = nc.vector.bn_aggr(mv[:, t, :], stats[:, t, :])
            link(last)
            nc.vector.tensor_scalar(var[:], mv[:, :, 1], EPS, None, ALU.add).then_inc(var_ready, 1)
            dve.wait_ge(std_ready, 1)
            link(nc.vector.reciprocal(rstd[:], std[:]))
            link(nc.vector.tensor_tensor(newton[:], rstd[:], rstd[:], ALU.mult))
            link(nc.vector.tensor_tensor(newton[:], newton[:], var[:], ALU.mult))
            link(nc.vector.tensor_scalar(newton[:], newton[:], -0.5, 1.5, ALU.mult, ALU.add))
            link(nc.vector.tensor_tensor(rstd[:], rstd[:], newton[:], ALU.mult))
            nc.vector.scalar_tensor_tensor(out=shift[:], in0=mv[:, :, 0], scalar=-1.0, in1=rstd[:],
                                           op0=ALU.mult, op1=ALU.mult).then_inc(scale_ready, 1)
            for t in range(0, NT, 2):
                nc.vector.tensor_scalar(xn[:, t, :], k.x[:, t, :], mv[:, t, 0:1], rstd[:, t:t + 1],
                                        ALU.subtract, ALU.mult).then_inc(even_ready, 1)
            for c in range(0, NCH, 2):
                dve.wait_ge(transposed, c + 1)
                nc.vector.tensor_copy(k.xnT[:, c * CH:(c + 1) * CH], ps[:, c, :]).then_inc(turned[0], 1)

        @block.scalar
        def _(act):
            act.wait_ge(var_ready, 1)
            nc.scalar.activation(std[:], var[:], ACT.Sqrt).then_inc(std_ready, 1)
            act.wait_ge(scale_ready, 1)
            for t in range(1, NT, 2):
                nc.scalar.activation(xn[:, t, :], k.x[:, t, :], ACT.Identity, bias=shift[:, t:t + 1],
                                     scale=rstd[:, t:t + 1]).then_inc(odd_ready, 1)
            for c in range(1, NCH, 2):
                act.wait_ge(transposed, c + 1)
                nc.scalar.activation(k.xnT[:, c * CH:(c + 1) * CH], ps[:, c, :], ACT.Copy).then_inc(turned[1], 1)

        @block.tensor
        def _(pe):
            def gate_chunk(c):
                pe.wait_ge(turned[c % 2], c // 2 + 1)
                for t in range(c * TPC, (c + 1) * TPC):
                    nc.tensor.matmul(ps[:, GATE, t * E:(t + 1) * E], k.xnT[:, t * P:(t + 1) * P], gate[:],
                                     start=True, stop=True)

            for t in range(NT):
                pe.wait_ge(odd_ready if t % 2 else even_ready, t // 2 + 1)
                ins = nc.tensor.transpose(ps[:, t // TPC, (t % TPC) * P:(t % TPC + 1) * P], xn[:, t, :], k.ident[:])
                if t % TPC == TPC - 1:
                    ins.then_inc(transposed, 1)
                    if gate is not None and t == NT - 1:
                        pe.wait_ge(*gate_loaded)
                        for c in range(NCH):
                            gate_chunk(c)


def moe_top1(k, tag, loads=None):
    nc, ps, d = k.nc, k.ps, k.dram
    with ExitStack() as ctx:
        def sb(name, shape, dt=F32):
            return ctx.enter_context(nc.sbuf_tensor(f"s_{name}_{tag}", shape, dt))

        def sem(name):
            return nc.alloc_semaphore(f"{name}_{tag}")

        xn = sb("t1_xn", [P, NT, M])
        layernorm(k, xn, tag, k.t1_wg, (k.gate_loaded, 16), loads)

        w1, w2, b1, b2 = k.t1_w1, k.t1_w2, k.t1_b1, k.t1_b2
        xn_hi = sb("t1_xn_hi", [P, NT, M], F32R)
        xn_lo = sb("t1_xn_lo", [P, NT, M], F32R)
        shifted = sb("t1_shifted", [P, NT, E])
        ex = sb("t1_ex", [P, NT, E])
        score = sb("t1_score", [P, NT, E])
        stat = sb("t1_stat", [P, 12, NT])
        mask = sb("t1_mask", [P, E, NT + 1], BF16)
        before = sb("t1_before", [P, E, NT + 1], BF16)
        own = sb("t1_own", [P, E, NT])
        own_base = sb("t1_own_base", [P, E, NT])
        slot_diag = sb("t1_slot_diag", [P, NT, P], F32R)
        slot_row = sb("t1_slot_row", [P, S])
        slot_iota = sb("t1_slot_iota", [P, S])
        onehot = sb("t1_onehot", [P, 2, S], F32R)
        xdT = sb("t1_dispatched", [M, S])
        hT = sb("t1_hidden", [P, 2, FT, CAP])
        eo = sb("t1_expert_rows", [P, NT, M])
        eo_hi = sb("t1_expert_hi", [P, NT, M], F32R)
        eo_lo = sb("t1_expert_lo", [P, NT, M], F32R)
        (row_max, row_sum, best_ex, r_sum, gate, best_rank, cnt_own, base_own, keep, slot, slot_kept,
         half_gate) = [stat[:, i, :] for i in range(12)]

        dve_step, mask_zero, iota_ready = sem("t1_dve_step"), sem("t1_mask_zero"), sem("t1_iota_ready")
        shift_ready, ex_ready, slot_ready = sem("t1_shift_ready"), sem("t1_ex_ready"), sem("t1_slot_ready")
        mask_ready, counts_ready, diag_ready = sem("t1_mask_ready"), sem("t1_counts_ready"), sem("t1_diag_ready")
        row_in_psum, row_ready = sem("t1_row_in_psum"), sem("t1_row_ready")
        hi_ready, lo_ready = sem("t1_hi_ready"), sem("t1_lo_ready")
        onehot_ready, onehot_used = sem("t1_onehot_ready"), sem("t1_onehot_used")
        gathered, xd_ready = sem("t1_gathered"), sem("t1_xd_ready")
        up_done, hidden_ready, down_done = sem("t1_up_done"), sem("t1_hidden_ready"), sem("t1_down_done")
        eo_ready, back, back_ready, tokens_back = (sem("t1_eo_ready"), sem("t1_back"), sem("t1_back_ready"),
                                                   sem("t1_tokens_back"))
        block = ctx.enter_context(nc.Block())

        @block.gpsimd
        def _(pool):
            nc.gpsimd.memset(mask[:, :, 0], 0.0).then_inc(mask_zero, 1)
            nc.gpsimd.iota(slot_iota[:], [[1, S]], base=0, channel_multiplier=0,
                           allow_small_or_imprecise_dtypes=True).then_inc(iota_ready, 1)
            pool.wait_ge(hi_ready, 1)
            nc.gpsimd.tensor_tensor(xn_lo[:], xn[:], xn_hi[:].bitcast(F32), ALU.subtract).then_inc(lo_ready, 1)
            pool.wait_ge(slot_ready, 1)
            nc.gpsimd.tensor_tensor(slot_diag[:], k.ident[:].unsqueeze(1).to_broadcast([P, NT, P]),
                                    broadcast_last(slot_kept, P), ALU.mult).then_inc(diag_ready, 1)

        @block.scalar
        def _(act):
            act.wait_ge(shift_ready, 1)
            nc.scalar.activation(ex[:], shifted[:], ACT.Exp).then_inc(ex_ready, 1)
            nc.scalar.activation(xn_hi[:], xn[:], ACT.Copy).then_inc(hi_ready, 1)
            for c in range(NCH):
                act.wait_ge(row_in_psum, c + 1)
                nc.scalar.activation(slot_row[:, c * CH:(c + 1) * CH], ps[:, c, :], ACT.Copy).then_inc(row_ready, 1)
            for c in range(NCH):
                act.wait_ge(gathered, c + 1)
                nc.scalar.activation(xdT[:, c * CH:(c + 1) * CH], ps[:, 4 + c, :], ACT.Copy).then_inc(xd_ready, 1)
            act.wait_ge(k.t1_loaded, 64)
            for e in range(E):
                if e >= 2:
                    act.wait_ge(down_done, e - 1)
                for f in range(FT):
                    act.wait_ge(up_done, e * 2 + f // 2 + 1)
                    bank = (e % 2) * 2 + f // 2
                    nc.scalar.activation(hT[:, e % 2, f, :], ps[:, bank, (f % 2) * CAP:(f % 2 + 1) * CAP],
                                         ACT.Gelu_apprx_tanh, bias=b1[:, e, f:f + 1]).then_inc(hidden_ready, 1)
            for c in range(NCH):
                act.wait_ge(back, c + 1)
                nc.scalar.activation(xdT[:, c * CH:(c + 1) * CH], ps[:, c, :], ACT.Copy).then_inc(back_ready, 1)

        @block.vector
        def _(dve):
            done = [0]

            def link(ins):
                done[0] += 1
                ins.then_inc(dve_step, 1)
                dve.wait_ge(dve_step, done[0])

            logits = ps[:, GATE, 0:NT * E].rearrange("p (t e) -> p t e", e=E)
            link(nc.vector.tensor_reduce(row_max, logits, X_AXIS, ALU.max))
            nc.vector.tensor_tensor(shifted[:], logits, broadcast_last(row_max, E), ALU.subtract)\
                .then_inc(shift_ready, 1)
            dve.wait_ge(ex_ready, 1)
            nc.vector.tensor_reduce(row_sum, ex[:], X_AXIS, ALU.add)
            link(nc.vector.tensor_reduce(best_ex, ex[:], X_AXIS, ALU.max))
            nc.vector.reciprocal(r_sum, row_sum)
            link(nc.vector.tensor_tensor(score[:], ex[:], broadcast_last(best_ex, E), ALU.is_equal))
            nc.vector.tensor_tensor(gate, best_ex, r_sum, ALU.mult)
            link(nc.vector.tensor_tensor(score[:], score[:], k.rank[:], ALU.mult))
            link(nc.vector.tensor_reduce(best_rank, score[:], X_AXIS, ALU.max))
            nc.vector.tensor_scalar(half_gate, gate, 0.5, None, ALU.mult)
            dve.wait_ge(mask_zero, 1)
            link(nc.vector.tensor_tensor(mask[:, :, 1:NT + 1].rearrange("p e t -> p t e"), score[:],
                                         broadcast_last(best_rank, E), ALU.is_equal))
            nc.vector.tensor_tensor_scan(before[:].rearrange("p e t -> p (e t)"),
                                         k.scan_keep[:].rearrange("p e t -> p (e t)"),
                                         mask[:].rearrange("p e t -> p (e t)"), 0.0, ALU.mult, ALU.add)\
                .then_inc(mask_ready, 1)
            counts = ps[:, 1, 0:E * NT].rearrange("p (e t) -> p e t", e=E)
            nc.vector.tensor_tensor(own_base[:], k.base_slot[:], mask[:, :, 1:NT + 1], ALU.mult)
            dve.wait_ge(counts_ready, 1)
            link(nc.vector.tensor_tensor(own[:], counts, mask[:, :, 1:NT + 1], ALU.mult))
            nc.vector.tensor_reduce(base_own, own_base[:].rearrange("p e t -> p t e"), X_AXIS, ALU.add)
            link(nc.vector.tensor_reduce(cnt_own, own[:].rearrange("p e t -> p t e"), X_AXIS, ALU.add))
            nc.vector.tensor_scalar(keep, cnt_own, float(CAP), None, ALU.is_lt)
            link(nc.vector.tensor_tensor(slot, cnt_own, base_own, ALU.add))
            link(nc.vector.scalar_tensor_tensor(out=slot, in0=slot, scalar=1.0, in1=keep, op0=ALU.add, op1=ALU.mult))
            link(nc.vector.tensor_scalar(slot_kept, slot, -1.0, None, ALU.add))
            nc.vector.sem_inc(slot_ready, 1)
            dve.wait_ge(iota_ready, 1)
            for t in range(NT):
                if t >= 2:
                    dve.wait_ge(onehot_used, t - 1)
                nc.vector.tensor_scalar(onehot[:, t % 2, :], slot_iota[:], slot_kept[:, t:t + 1], None,
                                        ALU.is_equal).then_inc(onehot_ready, 1)

            def expert_out(e):
                dve.wait_ge(down_done, e + 1)
                rows = ps[:, 4 + e % 4, 0:2 * M].rearrange("p (t m) -> p t m", m=M)
                exact = eo[:, 2 * e:2 * e + 2, :]
                link(nc.vector.tensor_tensor(exact, rows, b2[:, e:e + 1, :].to_broadcast([P, 2, M]), ALU.add))
                link(nc.vector.tensor_copy(eo_hi[:, 2 * e:2 * e + 2, :], exact))
                nc.vector.tensor_tensor(eo_lo[:, 2 * e:2 * e + 2, :], exact,
                                        eo_hi[:, 2 * e:2 * e + 2, :].bitcast(F32), ALU.subtract).then_inc(eo_ready, 1)

            def onehot_back(j):
                if j == 1:
                    dve.wait_ge(gathered, NCH)
                else:
                    dve.wait_ge(onehot_used, NT - 1 if j == 0 else NT - 1 + j - 1)
                nc.vector.tensor_scalar(onehot[:, j % 2, :], slot_row[:], k.slot_of_row[:, j:j + 1], None,
                                        ALU.is_equal).then_inc(onehot_ready, 1)

            dve.wait_ge(row_ready, NCH)
            onehot_back(0)
            onehot_back(1)
            for e in range(E):
                expert_out(e)
            for j in range(2, NT):
                onehot_back(j)
            for t in range(NT):
                dve.wait_ge(tokens_back, t // TPC + 1)
                nc.vector.scalar_tensor_tensor(out=k.x[:, t, :], in0=ps[:, 4 + t // TPC, (t % TPC) * P:(t % TPC + 1) * P],
                                               scalar=half_gate[:, t:t + 1], in1=k.x[:, t, :],
                                               op0=ALU.mult, op1=ALU.add)

        @block.tensor
        def _(pe):
            pe.wait_ge(mask_ready, 1)
            counts = ps[:, 1, 0:E * NT]
            nc.tensor.matmul(counts, k.earlier[:], mask[:, :, 1:NT + 1], start=True, stop=False)
            nc.tensor.matmul(counts, k.ones_b[:], before[:, :, 0:NT], start=False, stop=True)\
                .then_inc(counts_ready, 1)
            pe.wait_ge(lo_ready, 1)
            for t in range(NT):
                pe.wait_ge(onehot_ready, t + 1)
                for part, rows in enumerate((xn_hi, xn_lo)):
                    for c in range(NCH):
                        last = nc.tensor.matmul(ps[:, 4 + c, :], rows[:, t, :], onehot[:, t % 2, c * CH:(c + 1) * CH],
                                                start=(t == 0 and part == 0), stop=(t == NT - 1 and part == 1))
                        if t == NT - 1 and part == 1:
                            last.then_inc(gathered, 1)
                if t < NT - 1:
                    last.then_inc(onehot_used, 1)
                if t == 6:
                    pe.wait_ge(diag_ready, 1)
                    for c in range(NCH):
                        nc.tensor.matmul(ps[:, c, :], k.ones_r[:], slot_diag[:, c * TPC:(c + 1) * TPC, :],
                                         start=True, stop=True).then_inc(row_in_psum, 1)
            pe.wait_ge(k.t1_loaded, 64)
            pe.wait_ge(row_ready, NCH)

            def up(e):
                if e % 2 == 0:
                    pe.wait_ge(xd_ready, e // 2 + 1)
                if e >= 2:
                    pe.wait_ge(hidden_ready, (e - 1) * FT)
                for f in range(FT):
                    bank = (e % 2) * 2 + f // 2
                    last = nc.tensor.matmul(ps[:, bank, (f % 2) * CAP:(f % 2 + 1) * CAP],
                                            w1[:, e, f * P:(f + 1) * P], xdT[:, e * CAP:(e + 1) * CAP],
                                            start=True, stop=True)
                    if f % 2:
                        last.then_inc(up_done, 1)

            def down(e):
                pe.wait_ge(hidden_ready, (e + 1) * FT)
                if e < 4:
                    pe.wait_ge(xd_ready, NCH)
                else:
                    pe.wait_ge(eo_ready, e - 3)
                for half in range(2):
                    out = ps[:, 4 + e % 4, half * M:(half + 1) * M]
                    for f in range(FT):
                        last = nc.tensor.matmul(out, hT[:, e % 2, f, half * P:(half + 1) * P], w2[:, e, f, :],
                                                start=(f == 0), stop=(f == FT - 1))
                last.then_inc(down_done, 1)

            up(0)
            for e in range(E):
                if e + 1 < E:
                    up(e + 1)
                down(e)
            pe.wait_ge(hidden_ready, E * FT)
            for j in range(NT):
                pe.wait_ge(onehot_ready, NT + j + 1)
                pe.wait_ge(eo_ready, j // 2 + 1)
                for part, rows in enumerate((eo_hi, eo_lo)):
                    for c in range(NCH):
                        last = nc.tensor.matmul(ps[:, c, :], rows[:, j, :], onehot[:, j % 2, c * CH:(c + 1) * CH],
                                                start=(j == 0 and part == 0), stop=(j == NT - 1 and part == 1))
                        if j == NT - 1 and part == 1:
                            last.then_inc(back, 1)
                if j < NT - 1:
                    last.then_inc(onehot_used, 1)
            for t in range(NT):
                pe.wait_ge(back_ready, t // TPC + 1)
                if t == 0:
                    pe.wait_ge(eo_ready, E)
                last = nc.tensor.transpose(ps[:, 4 + t // TPC, (t % TPC) * P:(t % TPC + 1) * P],
                                           xdT[:, t * P:(t + 1) * P], k.ident[:])
                if t % TPC == TPC - 1:
                    last.then_inc(tokens_back, 1)


def moe_top2(k, tag):
    nc, ps, d = k.nc, k.ps, k.dram
    with ExitStack() as ctx:
        def sb(name, shape, dt=F32):
            return ctx.enter_context(nc.sbuf_tensor(f"s_{name}_{tag}", shape, dt))

        def sem(name):
            return nc.alloc_semaphore(f"{name}_{tag}")

        xn = sb("t2_xn", [P, NT, M])
        layernorm(k, xn, tag, k.t2_router, (k.t2_loaded, 48))

        w1, w2 = k.t2_w1, k.t2_w2
        shifted = sb("t2_shifted", [P, NT, E])
        ex = sb("t2_ex", [P, NT, E])
        rest = sb("t2_rest", [P, NT, E])
        score = sb("t2_score", [P, NT, E])
        first = sb("t2_first", [P, NT, E])
        second = sb("t2_second", [P, NT, E])
        weight = sb("t2_weight", [P, NT, E])
        stat = sb("t2_stat", [P, 8, NT])
        AHEAD, HIDDEN = E, E + 2
        hidden = sb("t2_hidden", [P, HIDDEN, CH])
        row_max, row_sum, best_ex, r_sum, best_rank, next_ex, next_rank, half = [stat[:, i, :] for i in range(8)]

        dve_step = sem("t2_dve_step")
        shift_ready, ex_ready = sem("t2_shift_ready"), sem("t2_ex_ready")
        up_done, hidden_ready, down_done, added = (sem("t2_up_done"), sem("t2_hidden_ready"), sem("t2_down_done"),
                                                   sem("t2_added"))
        block = ctx.enter_context(nc.Block())
        steps = [(c, e) for c in range(NCH) for e in range(E)]

        @block.scalar
        def _(act):
            act.wait_ge(shift_ready, 1)
            nc.scalar.activation(ex[:], shifted[:], ACT.Exp).then_inc(ex_ready, 1)
            for n in range(len(steps)):
                act.wait_ge(up_done, n + 1)
                if n >= HIDDEN:
                    act.wait_ge(down_done, n - HIDDEN + 1)
                nc.scalar.activation(hidden[:, n % HIDDEN, :], ps[:, n % 4, :], ACT.Relu).then_inc(hidden_ready, 1)

        @block.vector
        def _(dve):
            done = [0]

            def link(ins):
                done[0] += 1
                ins.then_inc(dve_step, 1)
                dve.wait_ge(dve_step, done[0])

            logits = ps[:, GATE, 0:NT * E].rearrange("p (t e) -> p t e", e=E)
            link(nc.vector.tensor_reduce(row_max, logits, X_AXIS, ALU.max))
            nc.vector.tensor_tensor(shifted[:], logits, broadcast_last(row_max, E), ALU.subtract)\
                .then_inc(shift_ready, 1)
            dve.wait_ge(ex_ready, 1)
            nc.vector.tensor_reduce(row_sum, ex[:], X_AXIS, ALU.add)
            link(nc.vector.tensor_reduce(best_ex, ex[:], X_AXIS, ALU.max))
            nc.vector.reciprocal(r_sum, row_sum)
            link(nc.vector.tensor_tensor(score[:], ex[:], broadcast_last(best_ex, E), ALU.is_equal))
            link(nc.vector.tensor_tensor(score[:], score[:], k.rank[:], ALU.mult))
            link(nc.vector.tensor_reduce(best_rank, score[:], X_AXIS, ALU.max))
            link(nc.vector.tensor_tensor(first[:], score[:], broadcast_last(best_rank, E), ALU.is_equal))
            link(nc.vector.tensor_tensor(rest[:], ex[:], first[:], ALU.mult))
            link(nc.vector.tensor_tensor(rest[:], ex[:], rest[:], ALU.subtract))
            link(nc.vector.tensor_tensor(rest[:], rest[:], first[:], ALU.subtract))
            link(nc.vector.tensor_reduce(next_ex, rest[:], X_AXIS, ALU.max))
            link(nc.vector.tensor_tensor(score[:], rest[:], broadcast_last(next_ex, E), ALU.is_equal))
            link(nc.vector.tensor_tensor(score[:], score[:], k.rank[:], ALU.mult))
            link(nc.vector.tensor_reduce(next_rank, score[:], X_AXIS, ALU.max))
            nc.vector.tensor_scalar(half, r_sum, 0.5, None, ALU.mult)
            link(nc.vector.tensor_tensor(second[:], score[:], broadcast_last(next_rank, E), ALU.is_equal))
            link(nc.vector.tensor_tensor(first[:], first[:], second[:], ALU.add))
            link(nc.vector.tensor_tensor(weight[:], first[:], ex[:], ALU.mult))
            link(nc.vector.tensor_tensor(weight[:], weight[:], broadcast_last(half, E), ALU.mult))
            for n, (c, e) in enumerate(steps):
                dve.wait_ge(down_done, n + 1)
                if n >= 1:
                    dve.wait_ge(added, n)
                for i in range(TPC):
                    t = c * TPC + i
                    last = nc.vector.scalar_tensor_tensor(
                        out=k.x[:, t, :], in0=ps[:, 4 + n % 3, i * P:(i + 1) * P], scalar=weight[:, t, e:e + 1],
                        in1=k.x[:, t, :], op0=ALU.mult, op1=ALU.add)
                last.then_inc(added, 1)

        @block.tensor
        def _(pe):
            pe.wait_ge(k.t2_loaded, 48)

            def up(n):
                c, e = steps[n]
                if n >= 4:
                    pe.wait_ge(hidden_ready, n - 3)
                nc.tensor.matmul(ps[:, n % 4, :], w1[:, e, :], k.xnT[:, c * CH:(c + 1) * CH],
                                 start=True, stop=True).then_inc(up_done, 1)

            def down(n):
                c, e = steps[n]
                pe.wait_ge(hidden_ready, n + 1)
                if n >= 3:
                    pe.wait_ge(added, n - 2)
                for i in range(TPC):
                    last = nc.tensor.matmul(ps[:, 4 + n % 3, i * P:(i + 1) * P], hidden[:, n % HIDDEN, i * P:(i + 1) * P],
                                            w2[:, e, :], start=True, stop=True)
                last.then_inc(down_done, 1)

            for n in range(AHEAD):
                up(n)
            for n in range(len(steps)):
                if n + AHEAD < len(steps):
                    up(n + AHEAD)
                down(n)


def store(k):
    nc = k.nc
    with ExitStack() as ctx:
        stored = nc.alloc_semaphore("stored")
        block = ctx.enter_context(nc.Block())

        @block.sync
        def _(sp):
            sp.dma_start(k.dram["out"].rearrange("b (t p) m -> p (b t) m", p=P), k.x[:]).then_inc(stored, 16)
            sp.wait_ge(stored, 16)


def attention_small(k):
    nc, ps, d = k.nc, k.ps, k.dram
    H, D, G = 16, 8, 4
    NG = H // G
    PARTS = 3
    ROWS = PARTS * PARTS * D
    SCALE = float(M) ** -0.5
    W = P // G
    JT = NT * G // 2
    NI = NG * NCH
    RING, PROBS = 3, 4
    TURNS = 2
    ACC, EPI = 6, 7
    q_dram = nc.dram_tensor("a0_q_parts", (H, PARTS, D, S), BF16, kind="Internal").ap()
    k_dram = nc.dram_tensor("a0_k_parts", (H, PARTS, D, S), BF16, kind="Internal").ap()

    with ExitStack() as ctx:
        def sb(name, shape, dt=F32):
            return ctx.enter_context(nc.sbuf_tensor(f"s_a0_{name}", shape, dt))

        def sem(name):
            return nc.alloc_semaphore(f"a0_{name}")

        safe = sb("safe", [H, 1], I32)
        values = sb("values", [P, NT, M])
        v_strip = sb("v_strip", [P, 2, NT, G, W])
        wo = sb("wo_strips", [P, NG, M])
        sum_row = sb("sum_row", [P, P])

        with ExitStack() as prep:
            def psb(name, shape, dt=F32):
                return prep.enter_context(nc.sbuf_tensor(f"s_a0_{name}", shape, dt))

            def psem(name):
                return sem(name)

            xn = psb("xn", [P, NT, M])
            layernorm(k, xn, "a0")
            wq, wk, bo = k.a0_wq, k.a0_wk, k.a0_bo
            qk = psb("qk", [P, 2, S])
            part = psb("part", [P, 2, PARTS, S], BF16)
            square = psb("square", [P, 2 * NCH, CH], BF16)
            head_rows = psb("head_rows", [P, H], BF16)
            norm = psb("norm", [H, 2 * NCH])
            most = psb("most", [H, 4])
            wo_zero, wo_loaded, filled = psem("wo_zero"), psem("wo_loaded"), psem("filled")
            projected, copied, squared = psem("projected"), psem("copied"), psem("squared")
            v_projected, normed, norm_read = psem("v_projected"), psem("normed"), psem("norm_read")
            split, stored, dve_step, product, reduced = (psem("split"), psem("stored"), psem("dve_step"),
                                                         psem("product"), psem("reduced"))
            block = prep.enter_context(nc.Block())

            @block.sync
            def _(sp):
                sp.wait_ge(wo_zero, 1)
                for h in range(G):
                    sp.dma_start(wo[W * h:W * h + D, :, :],
                                 d["a0_wo"].rearrange("(g h d) n -> h d g n", g=NG, h=G)[h]).then_inc(wo_loaded, 16)
                for side, dram in enumerate((q_dram, k_dram)):
                    for i in range(PARTS):
                        sp.wait_ge(split, side * PARTS + i + 1)
                        sp.dma_start(dram[:, i, :, :], part[:, side, i, :]).then_inc(stored, 16)
                sp.wait_ge(stored, 2 * PARTS * 16)
                sp.wait_ge(wo_loaded, G * 16)

            @block.gpsimd
            def _(pool):
                nc.gpsimd.memset(wo[:], 0.0).then_inc(wo_zero, 1)
                nc.gpsimd.memset(head_rows[:], 1.0).then_inc(filled, 1)
                nc.gpsimd.memset(sum_row[:], 0.0).then_inc(filled, 1)
                nc.gpsimd.memset(v_strip[:], 0.0).then_inc(filled, 1)
                pool.wait_ge(filled, 3)
                nc.gpsimd.affine_select(out=head_rows[:], in_=head_rows[:], compare_op=ALU.is_ge, fill=0.0,
                                        base=0, pattern=[[-D, H]], channel_multiplier=1).then_inc(filled, 1)
                pool.wait_ge(filled, 4)
                nc.gpsimd.affine_select(out=head_rows[:], in_=head_rows[:], compare_op=ALU.is_ge, fill=0.0,
                                        base=D - 1, pattern=[[D, H]], channel_multiplier=-1).then_inc(filled, 1)
                nc.gpsimd.affine_select(out=sum_row[:], in_=sum_row[:], compare_op=ALU.not_equal, fill=1.0,
                                        base=-D, pattern=[[-W, G], [0, W]], channel_multiplier=1)
                nc.gpsimd.memset(v_strip[:, :, :, :, D], 1.0)
                pool.wait_ge(k.a0_loaded, 48)
                nc.gpsimd.tensor_tensor(k.x[:], k.x[:], bo[:].unsqueeze(1).to_broadcast([P, NT, M]), ALU.add)
                pool.wait_ge(product, 1)
                nc.gpsimd.partition_all_reduce(most[:, 3:4], most[:, 2:3], H, RMAX).then_inc(reduced, 1)

            @block.scalar
            def _(act):
                for n in range(2 * NCH):
                    act.wait_ge(projected, n + 1)
                    nc.scalar.activation(qk[:, n // NCH, (n % NCH) * CH:(n % NCH + 1) * CH], ps[:, n, :],
                                         ACT.Copy).then_inc(copied, 1)
                    nc.scalar.activation(square[:, n, :], ps[:, n, :], ACT.Square).then_inc(squared, 1)
                for c in range(NCH):
                    act.wait_ge(v_projected, c + 1)
                    nc.scalar.activation(values[:, c * TPC:(c + 1) * TPC, :], ps[:, c, :], ACT.Copy)

            @block.vector
            def _(dve):
                done = [0]

                def link(ins):
                    done[0] += 1
                    ins.then_inc(dve_step, 1)
                    dve.wait_ge(dve_step, done[0])

                for side in range(2):
                    dve.wait_ge(copied, (side + 1) * NCH)
                    for i in range(PARTS):
                        nc.vector.tensor_copy(part[:, side, i, :], qk[:, side, :]).then_inc(split, 1)
                        dve.wait_ge(split, side * PARTS + i + 1)
                        if i < PARTS - 1:
                            link(nc.vector.tensor_tensor(qk[:, side, :], qk[:, side, :], part[:, side, i, :],
                                                         ALU.subtract))
                for n in range(2 * NCH):
                    dve.wait_ge(normed, n + 1)
                    nc.vector.tensor_reduce(norm[:, n:n + 1], ps[0:H, 4 + n % 4, :], X_AXIS, ALU.max)\
                        .then_inc(norm_read, 1)
                dve.wait_ge(norm_read, 2 * NCH)
                link(nc.vector.tensor_reduce(most[:, 0:2], norm[:].rearrange("h (s c) -> h s c", s=2), X_AXIS, ALU.max))
                nc.vector.tensor_tensor(most[:, 2:3], most[:, 0:1], most[:, 1:2], ALU.mult).then_inc(product, 1)
                dve.wait_ge(reduced, 1)
                nc.vector.tensor_scalar(safe[:], most[:, 3:4], 1.0625 * SCALE * SCALE, SAFE_ARGUMENT ** 2,
                                        ALU.mult, ALU.is_le)

            @block.tensor
            def _(pe):
                pe.wait_ge(k.a0_loaded, 48)
                for n in range(2 * NCH):
                    c = n % NCH
                    nc.tensor.matmul(ps[:, n, :], (wq, wk)[n // NCH][:], k.xnT[:, c * CH:(c + 1) * CH],
                                     start=True, stop=True).then_inc(projected, 1)
                for t in range(NT):
                    pe.wait_ge(squared, t // TPC + 1)
                    last = nc.tensor.matmul(ps[:, t // TPC, (t % TPC) * P:(t % TPC + 1) * P],
                                            k.xnT[:, t * P:(t + 1) * P], wk[:], start=True, stop=True)
                    if t % TPC == TPC - 1:
                        last.then_inc(v_projected, 1)
                pe.wait_ge(squared, 2 * NCH)
                pe.wait_ge(filled, 5)
                for n in range(2 * NCH):
                    if n >= 4:
                        pe.wait_ge(norm_read, n - 3)
                    nc.tensor.matmul(ps[0:H, 4 + n % 4, :], head_rows[:], square[:, n, :], start=True, stop=True)\
                        .then_inc(normed, 1)

        k_rows = sb("k_rows", [ROWS, 2, G, S], BF16)
        q_rows = sb("q_rows", [ROWS, 2, G, S], BF16)
        probs = sb("probs", [P, PROBS, 2, CH])
        weighted = sb("weighted", [P, CH])
        inverse = sb("inverse", [P, CH])
        attended = sb("attended", [P, CH])
        running_max = sb("running_max", [P, CH])
        minus_max = sb("minus_max", [P, TPC])
        shift = sb("shift", [P, G, TPC, P])

        loaded = sem("loaded")
        v_ready, score_done, exp_done, pv_done = sem("v_ready"), sem("score_done"), sem("exp_done"), sem("pv_done")
        acc_copied, sums_done, inverse_ready, attended_ready, out_done, x_added = (
            sem("acc_copied"), sem("sums_done"), sem("inverse_ready"), sem("attended_ready"), sem("out_done"),
            sem("x_added"))
        max_score, max_taken, max_turned, max_read, shift_ready = (
            sem("max_score"), sem("max_taken"), sem("max_turned"), sem("max_read"), sem("shift_ready"))
        LOADS = PARTS * PARTS + PARTS
        block = ctx.enter_context(nc.Block())

        @block.sync
        def _(sp):
            for g in range(NG):
                if g >= 1:
                    sp.wait_ge(loaded, g * (LOADS * 16))
                if g >= 2:
                    sp.wait_ge(pv_done, NCH * (g - 1) * JT + PROBS)
                for b in range(PARTS):
                    for a in range(PARTS):
                        r = (b * PARTS + a) * D
                        sp.dma_start(k_rows[r:r + D, g % 2, :, :],
                                     k_dram[g * G:(g + 1) * G, b].rearrange("h d t -> d h t"))\
                            .then_inc(loaded, 16)
                    r = b * PARTS * D
                    sp.dma_start(q_rows[r:r + PARTS * D, g % 2, :, :],
                                 q_dram[g * G:(g + 1) * G].rearrange("h a d t -> (a d) h t"))\
                        .then_inc(loaded, 16)

        @block.scalar
        def _(act):
            act.sem_inc(exp_done, RING)
            with act.Fori(0, NG) as g:
                for n in range(NCH * JT):
                    act.wait_ge(score_done, g * (NCH * JT) + (n + 1))
                    act.wait_ge(pv_done, g * (NCH * JT) + (n + 1))
                    bank = 2 * (n % JT % RING)
                    nc.scalar.activation(probs[:, n % PROBS, :, :], ps[:, bank:bank + 2, :],
                                         ACT.Exp, scale=SCALE).then_inc(exp_done, 1)

        def dve_program(dve, guarded):
            def strip_values(g, slot):
                nc.vector.tensor_copy(v_strip[:, slot, :, :, 0:D],
                                      values[:, :, bass.ds(g * (G * D), G * D)].rearrange("p t (h d) -> p t h d", d=D))\
                    .then_inc(v_ready, 1)

            def row_maxima(it):
                for n in range(G * NT):
                    h, kt = n // NT, n % NT
                    dve.wait_ge(max_score, it * (G * NT) + (n + 1))
                    if kt == 0:
                        ins = nc.vector.tensor_copy(running_max[:], ps[:, n % 2, :])
                    else:
                        ins = nc.vector.tensor_tensor(running_max[:], ps[:, n % 2, :], running_max[:], ALU.max)
                    ins.then_inc(max_taken, 1)
                    dve.wait_ge(max_taken, it * (G * NT) + (n + 1 + TURNS))
                    if kt == NT - 1:
                        dve.wait_ge(max_turned, it * G + (h + 1))
                        nc.vector.tensor_reduce(minus_max[:], ps[:, 2, :].rearrange("p (i k) -> p i k", i=TPC),
                                                X_AXIS, ALU.max, negate=True).then_inc(max_read, 1)
                        dve.wait_ge(max_read, it * G + (h + 2))
                        for i in range(TPC):
                            ins = nc.vector.tensor_scalar(shift[:, h, i, :], k.ident[:], minus_max[:, i:i + 1], None,
                                                          ALU.mult)
                        ins.then_inc(shift_ready, 1)

            def epilogue(it, qc):
                dve.wait_ge(pv_done, (it + 1) * JT + PROBS)
                nc.vector.tensor_copy(weighted[:], ps[:, ACC, :]).then_inc(acc_copied, 1)
                dve.wait_ge(sums_done, it + 1)
                nc.vector.reciprocal(inverse[:], ps[:, EPI, :]).then_inc(inverse_ready, 1)
                dve.wait_ge(inverse_ready, it + 1)
                nc.vector.tensor_tensor(attended[:], weighted[:], inverse[:], ALU.mult).then_inc(attended_ready, 1)
                dve.wait_ge(out_done, it + 1)
                rows = k.x[:, bass.ds(qc * TPC, TPC), :]
                nc.vector.tensor_tensor(rows, rows, ps[:, EPI, :].rearrange("p (i m) -> p i m", m=M), ALU.add)\
                    .then_inc(x_added, 1)

            strip_values(0, 0)
            with dve.Fori(0, NG // 2) as gg:
                for par in range(2):
                    g = gg * 2 + par
                    strip_values((g + 1) % NG, 1 - par)
                    with dve.Fori(0, NCH) as qc:
                        if guarded:
                            row_maxima(g * NCH + qc)
                        epilogue(g * NCH + qc, qc)

        @block.vector
        def _(dve):
            dve.sem_inc(max_taken, TURNS)
            is_safe = dve.value_load(safe[0:1, 0:1], min_val=0, max_val=1)
            with dve.If(is_safe == 1):
                dve_program(dve, guarded=False)
            with dve.Else():
                dve_program(dve, guarded=True)

        def pe_program(pe, guarded):
            def score(out, slot, h, kt, q0, last):
                k_flat = k_rows[:].rearrange("r b h t -> r (b h t)")
                q_flat = q_rows[:].rearrange("r b h t -> r (b h t)")
                return nc.tensor.matmul(out, k_flat[:, bass.ds(slot * (G * S) + (h * S + kt * P), P)],
                                        q_flat[:, bass.ds(slot * (G * S) + (h * S + q0), CH)], start=True, stop=last)

            def scores(it, par, qc, j):
                kt, pair = j // 2, j % 2
                before = j - RING if j >= RING else max(t for t in range(JT) if t % RING == j) - JT
                pe.wait_ge(exp_done, it * JT + (before + 1 + RING))
                for hh in range(2):
                    bank = 2 * (j % RING) + hh
                    ins = score(ps[:, bank, :], par, 2 * pair + hh, kt, qc * CH, not guarded)
                    if guarded:
                        ins = nc.tensor.matmul(ps[:, bank, :], k.ones[:], shift[:, 2 * pair + hh, :, :],
                                               start=False, stop=True)
                ins.then_inc(score_done, 1)

            def weigh(it, par, j):
                kt, pair = j // 2, j % 2
                pe.wait_ge(exp_done, it * JT + (j + 1 + RING))
                if j == 0:
                    pe.wait_ge(acc_copied, it + 1)
                for hh in range(2):
                    h = 2 * pair + hh
                    last = nc.tensor.matmul(ps[W * h:W * (h + 1), ACC, :], v_strip[:, par, kt, h, :],
                                            probs[:, j % PROBS, hh, :], start=(kt == 0), stop=(kt == NT - 1))
                last.then_inc(pv_done, 1)

            def sums(n):
                pe.wait_ge(acc_copied, n + 1)
                pe.wait_ge(x_added, n)
                nc.tensor.matmul(ps[:, EPI, :], sum_row[:], weighted[:], start=True, stop=True).then_inc(sums_done, 1)

            def project(n, g):
                pe.wait_ge(attended_ready, n)
                for i in range(TPC):
                    last = nc.tensor.matmul(ps[:, EPI, i * P:(i + 1) * P], attended[:, i * P:(i + 1) * P],
                                            wo[:, :, :].rearrange("p g m -> p (g m)")[:, bass.ds(g * M, M)],
                                            start=True, stop=True)
                last.then_inc(out_done, 1)

            def row_maxima(it, par, qc):
                pe.wait_ge(exp_done, it * JT + RING)
                for n in range(G * NT):
                    h, kt = n // NT, n % NT
                    pe.wait_ge(max_taken, it * (G * NT) + (n + 1))
                    score(ps[:, n % 2, :], par, h, kt, qc * CH, True).then_inc(max_score, 1)
                    if kt == NT - 1:
                        pe.wait_ge(max_taken, it * (G * NT) + (n + 1 + TURNS))
                        pe.wait_ge(max_read, it * G + (h + 1))
                        for i in range(TPC):
                            last = nc.tensor.transpose(ps[:, 2, i * P:(i + 1) * P], running_max[:, i * P:(i + 1) * P],
                                                       k.ident[:])
                        last.then_inc(max_turned, 1)
                pe.wait_ge(shift_ready, it * G + G)

            if not guarded:
                pe.wait_ge(loaded, LOADS * 16)
                for j in range(RING):
                    scores(0, 0, 0, j)
            with pe.Fori(0, NG // 2) as gg:
                for par in range(2):
                    g = gg * 2 + par
                    with pe.Fori(0, NCH) as qc:
                        pe.wait_ge(v_ready, g + 1)
                        it = g * NCH + qc
                        if guarded:
                            pe.wait_ge(loaded, (g + 1) * (LOADS * 16))
                            row_maxima(it, par, qc)
                            for j in range(RING):
                                scores(it, par, qc, j)
                        for j in range(JT):
                            if j + RING < JT:
                                scores(it, par, qc, j + RING)
                            weigh(it, par, j)
                            if not guarded and j + RING >= JT:
                                group = (it + 1) // NCH % NG
                                if j + RING == JT:
                                    pe.wait_ge(loaded, (group + 1) * (LOADS * 16))
                                scores(it + 1, group % 2, (qc + 1) % NCH, j + RING - JT)
                            if not guarded and j == 4:
                                with pe.If(it > 0):
                                    sums(it)
                            if not guarded and j == 10:
                                with pe.If(it > 0):
                                    project(it, (it + NI - 1) // NCH % NG)
                        if guarded:
                            sums(it + 1)
                            project(it + 1, g)
            if not guarded:
                sums(NI)
                project(NI, NG - 1)

        @block.tensor
        def _(pe):
            pe.sem_inc(pv_done, PROBS)
            pe.sem_inc(x_added, 1)
            pe.sem_inc(acc_copied, 1)
            pe.sem_inc(max_read, 1)
            is_safe = pe.value_load(safe[0:1, 0:1], min_val=0, max_val=1)
            with pe.If(is_safe == 1):
                pe_program(pe, guarded=False)
            with pe.Else():
                pe_program(pe, guarded=True)


def attention_wide(k):
    nc, ps, d = k.nc, k.ps, k.dram
    H, D = 16, 64
    NP = H // 2
    SCALE = float(D) ** -0.5
    NI = NP * NCH
    RING, PROBS = 2, 8
    ACC, EPI, QV, KB = 4, 5, 6, 7
    ADDS = NT - 2

    with ExitStack() as ctx:
        def sb(name, shape, dt=F32):
            return ctx.enter_context(nc.sbuf_tensor(f"s_a1_{name}", shape, dt))

        def sem(name):
            return nc.alloc_semaphore(f"a1_{name}")

        safe = sb("safe", [P, 1], I32)
        w_all, wp = k.a1_w, k.a1_wp

        k_rows = sb("k_rows", [P, 2, 2, S], F32R)
        q_rows = sb("q_rows", [P, 2, 2, 2, CH], F32R)
        values = sb("values", [P, 2, NT, P])

        def hi_halves(rows, source, order):
            out = []
            for s in range(2):
                half = s ^ order
                out.append((rows(s, order)[D * half:D * (half + 1)], source[D * s:D * (s + 1)]))
            return out

        def lo_halves(rows, source, order):
            out = []
            for s in range(2):
                half = s ^ order
                out.append((rows(s, order)[D * (1 - half):D * (2 - half)], source[D * s:D * (s + 1)],
                            rows(s, 0)[D * s:D * (s + 1)]))
            return out

        def q_at(slot):
            flat = q_rows[:].rearrange("p i s o c -> p (i s o c)")
            return lambda s, order: flat[:, bass.ds(slot * (4 * CH) + (2 * s + order) * CH, CH)]

        def k_at(par, c0):
            return lambda s, order: k_rows[:, par, s, bass.ds(c0, CH)]

        with ExitStack() as prep:
            def psb(name, shape, dt=F32):
                return prep.enter_context(nc.sbuf_tensor(f"s_a1_{name}", shape, dt))

            xn = psb("xn", [P, NT, M])
            layernorm(k, xn, "a1")
            SQUARES = 8
            x_hi = psb("x_hi", [M, S], F32R)
            w_hi = psb("w_hi", [M, 2, NP, P], F32R)
            w_square = psb("w_square", [M, 2, H * D], BF16)
            square = psb("square", [P, SQUARES, CH], BF16)
            head_rows = psb("head_rows", [P, NP, P // NCH], BF16)
            rounded = psb("rounded", [P, 2, CH], BF16)
            norm = psb("norm", [P, 8])
            w_norm = psb("w_norm", [P, 4])
            filled, hi_ready, w_squared, w_reduced = sem("filled"), sem("hi_ready"), sem("w_squared"), sem("w_reduced")
            projected, normed = sem("projected"), sem("normed")
            squared = {"act": sem("squared_by_act"), "dve": sem("squared_by_dve")}
            dve_step, most_ready, reduced = sem("dve_step"), sem("most_ready"), sem("reduced")
            piece_done, hi_done, lo_done, v_done = sem("first_piece"), sem("first_hi"), sem("first_lo"), sem("first_v")
            steps = [(side, p, c) for side in range(2) for p in range(NP) for c in range(NCH)]
            GROUPS = len(steps) // NCH
            KQ = NCH + 1
            PIECES = KQ + NCH

            def squarer(n):
                return "dve" if n % 3 == 1 else "act"

            def squares_of(engine, n):
                return sum(squarer(m) == engine for m in range(n + 1))

            def piece_bank(i):
                return 6 + i % 2

            def piece_halves(fn, i):
                if i < NCH:
                    return fn(k_at(0, i * CH), ps[:, piece_bank(i), :], 0)
                return fn(q_at(0), ps[:, piece_bank(i), :], 0) + fn(q_at(0), ps[:, piece_bank(i), :], 1)

            block = prep.enter_context(nc.Block())

            @block.gpsimd
            def _(pool):
                nc.gpsimd.memset(head_rows[:], 0.0).then_inc(filled, 1)
                pool.wait_ge(filled, 1)
                for s in range(2):
                    half = head_rows[D * s:D * (s + 1), :, :]
                    nc.gpsimd.affine_select(out=half, in_=half, compare_op=ALU.not_equal, fill=1.0,
                                            base=-s, pattern=[[-2, NP], [1, P // NCH]], channel_multiplier=0)\
                        .then_inc(filled, 1)
                pool.wait_ge(filled, 3)
                pool.wait_ge(k.a1_loaded, 96)
                nc.gpsimd.tensor_tensor(k.x[:], k.x[:], k.a1_bp[:].unsqueeze(1).to_broadcast([P, NT, M]), ALU.add)
                pool.wait_ge(w_squared, 2)
                nc.gpsimd.partition_all_reduce(w_norm[:, 2:4], w_norm[:, 0:2], P, RADD).then_inc(w_reduced, 1)
                pool.wait_ge(most_ready, 1)
                nc.gpsimd.partition_all_reduce(norm[:, 2:4], norm[:, 0:2], P, RMAX).then_inc(reduced, 1)

            @block.scalar
            def _(act):
                def square_step(n):
                    act.wait_ge(projected, n + 1)
                    if n >= SQUARES:
                        act.wait_ge(normed, n - SQUARES + 1)
                    nc.scalar.activation(square[:, n % SQUARES, :], ps[:, n % 4, :], ACT.Square)\
                        .then_inc(squared["act"], 1)

                def piece(i):
                    act.wait_ge(piece_done, i + 1)
                    if i < KQ:
                        for dst, src in piece_halves(hi_halves, i):
                            last = nc.scalar.activation(dst, src, ACT.Copy)
                        last.then_inc(hi_done, 1)
                    else:
                        c = i - KQ
                        nc.scalar.activation(values[:, 0, c * TPC:(c + 1) * TPC, :], ps[:, piece_bank(i), :],
                                             ACT.Copy).then_inc(v_done, 1)

                act.wait_ge(k.a1_loaded, 96)
                for side in range(2):
                    nc.scalar.activation(w_square[:, side, :], w_all[:, side, :, :].rearrange("m h e -> m (h e)"),
                                         ACT.Square, accum_out=w_norm[:, side:side + 1]).then_inc(w_squared, 1)
                piece(0)
                for g in range(GROUPS):
                    for n in range(g * NCH, (g + 1) * NCH):
                        if squarer(n) == "act":
                            square_step(n)
                    if g + 1 < PIECES:
                        piece(g + 1)

            @block.vector
            def _(dve):
                done = [0]

                def link(ins):
                    done[0] += 1
                    ins.then_inc(dve_step, 1)
                    dve.wait_ge(dve_step, done[0])

                def square_step(n):
                    dve.wait_ge(projected, n + 1)
                    if n >= SQUARES:
                        dve.wait_ge(normed, n - SQUARES + 1)
                    value = rounded[:, n // 3 % 2, :]
                    link(nc.vector.tensor_copy(value, ps[:, n % 4, :]))
                    nc.vector.tensor_tensor(square[:, n % SQUARES, :], value, value, ALU.mult)\
                        .then_inc(squared["dve"], 1)

                def piece(i):
                    dve.wait_ge(hi_done, i + 1)
                    for dst, src, hi in piece_halves(lo_halves, i):
                        last = nc.vector.tensor_tensor(dst, src, hi.bitcast(F32), ALU.subtract)
                    last.then_inc(lo_done, 1)

                nc.vector.tensor_copy(x_hi[:], k.xnT[:])
                dve.wait_ge(k.a1_loaded, 96)
                nc.vector.tensor_copy(w_hi[:].rearrange("m s p r -> m s (p r)"),
                                      w_all[:, 0:2, :, :].rearrange("m s h e -> m s (h e)")).then_inc(hi_ready, 1)
                piece(0)
                for g in range(GROUPS):
                    for n in range(g * NCH, (g + 1) * NCH):
                        if squarer(n) == "dve":
                            square_step(n)
                    if g + 1 < KQ:
                        piece(g + 1)
                dve.wait_ge(normed, len(steps))
                for side in range(2):
                    last = nc.vector.tensor_reduce(norm[:, side:side + 1], ps[:, 4 + side, :], X_AXIS, ALU.max)
                last.then_inc(most_ready, 1)
                dve.wait_ge(reduced, 1)
                dve.wait_ge(w_reduced, 1)
                link(nc.vector.tensor_scalar(norm[:, 4:6], norm[:, 2:4], 1.08, None, ALU.mult))
                link(nc.vector.scalar_tensor_tensor(out=norm[:, 4:6], in0=w_norm[:, 2:4],
                                                    scalar=18.0 * M * 2.0 ** -22, in1=norm[:, 4:6],
                                                    op0=ALU.mult, op1=ALU.add))
                link(nc.vector.tensor_tensor(norm[:, 6:7], norm[:, 4:5], norm[:, 5:6], ALU.mult))
                nc.vector.tensor_scalar(safe[:], norm[:, 6:7], SCALE * SCALE, SAFE_ARGUMENT ** 2,
                                        ALU.mult, ALU.is_le)

            @block.tensor
            def _(pe):
                def wait_squared(n):
                    pe.wait_ge(squared[squarer(n)], squares_of(squarer(n), n))

                def project(n):
                    side, p, c = steps[n]
                    if n >= 4:
                        wait_squared(n - 4)
                    nc.tensor.matmul(ps[:, n % 4, :], w_hi[:, side, p, :], x_hi[:, c * CH:(c + 1) * CH],
                                     start=True, stop=True).then_inc(projected, 1)

                def head_norms(n):
                    side, p, c = steps[n]
                    rows = P // NCH
                    wait_squared(n)
                    nc.tensor.matmul(ps[rows * c:rows * (c + 1), 4 + side, :], head_rows[:, p, :],
                                     square[:, n % SQUARES, :], start=(p == 0), stop=(p == NP - 1)).then_inc(normed, 1)

                def piece(i):
                    bank = piece_bank(i)
                    if i >= 2:
                        if i - 2 < KQ:
                            pe.wait_ge(lo_done, i - 1)
                        else:
                            pe.wait_ge(v_done, i - 1 - KQ)
                    if i < NCH:
                        last = nc.tensor.matmul(ps[:, bank, :], w_all[:, 1, 0:2, :], k.xnT[:, i * CH:(i + 1) * CH],
                                                start=True, stop=True)
                    elif i < KQ:
                        last = nc.tensor.matmul(ps[:, bank, :], w_all[:, 0, 0:2, :], k.xnT[:, 0:CH],
                                                start=True, stop=True)
                    else:
                        for t in range(TPC):
                            first = ((i - KQ) * TPC + t) * P
                            last = nc.tensor.matmul(ps[:, bank, t * P:(t + 1) * P], k.xnT[:, first:first + P],
                                                    w_all[:, 2, 0:2, :], start=True, stop=True)
                    last.then_inc(piece_done, 1)

                pe.wait_ge(k.a1_loaded, 96)
                piece(0)
                pe.wait_ge(hi_ready, 1)
                pe.wait_ge(filled, 3)
                for g in range(GROUPS + 1):
                    for n in range(g * NCH, (g + 1) * NCH):
                        if g < GROUPS:
                            project(n)
                    if g >= 1:
                        for n in range((g - 1) * NCH, g * NCH):
                            head_norms(n)
                    if g + 1 < PIECES:
                        piece(g + 1)

        probs = sb("probs", [P, PROBS, 2, CH])
        part_sum = sb("part_sum", [P, 2, 2, CH])
        weight_sum = sb("weight_sum", [P, 2, CH])
        wq_now, wk_now, wv_now = sb("wq_now", [M, P]), sb("wk_now", [M, P]), sb("wv_now", [M, P])
        x_now = sb("x_now", [M, CH])
        weighted = sb("weighted", [P, CH])
        inverse = sb("inverse", [P, CH])
        attended = sb("attended", [P, CH])
        running_max = sb("running_max", [P, CH])
        minus_max = sb("minus_max", [P, TPC])
        shift = sb("shift", [P, 2, TPC, P])

        v_out, q_hi, k_hi, q_lo, k_lo = sem("v_out"), sem("q_hi"), sem("k_hi"), sem("q_lo"), sem("k_lo")
        q_proj, k_proj, v_proj, staged = sem("q_proj"), sem("k_proj"), sem("v_proj"), sem("staged")
        score_done, exp_done, pv_done, summed = sem("score_done"), sem("exp_done"), sem("pv_done"), sem("summed")
        total_ready, acc_copied, sums_done, inverse_ready = (sem("total_ready"), sem("acc_copied"), sem("sums_done"),
                                                             sem("inverse_ready"))
        attended_ready, out_done, x_added = sem("attended_ready"), sem("out_done"), sem("x_added")
        max_score, max_taken, max_turned, max_read, shift_ready = (
            sem("max_score"), sem("max_taken"), sem("max_turned"), sem("max_read"), sem("shift_ready"))
        block = ctx.enter_context(nc.Block())

        def pairs(eng):
            with eng.Fori(0, NP // 2) as pp:
                for par in range(2):
                    with eng.Fori(0, NCH) as qc:
                        pair = pp * 2 + par
                        yield pair, par, qc, pair * NCH + qc

        def additions_over(t):
            return t + 1 if t < 2 else t - 1

        @block.gpsimd
        def _(pool):
            for pair, par, qc, it in pairs(pool):
                pool.wait_ge(v_proj, it + 1)
                flat = w_all[:].rearrange("m w h e -> m w (h e)")
                nc.gpsimd.tensor_copy(wq_now[:], flat[:, 0, bass.ds((it + 1) // NCH % NP * P, P)])
                nc.gpsimd.tensor_copy(wk_now[:], flat[:, 1, bass.ds((pair + 1) % NP * P, P)])
                nc.gpsimd.tensor_copy(wv_now[:], flat[:, 2, bass.ds((pair + 1) % NP * P, P)])
                nc.gpsimd.tensor_copy(x_now[:], k.xnT[:, bass.ds(qc * CH, CH)]).then_inc(staged, 1)

        @block.scalar
        def _(act):
            act.sem_inc(exp_done, RING)
            for pair, par, qc, it in pairs(act):
                for j in range(NT):
                    act.wait_ge(score_done, it * NT + (j + 1))
                    act.wait_ge(pv_done, it * NT + (j + 1))
                    taken = additions_over(j - PROBS) + ADDS if j >= PROBS else additions_over(NT + j - PROBS)
                    act.wait_ge(summed, it * ADDS + taken)
                    nc.scalar.activation(probs[:, j % PROBS, :, :], ps[:, 2 * (j % RING):2 * (j % RING) + 2, :],
                                         ACT.Exp, scale=SCALE).then_inc(exp_done, 1)
                    if j in (3, 4):
                        if j == 3:
                            act.wait_ge(q_proj, it + 1)
                        for dst, src in hi_halves(q_at((it + 1) % 2), ps[:, QV, :], j - 3):
                            nc.scalar.activation(dst, src, ACT.Copy).then_inc(q_hi, 1)
                    if j in (6, 7):
                        if j == 6:
                            act.wait_ge(k_proj, it + 1)
                        dst, src = hi_halves(k_at(1 - par, qc * CH), ps[:, KB, :], 0)[j - 6]
                        nc.scalar.activation(dst, src, ACT.Copy).then_inc(k_hi, 1)
                    if j == 12:
                        act.wait_ge(v_proj, it + 2)
                        nc.scalar.activation(values[:, 1 - par, bass.ds(qc * TPC, TPC), :], ps[:, QV, :], ACT.Copy)\
                            .then_inc(v_out, 1)

        def dve_program(dve, guarded):
            def row_maxima(it):
                for n in range(2 * NT):
                    s, kt = n // NT, n % NT
                    dve.wait_ge(max_score, it * (2 * NT) + (n + 1))
                    if kt == 0:
                        ins = nc.vector.tensor_copy(running_max[:], ps[:, n % 2, :])
                    else:
                        ins = nc.vector.tensor_tensor(running_max[:], ps[:, n % 2, :], running_max[:], ALU.max)
                    ins.then_inc(max_taken, 1)
                    dve.wait_ge(max_taken, it * (2 * NT) + (n + 1 + RING))
                    if kt == NT - 1:
                        dve.wait_ge(max_turned, it * 2 + (s + 1))
                        nc.vector.tensor_reduce(minus_max[:], ps[:, 2, :].rearrange("p (i k) -> p i k", i=TPC),
                                                X_AXIS, ALU.max, negate=True).then_inc(max_read, 1)
                        dve.wait_ge(max_read, it * 2 + (s + 2))
                        for i in range(TPC):
                            ins = nc.vector.tensor_scalar(shift[:, s, i, :], k.ident[:], minus_max[:, i:i + 1], None,
                                                          ALU.mult)
                        ins.then_inc(shift_ready, 1)

            def take_weighted(n):
                dve.wait_ge(pv_done, n * NT + PROBS)
                nc.vector.tensor_copy(weighted[:], ps[:, ACC, :]).then_inc(acc_copied, 1)

            def divide(n):
                dve.wait_ge(sums_done, n)
                nc.vector.reciprocal(inverse[:], ps[:, EPI, :]).then_inc(inverse_ready, 1)
                dve.wait_ge(inverse_ready, n)
                nc.vector.tensor_tensor(attended[:], weighted[:], inverse[:], ALU.mult).then_inc(attended_ready, 1)

            def add_to_x(n, qc):
                dve.wait_ge(out_done, n)
                rows = k.x[:, bass.ds(qc * TPC, TPC), :]
                nc.vector.tensor_tensor(rows, rows, ps[:, EPI, :].rearrange("p (i m) -> p i m", m=M), ALU.add)\
                    .then_inc(x_added, 1)

            for pair, par, qc, it in pairs(dve):
                if guarded:
                    row_maxima(it)
                dve.wait_ge(total_ready, it + 1)
                for j in range(2, NT):
                    dve.wait_ge(exp_done, it * NT + (j + 1 + RING))
                    if j < 4:
                        other = probs[:, (j - 2) % PROBS, :, :]
                    else:
                        dve.wait_ge(summed, it * ADDS + (ADDS + j - 3))
                        other = part_sum[:, j % 2, :, :]
                    nc.vector.tensor_tensor(part_sum[:, j % 2, :, :], probs[:, j % PROBS, :, :], other, ALU.add)\
                        .then_inc(summed, 1)
                    if j == 3 and not guarded:
                        with dve.If(it > 0):
                            divide(it)
                    if j in (5, 6):
                        dve.wait_ge(q_hi, it * 4 + (2 * j - 8))
                        for dst, src, hi in lo_halves(q_at((it + 1) % 2), ps[:, QV, :], j - 5):
                            last = nc.vector.tensor_tensor(dst, src, hi.bitcast(F32), ALU.subtract)
                        if j == 6:
                            last.then_inc(q_lo, 1)
                    if j in (8, 9):
                        dve.wait_ge(k_hi, it * 2 + (j - 7))
                        dst, src, hi = lo_halves(k_at(1 - par, qc * CH), ps[:, KB, :], 0)[j - 8]
                        last = nc.vector.tensor_tensor(dst, src, hi.bitcast(F32), ALU.subtract)
                        if j == 9:
                            last.then_inc(k_lo, 1)
                    if j == 12 and not guarded:
                        with dve.If(it > 0):
                            add_to_x(it, (qc + NCH - 1) % NCH)
                dve.wait_ge(summed, it * ADDS + 2 * ADDS)
                nc.vector.tensor_tensor(weight_sum[:], part_sum[:, 0, :, :], part_sum[:, 1, :, :], ALU.add)\
                    .then_inc(total_ready, 1)
                take_weighted(it + 1)
                if guarded:
                    divide(it + 1)
                    add_to_x(it + 1, qc)
            if not guarded:
                divide(NI)
                add_to_x(NI, NCH - 1)

        @block.vector
        def _(dve):
            dve.sem_inc(max_taken, RING)
            dve.sem_inc(summed, ADDS)
            dve.sem_inc(total_ready, 1)
            is_safe = dve.value_load(safe[0:1, 0:1], min_val=0, max_val=1)
            with dve.If(is_safe == 1):
                dve_program(dve, guarded=False)
            with dve.Else():
                dve_program(dve, guarded=True)

        def pe_program(pe, guarded):
            def score(out, par, s, kt, it, last):
                for order in range(2):
                    ins = nc.tensor.matmul(out, k_rows[:, par, s, kt * P:(kt + 1) * P], q_at(it % 2)(s, order),
                                           start=(order == 0), stop=(order == 1 and last))
                return ins

            def scores(it, par, j):
                pe.wait_ge(exp_done, it * NT + (j + 1))
                for s in range(2):
                    bank = 2 * (j % RING) + s
                    ins = score(ps[:, bank, :], par, s, j, it, not guarded)
                    if guarded:
                        ins = nc.tensor.matmul(ps[:, bank, :], k.ones[:], shift[:, s, :, :], start=False, stop=True)
                ins.then_inc(score_done, 1)

            def weigh(it, par, j):
                pe.wait_ge(exp_done, it * NT + (j + 1 + RING))
                if j == 0:
                    pe.wait_ge(acc_copied, it + 1)
                for s in range(2):
                    last = nc.tensor.matmul(ps[D * s:D * (s + 1), ACC, :], values[:, par, j, D * s:D * (s + 1)],
                                            probs[:, j % PROBS, s, :], start=(j == 0), stop=(j == NT - 1))
                last.then_inc(pv_done, 1)

            def sums(n):
                pe.wait_ge(total_ready, n + 1)
                pe.wait_ge(x_added, n)
                for s in range(2):
                    last = nc.tensor.matmul(ps[D * s:D * (s + 1), EPI, :], k.ones[:, 0:D], weight_sum[:, s, :],
                                            start=True, stop=True)
                last.then_inc(sums_done, 1)

            def project(n, pair):
                pe.wait_ge(attended_ready, n)
                for i in range(TPC):
                    last = nc.tensor.matmul(ps[:, EPI, i * P:(i + 1) * P], attended[:, i * P:(i + 1) * P],
                                            wp[:].rearrange("p g m -> p (g m)")[:, bass.ds(pair * M, M)],
                                            start=True, stop=True)
                last.then_inc(out_done, 1)

            def row_maxima(it, par):
                pe.wait_ge(exp_done, it * NT + RING)
                for n in range(2 * NT):
                    s, kt = n // NT, n % NT
                    pe.wait_ge(max_taken, it * (2 * NT) + (n + 1))
                    score(ps[:, n % 2, :], par, s, kt, it, True).then_inc(max_score, 1)
                    if kt == NT - 1:
                        pe.wait_ge(max_taken, it * (2 * NT) + (n + 1 + RING))
                        pe.wait_ge(max_read, it * 2 + (s + 1))
                        for i in range(TPC):
                            last = nc.tensor.transpose(ps[:, 2, i * P:(i + 1) * P], running_max[:, i * P:(i + 1) * P],
                                                       k.ident[:])
                        last.then_inc(max_turned, 1)
                pe.wait_ge(shift_ready, it * 2 + 2)

            def operands_ready(it):
                pe.wait_ge(q_lo, it + 1)
                pe.wait_ge(k_lo, it + 1)

            if not guarded:
                operands_ready(0)
                for j in range(RING):
                    scores(0, 0, j)
            for pair, par, qc, it in pairs(pe):
                pe.wait_ge(v_out, it + 1)
                if guarded:
                    operands_ready(it)
                    row_maxima(it, par)
                    for j in range(RING):
                        scores(it, par, j)
                for j in range(NT):
                    if j + RING < NT:
                        scores(it, par, j + RING)
                    if j + RING == NT and not guarded:
                        operands_ready(it + 1)
                        with pe.If(qc < NCH - 1):
                            for first in range(RING):
                                scores(it + 1, par, first)
                        with pe.Else():
                            for first in range(RING):
                                scores(it + 1, 1 - par, first)
                    weigh(it, par, j)
                    if j == 1:
                        pe.wait_ge(staged, it + 1)
                        nc.tensor.matmul(ps[:, QV, :], wq_now[:], k.xnT[:, bass.ds((qc + 1) % NCH * CH, CH)],
                                         start=True, stop=True).then_inc(q_proj, 1)
                    if j == 3 and not guarded:
                        with pe.If(it > 0):
                            sums(it)
                    if j == 4:
                        nc.tensor.matmul(ps[:, KB, :], wk_now[:], x_now[:], start=True, stop=True).then_inc(k_proj, 1)
                    if j == 9 and not guarded:
                        with pe.If(it > 0):
                            project(it, (it + NI - 1) // NCH % NP)
                    if j == 10:
                        pe.wait_ge(q_lo, it + 2)
                        for i in range(TPC):
                            last = nc.tensor.matmul(ps[:, QV, i * P:(i + 1) * P], x_now[:, i * P:(i + 1) * P],
                                                    wv_now[:], start=True, stop=True)
                        last.then_inc(v_proj, 1)
                if guarded:
                    sums(it + 1)
                    project(it + 1, pair)
            if not guarded:
                sums(NI)
                project(NI, NP - 1)

        @block.tensor
        def _(pe):
            pe.sem_inc(pv_done, PROBS)
            for ahead in (x_added, acc_copied, max_read, v_proj, q_lo, k_lo, v_out):
                pe.sem_inc(ahead, 1)
            is_safe = pe.value_load(safe[0:1, 0:1], min_val=0, max_val=1)
            with pe.If(is_safe == 1):
                pe_program(pe, guarded=False)
            with pe.Else():
                pe_program(pe, guarded=True)


def macaron(nc, dram):
    with ExitStack() as ctx:
        k = Kernel(nc, ctx, dram)

        def run(*stages):
            for stage in stages:
                with nc.cleanup_on_exit():
                    stage(k)

        run(constants, lambda k: moe_top1(k, "a", load_weights), attention_small, lambda k: moe_top1(k, "b"))
        k.top1_weights.close()
        run(lambda k: moe_top2(k, "c"), attention_wide, lambda k: moe_top2(k, "d"), store)


INPUTS = {
    "x": "L0_attn_x",
    "t1_wg": "L0_ffn_wg", "t1_w1": "L0_ffn_w1", "t1_b1": "L0_ffn_b1", "t1_w2": "L0_ffn_w2", "t1_b2": "L0_ffn_b2",
    "a0_wk": "L0_attn_Wk", "a0_wq": "L0_attn_Wq", "a0_wo": "L0_attn_Wo", "a0_bo": "L0_attn_bo",
    "t2_router": "L1_ffn_router_w", "t2_w1": "L1_ffn_w1", "t2_w2": "L1_ffn_w2",
    "a1_wq": "L1_attn_Wq", "a1_wk": "L1_attn_Wk", "a1_wv": "L1_attn_Wv", "a1_wp": "L1_attn_Wp", "a1_bp": "L1_attn_bp",
}


def kernel(**inputs):
    import numpy as np
    import concourse.bacc as bacc
    from concourse.bass_utils import run_bass_kernel_spmd

    nc = bacc.Bacc("TRN2", target_bir_lowering=False, num_devices=1)
    arrays, dram = {}, {}
    for short, name in INPUTS.items():
        a = np.asarray(inputs[name])
        a = np.ascontiguousarray(a.T if short == "t2_router" else a)
        arrays[f"in_{name}_dram"] = a
        dram[short] = nc.dram_tensor(f"in_{name}_dram", a.shape, mybir.dt.from_np(a.dtype), kind="ExternalInput").ap()
    dram["out"] = nc.dram_tensor("out_0_dram", (1, S, M), F32, kind="ExternalOutput").ap()
    macaron(nc, dram)
    r = run_bass_kernel_spmd(nc, [arrays], core_ids=[0])
    return r.results[0]["out_0_dram"]
```

```python
from contextlib import ExitStack

import concourse.bass as bass
from concourse import mybir

ALU = mybir.AluOpType
ACT = mybir.ActivationFunctionType
X_AXIS = mybir.AxisListType.X
F32 = mybir.dt.float32
F32R = mybir.dt.float32r
BF16 = mybir.dt.bfloat16
I32 = mybir.dt.int32
RMAX = bass.bass_isa.ReduceOp.max
RADD = bass.bass_isa.ReduceOp.add

P = 128
S = 2048
M = 128
NT = S // P
CH = 512
NCH = S // CH
TPC = CH // P
E = 8
STRIP = P // NCH
GATE_ROWS, GATE = 6, 7
F0 = 512
FT = F0 // P
CAP = S // E
EPS = 1e-5
SAFE_ARGUMENT = 64.0


def broadcast_last(ap, n):
    return ap.unsqueeze(2).to_broadcast([ap.shape[0], ap.shape[1], n])


class Kernel:

    def __init__(self, nc, ctx, dram):
        self.nc, self.dram = nc, dram

        def sb(name, shape, dt=F32):
            return ctx.enter_context(nc.sbuf_tensor(name, shape, dt))

        self.ps = ctx.enter_context(nc.psum_tensor("banks", [P, 8, CH], F32))
        self.x = sb("x_tokens", [P, NT, M])
        self.xnT = sb("xn_transposed", [M, S])
        self.stats = sb("ln_stats", [P, NT, 6])
        self.ident = sb("ident", [P, P])
        self.ones = sb("ones", [P, P])
        self.ones_r = sb("ones_r", [P, P], F32R)
        self.ones_b = sb("ones_b", [P, P], BF16)
        self.earlier = sb("earlier_tokens", [P, P], BF16)
        self.rank = sb("expert_rank", [P, NT, E])
        self.base_slot = sb("base_slot", [P, E, NT])
        self.scan_keep = sb("scan_keep", [P, E, NT + 1])
        self.slot_of_row = sb("slot_of_row", [P, NT])
        self.t1_wg = sb("t1_wg_all", [M, STRIP])
        self.a0_wq, self.a0_wk = sb("a0_wq_all", [M, M]), sb("a0_wk_all", [M, M])
        self.a0_bo = sb("a0_bo_all", [P, M])
        self.t2_router = sb("t2_router_all", [M, STRIP])
        self.t2_w1 = sb("t2_w1_all", [M, E, P])
        self.t2_w2 = sb("t2_w2_all", [P, E, M])
        self.top1_weights = ctx.enter_context(ExitStack())
        self.t1_w1 = self.top1_weights.enter_context(nc.sbuf_tensor("t1_w1_all", [M, E, F0], F32))
        self.t1_w2 = self.top1_weights.enter_context(nc.sbuf_tensor("t1_w2_all", [P, E, FT, M], F32))
        self.t1_b1 = self.top1_weights.enter_context(nc.sbuf_tensor("t1_b1_all", [P, E, FT], F32))
        self.t1_b2 = self.top1_weights.enter_context(nc.sbuf_tensor("t1_b2_all", [P, E, M], F32))
        self.x_loaded = [nc.alloc_semaphore(f"x_chunk{c}_loaded") for c in range(NCH)]
        self.gate_loaded = nc.alloc_semaphore("gate_weights_loaded")
        self.t1_loaded = nc.alloc_semaphore("t1_weights_loaded")
        self.a0_loaded = nc.alloc_semaphore("a0_weights_loaded")
        self.t2_loaded = nc.alloc_semaphore("t2_weights_loaded")
        self.a1_loaded = nc.alloc_semaphore("a1_weights_loaded")

    def place_attention_weights(self, ctx):
        def sb(name, shape, dt=F32):
            return ctx.enter_context(self.nc.sbuf_tensor(name, shape, dt))

        self.a1_w = sb("a1_w_all", [M, 3, 16, 64])
        self.a1_wp = sb("a1_wp_all", [P, 8, M])
        self.a1_bp = sb("a1_bp_all", [P, M])


def constants(k):
    nc = k.nc
    with ExitStack() as ctx:
        filled, padded = nc.alloc_semaphore("const_filled"), nc.alloc_semaphore("gates_padded")
        block = ctx.enter_context(nc.Block())

        @block.sync
        def _(sp):
            for c in range(NCH):
                sp.dma_start(k.x[:, c * TPC:(c + 1) * TPC, :],
                             k.dram["x"].rearrange("b (t p) m -> p (b t) m", p=P)[:, c * TPC:(c + 1) * TPC, :])\
                    .then_inc(k.x_loaded[c], 16)
            sp.wait_ge(padded, 2)
            sp.dma_start(k.t1_wg[:, 0:E], k.dram["t1_wg"]).then_inc(k.gate_loaded, 16)

        @block.vector
        def _(dve):
            nc.vector.memset(k.t1_wg[:], 0.0).then_inc(padded, 1)
            nc.vector.memset(k.t2_router[:], 0.0).then_inc(padded, 1)
            nc.vector.memset(k.ones_r[:].bitcast(F32), 1.0)
            nc.vector.memset(k.ones_b[:], 1.0)
            for e in range(E):
                nc.vector.memset(k.rank[:, :, e], float(E - e))
                nc.vector.memset(k.base_slot[:, e, :], float(e * CAP))

        @block.gpsimd
        def _(pool):
            nc.gpsimd.memset(k.ident[:], 0.0).then_inc(filled, 1)
            nc.gpsimd.memset(k.ones[:], 1.0).then_inc(filled, 1)
            nc.gpsimd.memset(k.scan_keep[:], 1.0).then_inc(filled, 1)
            nc.gpsimd.iota(k.slot_of_row[:], [[P, NT]], base=0, channel_multiplier=1,
                           allow_small_or_imprecise_dtypes=True)
            pool.wait_ge(filled, 3)
            nc.gpsimd.affine_select(out=k.ident[:], in_=k.ident[:], compare_op=ALU.not_equal, fill=1.0,
                                    base=0, pattern=[[-1, P]], channel_multiplier=1)
            nc.gpsimd.affine_select(out=k.earlier[:], in_=k.ones[:], compare_op=ALU.is_gt, fill=0.0,
                                    base=0, pattern=[[1, P]], channel_multiplier=-1)
            nc.gpsimd.memset(k.scan_keep[:, :, 0], 0.0)

def load_weights(k, sp):
    nc, d = k.nc, k.dram
    sp.dma_start(k.t1_w1[:], d["t1_w1"].rearrange("e m f -> m e f")).then_inc(k.t1_loaded, 16)
    sp.dma_start(k.t1_w2[:], d["t1_w2"].rearrange("e (t f) m -> f e t m", f=P)).then_inc(k.t1_loaded, 16)
    with nc.allow_non_contiguous_dma(reason="the biases, one per hidden unit's partition"):
        sp.dma_start(k.t1_b1[:], d["t1_b1"].rearrange("e (t f) -> f e t", f=P)).then_inc(k.t1_loaded, 16)
    sp.dma_start(k.t1_b2[:], d["t1_b2"].partition_broadcast(P)).then_inc(k.t1_loaded, 16)
    sp.dma_start(k.a0_wq[:], d["a0_wq"]).then_inc(k.a0_loaded, 16)
    sp.dma_start(k.a0_wk[:], d["a0_wk"]).then_inc(k.a0_loaded, 16)
    sp.dma_start(k.a0_bo[:], d["a0_bo"].partition_broadcast(P)).then_inc(k.a0_loaded, 16)
    sp.dma_start(k.t2_router[:, 0:E], d["t2_router"]).then_inc(k.t2_loaded, 16)
    sp.dma_start(k.t2_w1[:], d["t2_w1"].rearrange("e m f -> m e f")).then_inc(k.t2_loaded, 16)
    sp.dma_start(k.t2_w2[:], d["t2_w2"].rearrange("e f m -> f e m")).then_inc(k.t2_loaded, 16)


def load_attention_weights(k, sp):
    nc, d = k.nc, k.dram
    for i, name in enumerate(("a1_wq", "a1_wk", "a1_wv")):
        sp.dma_start(k.a1_w[:, i, :, :], d[name].rearrange("h m e -> m h e")).then_inc(k.a1_loaded, 16)
    for s in range(2):
        sp.dma_start(k.a1_wp[64 * s:64 * (s + 1), :, :],
                     d["a1_wp"].rearrange("(e p s) o -> s e p o", p=8, s=2)[s]).then_inc(k.a1_loaded, 16)
    sp.dma_start(k.a1_bp[:], d["a1_bp"].partition_broadcast(P)).then_inc(k.a1_loaded, 16)


def layernorm(k, xn, tag, gate=None, gate_loaded=None, loads=None, has_stats=False, x_loaded=None, fill=None):
    nc, ps = k.nc, k.ps
    with ExitStack() as ctx:
        def sb(name, shape, dt=F32):
            return ctx.enter_context(nc.sbuf_tensor(f"s_{name}_{tag}", shape, dt))

        def sem(name):
            return nc.alloc_semaphore(f"{name}_{tag}")

        mv = sb("ln_mean_var", [P, NT, 2])
        var = sb("ln_var", [P, NT])
        std = sb("ln_std", [P, NT])
        rstd = sb("ln_rstd", [P, NT])
        newton = sb("ln_newton", [P, NT])
        shift = sb("ln_shift", [P, NT])
        dve_step, scale_ready = sem("ln_dve_step"), sem("ln_scale_ready")
        var_ready, std_ready = sem("ln_var_ready"), sem("ln_std_ready")
        even_ready, odd_ready, transposed = sem("ln_even_ready"), sem("ln_odd_ready"), sem("ln_transposed")
        gate_rows = sb("ln_gate_rows", [P, CH])
        gate_done, gate_copied = sem("ln_gate_done"), sem("ln_gate_copied")
        turned = [sem("ln_even_chunks_turned"), sem("ln_odd_chunks_turned")]
        block = ctx.enter_context(nc.Block())

        if fill:
            @block.gpsimd
            def _(pool):
                fill()

        if loads:
            @block.sync
            def _(sp):
                loads(k, sp)

        @block.vector
        def _(dve):
            done = [0]

            def link(ins):
                done[0] += 1
                ins.then_inc(dve_step, 1)
                dve.wait_ge(dve_step, done[0])

            if not has_stats:
                for t in range(NT):
                    if x_loaded and t % TPC == 0:
                        dve.wait_ge(x_loaded[t // TPC], 16)
                    last = nc.vector.bn_stats(k.stats[:, t, :], k.x[:, t, :])
                link(last)
            for t in range(NT):
                last = nc.vector.bn_aggr(mv[:, t, :], k.stats[:, t, :])
            link(last)
            nc.vector.tensor_scalar(var[:], mv[:, :, 1], EPS, None, ALU.add).then_inc(var_ready, 1)
            dve.wait_ge(std_ready, 1)
            link(nc.vector.reciprocal(rstd[:], std[:]))
            link(nc.vector.tensor_tensor(newton[:], rstd[:], rstd[:], ALU.mult))
            link(nc.vector.tensor_tensor(newton[:], newton[:], var[:], ALU.mult))
            link(nc.vector.tensor_scalar(newton[:], newton[:], -0.5, 1.5, ALU.mult, ALU.add))
            link(nc.vector.tensor_tensor(rstd[:], rstd[:], newton[:], ALU.mult))
            nc.vector.scalar_tensor_tensor(out=shift[:], in0=mv[:, :, 0], scalar=-1.0, in1=rstd[:],
                                           op0=ALU.mult, op1=ALU.mult).then_inc(scale_ready, 1)
            for t in range(0, NT, 2):
                nc.vector.tensor_scalar(xn[:, t, :], k.x[:, t, :], mv[:, t, 0:1], rstd[:, t:t + 1],
                                        ALU.subtract, ALU.mult).then_inc(even_ready, 1)
            for c in range(0, NCH, 2):
                dve.wait_ge(transposed, c + 1)
                nc.vector.tensor_copy(k.xnT[:, c * CH:(c + 1) * CH], ps[:, c, :]).then_inc(turned[0], 1)
            if gate is not None:
                dve.wait_ge(gate_done, 1)
                nc.vector.tensor_copy(gate_rows[:], ps[:, GATE_ROWS, :]).then_inc(gate_copied, 1)

        @block.scalar
        def _(act):
            act.wait_ge(var_ready, 1)
            nc.scalar.activation(std[:], var[:], ACT.Sqrt).then_inc(std_ready, 1)
            act.wait_ge(scale_ready, 1)
            for wait in x_loaded or ():
                act.wait_ge(wait, 16)
            for t in range(1, NT, 2):
                nc.scalar.activation(xn[:, t, :], k.x[:, t, :], ACT.Identity, bias=shift[:, t:t + 1],
                                     scale=rstd[:, t:t + 1]).then_inc(odd_ready, 1)
            for c in range(1, NCH, 2):
                act.wait_ge(transposed, c + 1)
                nc.scalar.activation(k.xnT[:, c * CH:(c + 1) * CH], ps[:, c, :], ACT.Copy).then_inc(turned[1], 1)

        @block.tensor
        def _(pe):
            for t in range(NT):
                pe.wait_ge(odd_ready if t % 2 else even_ready, t // 2 + 1)
                ins = nc.tensor.transpose(ps[:, t // TPC, (t % TPC) * P:(t % TPC + 1) * P], xn[:, t, :], k.ident[:])
                if t % TPC == TPC - 1:
                    ins.then_inc(transposed, 1)
            if gate is not None:
                pe.wait_ge(*gate_loaded)
                for c in (0, 2, 1, 3):
                    pe.wait_ge(turned[c % 2], c // 2 + 1)
                    last = nc.tensor.matmul(ps[c * STRIP:(c + 1) * STRIP, GATE_ROWS, :], gate[:],
                                            k.xnT[:, c * CH:(c + 1) * CH], start=True, stop=True)
                last.then_inc(gate_done, 1)
                pe.wait_ge(gate_copied, 1)
                for i in range(TPC):
                    nc.tensor.transpose(ps[:, GATE, i * P:(i + 1) * P], gate_rows[:, i * P:(i + 1) * P], k.ident[:])


def by_chunk(ap):
    if len(ap.shape) == 2:
        return ap.rearrange("p (c i) -> p c i", i=TPC)
    return ap.rearrange("p (c i) e -> p c i e", i=TPC)


def gate_logits(k):
    return k.ps[:, GATE, :].rearrange("p (i c w) -> p c i w", i=TPC, c=NCH)[:, :, :, 0:E]


def moe_top1(k, tag, loads=None, x_loaded=None):
    nc, ps, d = k.nc, k.ps, k.dram
    with ExitStack() as ctx:
        def sb(name, shape, dt=F32):
            return ctx.enter_context(nc.sbuf_tensor(f"s_{name}_{tag}", shape, dt))

        def sem(name):
            return nc.alloc_semaphore(f"{name}_{tag}")

        xn = sb("t1_xn", [P, NT, M])
        mask = sb("t1_mask", [P, E, NT + 1], BF16)
        slot_iota = sb("t1_slot_iota", [P, S])

        def fill():
            nc.gpsimd.memset(mask[:, :, 0], 0.0)
            nc.gpsimd.iota(slot_iota[:], [[1, S]], base=0, channel_multiplier=0, allow_small_or_imprecise_dtypes=True)

        layernorm(k, xn, tag, k.t1_wg, (k.gate_loaded, 16), loads, x_loaded=x_loaded, fill=fill)

        w1, w2, b1, b2 = k.t1_w1, k.t1_w2, k.t1_b1, k.t1_b2
        xn_hi = sb("t1_xn_hi", [P, NT, M], F32R)
        xn_lo = sb("t1_xn_lo", [P, NT, M], F32R)
        shifted = sb("t1_shifted", [P, NT, E])
        ex = sb("t1_ex", [P, NT, E])
        score = sb("t1_score", [P, NT, E])
        stat = sb("t1_stat", [P, 12, NT])
        before = sb("t1_before", [P, E, NT + 1], BF16)
        own = sb("t1_own", [P, E, NT])
        own_base = sb("t1_own_base", [P, E, NT])
        slot_diag = sb("t1_slot_diag", [P, NT, P], F32R)
        slot_row = sb("t1_slot_row", [P, S])
        onehot = sb("t1_onehot", [P, 2, S], F32R)
        BACK = 8

        def onehot_at(n):
            return onehot[:, n % BACK // NCH, n % NCH * CH:(n % NCH + 1) * CH]

        xdT = sb("t1_dispatched", [M, S])
        hT = sb("t1_hidden", [P, 2, FT, CAP])
        eo = sb("t1_expert_rows", [P, NT, M])
        eo_hi = sb("t1_expert_hi", [P, NT, M], F32R)
        eo_lo = sb("t1_expert_lo", [P, NT, M], F32R)
        (row_max, row_sum, best_ex, r_sum, gate, best_rank, cnt_own, base_own, keep, slot, slot_kept,
         half_gate) = [stat[:, i, :] for i in range(12)]

        dve_step = sem("t1_dve_step")
        shift_ready, ex_ready, slot_ready = sem("t1_shift_ready"), sem("t1_ex_ready"), sem("t1_slot_ready")
        mask_ready, counts_ready, diag_ready = sem("t1_mask_ready"), sem("t1_counts_ready"), sem("t1_diag_ready")
        row_in_psum, row_ready = sem("t1_row_in_psum"), sem("t1_row_ready")
        hi_ready, lo_ready = sem("t1_hi_ready"), sem("t1_lo_ready")
        onehot_ready, onehot_used = sem("t1_onehot_ready"), sem("t1_onehot_used")
        gathered, xd_ready = sem("t1_gathered"), sem("t1_xd_ready")
        up_done, hidden_ready, down_done = sem("t1_up_done"), sem("t1_hidden_ready"), sem("t1_down_done")
        eo_ready, back, back_ready, tokens_back = (sem("t1_eo_ready"), sem("t1_back"), sem("t1_back_ready"),
                                                   sem("t1_tokens_back"))
        block = ctx.enter_context(nc.Block())

        @block.gpsimd
        def _(pool):
            for c in range(NCH):
                rows = slice(c * TPC, (c + 1) * TPC)
                pool.wait_ge(hi_ready, c + 1)
                nc.gpsimd.tensor_tensor(xn_lo[:, rows, :], xn[:, rows, :], xn_hi[:, rows, :].bitcast(F32),
                                        ALU.subtract).then_inc(lo_ready, 1)
            pool.wait_ge(slot_ready, 1)
            nc.gpsimd.tensor_tensor(slot_diag[:], k.ident[:].unsqueeze(1).to_broadcast([P, NT, P]),
                                    broadcast_last(slot_kept, P), ALU.mult).then_inc(diag_ready, 1)

        @block.scalar
        def _(act):
            act.wait_ge(shift_ready, 1)
            nc.scalar.activation(ex[:], shifted[:], ACT.Exp).then_inc(ex_ready, 1)
            for c in range(NCH):
                rows = slice(c * TPC, (c + 1) * TPC)
                nc.scalar.activation(xn_hi[:, rows, :], xn[:, rows, :], ACT.Copy).then_inc(hi_ready, 1)
            for c in range(NCH):
                act.wait_ge(row_in_psum, c + 1)
                nc.scalar.activation(slot_row[:, c * CH:(c + 1) * CH], ps[:, c, :], ACT.Copy).then_inc(row_ready, 1)
            for c in range(NCH):
                act.wait_ge(gathered, c + 1)
                nc.scalar.activation(xdT[:, c * CH:(c + 1) * CH], ps[:, 4 + c, :], ACT.Copy).then_inc(xd_ready, 1)
            act.wait_ge(k.t1_loaded, 64)
            for e in range(E):
                if e >= 2:
                    act.wait_ge(down_done, e - 1)
                for f in range(FT):
                    act.wait_ge(up_done, e * 2 + f // 2 + 1)
                    bank = (e % 2) * 2 + f // 2
                    nc.scalar.activation(hT[:, e % 2, f, :], ps[:, bank, (f % 2) * CAP:(f % 2 + 1) * CAP],
                                         ACT.Gelu_apprx_tanh, bias=b1[:, e, f:f + 1]).then_inc(hidden_ready, 1)
            for c in range(NCH):
                act.wait_ge(back, c + 1)
                nc.scalar.activation(xdT[:, c * CH:(c + 1) * CH], ps[:, c, :], ACT.Copy).then_inc(back_ready, 1)

        @block.vector
        def _(dve):
            done = [0]

            def link(ins):
                done[0] += 1
                ins.then_inc(dve_step, 1)
                dve.wait_ge(dve_step, done[0])

            link(nc.vector.tensor_reduce(by_chunk(row_max), gate_logits(k), X_AXIS, ALU.max))
            nc.vector.tensor_tensor(by_chunk(shifted[:]), gate_logits(k), by_chunk(broadcast_last(row_max, E)),
                                    ALU.subtract)\
                .then_inc(shift_ready, 1)
            dve.wait_ge(ex_ready, 1)
            nc.vector.tensor_reduce(row_sum, ex[:], X_AXIS, ALU.add)
            link(nc.vector.tensor_reduce(best_ex, ex[:], X_AXIS, ALU.max))
            nc.vector.reciprocal(r_sum, row_sum)
            link(nc.vector.tensor_tensor(score[:], ex[:], broadcast_last(best_ex, E), ALU.is_equal))
            nc.vector.tensor_tensor(gate, best_ex, r_sum, ALU.mult)
            link(nc.vector.tensor_tensor(score[:], score[:], k.rank[:], ALU.mult))
            link(nc.vector.tensor_reduce(best_rank, score[:], X_AXIS, ALU.max))
            nc.vector.tensor_scalar(half_gate, gate, 0.5, None, ALU.mult)
            link(nc.vector.tensor_tensor(mask[:, :, 1:NT + 1].rearrange("p e t -> p t e"), score[:],
                                         broadcast_last(best_rank, E), ALU.is_equal))
            nc.vector.tensor_tensor_scan(before[:].rearrange("p e t -> p (e t)"),
                                         k.scan_keep[:].rearrange("p e t -> p (e t)"),
                                         mask[:].rearrange("p e t -> p (e t)"), 0.0, ALU.mult, ALU.add)\
                .then_inc(mask_ready, 1)
            counts = ps[:, 1, 0:E * NT].rearrange("p (e t) -> p e t", e=E)
            nc.vector.tensor_tensor(own_base[:], k.base_slot[:], mask[:, :, 1:NT + 1], ALU.mult)
            dve.wait_ge(counts_ready, 1)
            link(nc.vector.tensor_tensor(own[:], counts, mask[:, :, 1:NT + 1], ALU.mult))
            nc.vector.tensor_reduce(base_own, own_base[:].rearrange("p e t -> p t e"), X_AXIS, ALU.add)
            link(nc.vector.tensor_reduce(cnt_own, own[:].rearrange("p e t -> p t e"), X_AXIS, ALU.add))
            nc.vector.tensor_scalar(keep, cnt_own, float(CAP), None, ALU.is_lt)
            link(nc.vector.tensor_tensor(slot, cnt_own, base_own, ALU.add))
            link(nc.vector.scalar_tensor_tensor(out=slot, in0=slot, scalar=1.0, in1=keep, op0=ALU.add, op1=ALU.mult))
            link(nc.vector.tensor_scalar(slot_kept, slot, -1.0, None, ALU.add))
            nc.vector.sem_inc(slot_ready, 1)
            for t in range(NT):
                if t >= 2:
                    dve.wait_ge(onehot_used, t - 1)
                nc.vector.tensor_scalar(onehot[:, t % 2, :], slot_iota[:], slot_kept[:, t:t + 1], None,
                                        ALU.is_equal).then_inc(onehot_ready, 1)

            def expert_out(e):
                dve.wait_ge(down_done, e + 1)
                rows = ps[:, 4 + e % 4, 0:2 * M].rearrange("p (t m) -> p t m", m=M)
                exact = eo[:, 2 * e:2 * e + 2, :]
                link(nc.vector.tensor_tensor(exact, rows, b2[:, e:e + 1, :].to_broadcast([P, 2, M]), ALU.add))
                link(nc.vector.tensor_copy(eo_hi[:, 2 * e:2 * e + 2, :], exact))
                nc.vector.tensor_tensor(eo_lo[:, 2 * e:2 * e + 2, :], exact,
                                        eo_hi[:, 2 * e:2 * e + 2, :].bitcast(F32), ALU.subtract).then_inc(eo_ready, 1)

            def onehot_back(n):
                c, j = n // NT, n % NT
                m = n - BACK
                if m >= 0 and m % NT == NT - 1:
                    dve.wait_ge(back, m // NT + 1)
                elif m >= 0:
                    dve.wait_ge(onehot_used, NT - 1 + (m + 1) - (m + 1) // NT)
                nc.vector.tensor_scalar(onehot_at(n), slot_row[:, c * CH:(c + 1) * CH], k.slot_of_row[:, j:j + 1],
                                        None, ALU.is_equal).then_inc(onehot_ready, 1)

            def update(c):
                dve.wait_ge(tokens_back, c + 1)
                for i in range(TPC):
                    t = c * TPC + i
                    last = nc.vector.scalar_tensor_tensor(
                        out=k.x[:, t, :], in0=ps[:, 4 + c, i * P:(i + 1) * P], scalar=half_gate[:, t:t + 1],
                        in1=k.x[:, t, :], op0=ALU.mult, op1=ALU.add)
                link(last)
                for t in range(c * TPC, (c + 1) * TPC):
                    nc.vector.bn_stats(k.stats[:, t, :], k.x[:, t, :])

            dve.wait_ge(row_ready, NCH)
            dve.wait_ge(gathered, NCH)
            for n in range(BACK):
                onehot_back(n)
            for e in range(E):
                expert_out(e)
            for n in range(BACK, NCH * NT):
                onehot_back(n)
                if n > NT and n % NT == NT - 2:
                    update(n // NT - 1)
            update(NCH - 1)

        @block.tensor
        def _(pe):
            pe.wait_ge(mask_ready, 1)
            counts = ps[:, 1, 0:E * NT]
            nc.tensor.matmul(counts, k.earlier[:], mask[:, :, 1:NT + 1], start=True, stop=False)
            nc.tensor.matmul(counts, k.ones_b[:], before[:, :, 0:NT], start=False, stop=True)\
                .then_inc(counts_ready, 1)
            for t in range(NT):
                pe.wait_ge(lo_ready, t // TPC + 1)
                pe.wait_ge(onehot_ready, t + 1)
                for part, rows in enumerate((xn_hi, xn_lo)):
                    for c in range(NCH):
                        last = nc.tensor.matmul(ps[:, 4 + c, :], rows[:, t, :], onehot[:, t % 2, c * CH:(c + 1) * CH],
                                                start=(t == 0 and part == 0), stop=(t == NT - 1 and part == 1))
                        if t == NT - 1 and part == 1:
                            last.then_inc(gathered, 1)
                if t < NT - 1:
                    last.then_inc(onehot_used, 1)
                if t == 6:
                    pe.wait_ge(diag_ready, 1)
                    for c in range(NCH):
                        nc.tensor.matmul(ps[:, c, :], k.ones_r[:], slot_diag[:, c * TPC:(c + 1) * TPC, :],
                                         start=True, stop=True).then_inc(row_in_psum, 1)
            pe.wait_ge(k.t1_loaded, 64)
            pe.wait_ge(row_ready, NCH)

            def up(e):
                if e % 2 == 0:
                    pe.wait_ge(xd_ready, e // 2 + 1)
                if e >= 2:
                    pe.wait_ge(hidden_ready, (e - 1) * FT)
                for f in range(FT):
                    bank = (e % 2) * 2 + f // 2
                    last = nc.tensor.matmul(ps[:, bank, (f % 2) * CAP:(f % 2 + 1) * CAP],
                                            w1[:, e, f * P:(f + 1) * P], xdT[:, e * CAP:(e + 1) * CAP],
                                            start=True, stop=True)
                    if f % 2:
                        last.then_inc(up_done, 1)

            def down(e):
                pe.wait_ge(hidden_ready, (e + 1) * FT)
                if e < 4:
                    pe.wait_ge(xd_ready, NCH)
                else:
                    pe.wait_ge(eo_ready, e - 3)
                for half in range(2):
                    out = ps[:, 4 + e % 4, half * M:(half + 1) * M]
                    for f in range(FT):
                        last = nc.tensor.matmul(out, hT[:, e % 2, f, half * P:(half + 1) * P], w2[:, e, f, :],
                                                start=(f == 0), stop=(f == FT - 1))
                last.then_inc(down_done, 1)

            up(0)
            for e in range(E):
                if e + 1 < E:
                    up(e + 1)
                down(e)
            pe.wait_ge(hidden_ready, E * FT)

            def turn(c):
                pe.wait_ge(back_ready, c + 1)
                for t in range(c * TPC, (c + 1) * TPC):
                    last = nc.tensor.transpose(ps[:, 4 + c, (t % TPC) * P:(t % TPC + 1) * P],
                                               xdT[:, t * P:(t + 1) * P], k.ident[:])
                last.then_inc(tokens_back, 1)

            pe.wait_ge(eo_ready, E)
            for n in range(NCH * NT):
                c, j = n // NT, n % NT
                pe.wait_ge(onehot_ready, NT + n + 1)
                for part, rows in enumerate((eo_hi, eo_lo)):
                    last = nc.tensor.matmul(ps[:, c, :], rows[:, j, :], onehot_at(n),
                                            start=(j == 0 and part == 0), stop=(j == NT - 1 and part == 1))
                if j < NT - 1:
                    last.then_inc(onehot_used, 1)
                else:
                    last.then_inc(back, 1)
                if c > 0 and j == 3:
                    turn(c - 1)
            turn(NCH - 1)


def moe_top2(k, tag, loads=None, has_stats=False, store=False):
    nc, ps, d = k.nc, k.ps, k.dram
    with ExitStack() as ctx:
        def sb(name, shape, dt=F32):
            return ctx.enter_context(nc.sbuf_tensor(f"s_{name}_{tag}", shape, dt))

        def sem(name):
            return nc.alloc_semaphore(f"{name}_{tag}")

        xn = sb("t2_xn", [P, NT, M])
        layernorm(k, xn, tag, k.t2_router, (k.t2_loaded, 48), loads, has_stats)

        w1, w2 = k.t2_w1, k.t2_w2
        shifted = sb("t2_shifted", [P, NT, E])
        ex = sb("t2_ex", [P, NT, E])
        rest = sb("t2_rest", [P, NT, E])
        score = sb("t2_score", [P, NT, E])
        first = sb("t2_first", [P, NT, E])
        second = sb("t2_second", [P, NT, E])
        weight = sb("t2_weight", [P, NT, E])
        stat = sb("t2_stat", [P, 8, NT])
        AHEAD, HIDDEN = E, E + 2
        hidden = sb("t2_hidden", [P, HIDDEN, CH])
        row_max, row_sum, best_ex, r_sum, best_rank, next_ex, next_rank, half = [stat[:, i, :] for i in range(8)]

        dve_step = sem("t2_dve_step")
        shift_ready, ex_ready = sem("t2_shift_ready"), sem("t2_ex_ready")
        stored = sem("t2_stored")
        up_done, hidden_ready, down_done, added = (sem("t2_up_done"), sem("t2_hidden_ready"), sem("t2_down_done"),
                                                   sem("t2_added"))
        block = ctx.enter_context(nc.Block())
        steps = [(c, e) for c in range(NCH) for e in range(E)]

        if store:
            @block.sync
            def _(sp):
                for c in range(NCH):
                    sp.wait_ge(added, (c + 1) * E)
                    sp.dma_start(k.dram["out"].rearrange("b (t p) m -> p (b t) m", p=P)[:, c * TPC:(c + 1) * TPC, :],
                                 k.x[:, c * TPC:(c + 1) * TPC, :]).then_inc(stored, 16)
                sp.wait_ge(stored, NCH * 16)

        @block.scalar
        def _(act):
            act.wait_ge(shift_ready, 1)
            nc.scalar.activation(ex[:], shifted[:], ACT.Exp).then_inc(ex_ready, 1)
            for n in range(len(steps)):
                act.wait_ge(up_done, n + 1)
                if n >= HIDDEN:
                    act.wait_ge(down_done, n - HIDDEN + 1)
                nc.scalar.activation(hidden[:, n % HIDDEN, :], ps[:, n % 4, :], ACT.Relu).then_inc(hidden_ready, 1)

        @block.vector
        def _(dve):
            done = [0]

            def link(ins):
                done[0] += 1
                ins.then_inc(dve_step, 1)
                dve.wait_ge(dve_step, done[0])

            link(nc.vector.tensor_reduce(by_chunk(row_max), gate_logits(k), X_AXIS, ALU.max))
            nc.vector.tensor_tensor(by_chunk(shifted[:]), gate_logits(k), by_chunk(broadcast_last(row_max, E)),
                                    ALU.subtract)\
                .then_inc(shift_ready, 1)
            dve.wait_ge(ex_ready, 1)
            nc.vector.tensor_reduce(row_sum, ex[:], X_AXIS, ALU.add)
            link(nc.vector.tensor_reduce(best_ex, ex[:], X_AXIS, ALU.max))
            nc.vector.reciprocal(r_sum, row_sum)
            link(nc.vector.tensor_tensor(score[:], ex[:], broadcast_last(best_ex, E), ALU.is_equal))
            link(nc.vector.tensor_tensor(score[:], score[:], k.rank[:], ALU.mult))
            link(nc.vector.tensor_reduce(best_rank, score[:], X_AXIS, ALU.max))
            link(nc.vector.tensor_tensor(first[:], score[:], broadcast_last(best_rank, E), ALU.is_equal))
            link(nc.vector.tensor_tensor(rest[:], ex[:], first[:], ALU.mult))
            link(nc.vector.tensor_tensor(rest[:], ex[:], rest[:], ALU.subtract))
            link(nc.vector.tensor_tensor(rest[:], rest[:], first[:], ALU.subtract))
            link(nc.vector.tensor_reduce(next_ex, rest[:], X_AXIS, ALU.max))
            link(nc.vector.tensor_tensor(score[:], rest[:], broadcast_last(next_ex, E), ALU.is_equal))
            link(nc.vector.tensor_tensor(score[:], score[:], k.rank[:], ALU.mult))
            link(nc.vector.tensor_reduce(next_rank, score[:], X_AXIS, ALU.max))
            nc.vector.tensor_scalar(half, r_sum, 0.5, None, ALU.mult)
            link(nc.vector.tensor_tensor(second[:], score[:], broadcast_last(next_rank, E), ALU.is_equal))
            link(nc.vector.tensor_tensor(first[:], first[:], second[:], ALU.add))
            link(nc.vector.tensor_tensor(weight[:], first[:], ex[:], ALU.mult))
            link(nc.vector.tensor_tensor(weight[:], weight[:], broadcast_last(half, E), ALU.mult))
            for n, (c, e) in enumerate(steps):
                dve.wait_ge(down_done, n + 1)
                if n >= 1:
                    dve.wait_ge(added, n)
                for i in range(TPC):
                    t = c * TPC + i
                    last = nc.vector.scalar_tensor_tensor(
                        out=k.x[:, t, :], in0=ps[:, 4 + n % 3, i * P:(i + 1) * P], scalar=weight[:, t, e:e + 1],
                        in1=k.x[:, t, :], op0=ALU.mult, op1=ALU.add)
                last.then_inc(added, 1)
                if e == E - 1 and not store:
                    dve.wait_ge(added, n + 1)
                    for t in range(c * TPC, (c + 1) * TPC):
                        nc.vector.bn_stats(k.stats[:, t, :], k.x[:, t, :])

        @block.tensor
        def _(pe):
            pe.wait_ge(k.t2_loaded, 48)

            def up(n):
                c, e = steps[n]
                if n >= 4:
                    pe.wait_ge(hidden_ready, n - 3)
                nc.tensor.matmul(ps[:, n % 4, :], w1[:, e, :], k.xnT[:, c * CH:(c + 1) * CH],
                                 start=True, stop=True).then_inc(up_done, 1)

            def down(n):
                c, e = steps[n]
                pe.wait_ge(hidden_ready, n + 1)
                if n >= 3:
                    pe.wait_ge(added, n - 2)
                for i in range(TPC):
                    last = nc.tensor.matmul(ps[:, 4 + n % 3, i * P:(i + 1) * P], hidden[:, n % HIDDEN, i * P:(i + 1) * P],
                                            w2[:, e, :], start=True, stop=True)
                last.then_inc(down_done, 1)

            for n in range(AHEAD):
                up(n)
            for n in range(len(steps)):
                if n + AHEAD < len(steps):
                    up(n + AHEAD)
                down(n)




def attention_small(k):
    nc, ps, d = k.nc, k.ps, k.dram
    H, D, G = 16, 8, 4
    NG = H // G
    PARTS = 3
    ROWS = PARTS * PARTS * D
    SCALE = float(M) ** -0.5
    W = P // G
    JT = NT * G // 2
    NI = NG * NCH
    RING, PROBS = 3, 4
    TURNS = 2
    ACC, EPI = 6, 7
    q_dram = nc.dram_tensor("a0_q_parts", (H, PARTS, D, S), BF16, kind="Internal").ap()
    k_dram = nc.dram_tensor("a0_k_parts", (H, PARTS, D, S), BF16, kind="Internal").ap()

    with ExitStack() as ctx:
        def sb(name, shape, dt=F32):
            return ctx.enter_context(nc.sbuf_tensor(f"s_a0_{name}", shape, dt))

        def sem(name):
            return nc.alloc_semaphore(f"a0_{name}")

        safe = sb("safe", [P, 1], I32)
        values = sb("values", [P, NT, M])
        v_strip = sb("v_strip", [P, 2, NT, G, W])
        wo = sb("wo_strips", [P, NG, M])
        sum_row = sb("sum_row", [P, P])
        k_rows = sb("k_rows", [ROWS, 2, G, S], BF16)
        q_rows = sb("q_rows", [ROWS, 2, G, S], BF16)
        loaded = sem("loaded")
        LOADS = PARTS * PARTS + PARTS

        def load_k(sp, g):
            for b in range(PARTS):
                for a in range(PARTS):
                    r = (b * PARTS + a) * D
                    sp.dma_start(k_rows[r:r + D, g % 2, :, :],
                                 k_dram[g * G:(g + 1) * G, b].rearrange("h d t -> d h t")).then_inc(loaded, 16)

        def load_q(sp, g):
            for b in range(PARTS):
                r = b * PARTS * D
                sp.dma_start(q_rows[r:r + PARTS * D, g % 2, :, :],
                             q_dram[g * G:(g + 1) * G].rearrange("h a d t -> (a d) h t")).then_inc(loaded, 16)

        with ExitStack() as prep:
            def psb(name, shape, dt=F32):
                return prep.enter_context(nc.sbuf_tensor(f"s_a0_{name}", shape, dt))

            def psem(name):
                return sem(name)

            with ExitStack() as norm_only:
                layernorm(k, norm_only.enter_context(nc.sbuf_tensor("s_a0_xn", [P, NT, M], F32)), "a0",
                          has_stats=True)
            sides = (k.a0_wk, k.a0_wq)
            bo = k.a0_bo
            rest = psb("rest", [P, 2, S])
            part = psb("part", [P, 2, PARTS, S], BF16)
            square = psb("square", [P, 4, CH], BF16)
            head_rows = psb("head_rows", [P, P // NCH], BF16)
            norm = psb("norm", [P, 4])
            wo_zero, wo_loaded, filled = sem("wo_zero"), sem("wo_loaded"), sem("filled")
            projected, squared, v_projected, normed = (sem("projected"), sem("squared"), sem("v_projected"),
                                                       sem("normed"))
            part_ready = [sem("part0_ready"), sem("part1_ready"), sem("part2_ready")]
            rest_ready, stored, most_ready, reduced, product = (sem("rest_ready"), sem("stored"), sem("most_ready"),
                                                                sem("reduced"), sem("product"))
            STEPS = 2 * NCH
            block = prep.enter_context(nc.Block())

            def columns(n):
                return n // NCH, slice((n % NCH) * CH, (n % NCH + 1) * CH)

            @block.sync
            def _(sp):
                sp.wait_ge(wo_zero, 1)
                for h in range(G):
                    sp.dma_start(wo[W * h:W * h + D, :, :],
                                 d["a0_wo"].rearrange("(g h d) n -> h d g n", g=NG, h=G)[h]).then_inc(wo_loaded, 16)
                for side, dram in enumerate((k_dram, q_dram)):
                    for i in range(PARTS):
                        sp.wait_ge(part_ready[i], (side + 1) * NCH)
                        sp.dma_start(dram[:, i, :, :], part[:, side, i, :]).then_inc(stored, 16)
                sp.wait_ge(stored, 2 * PARTS * 16)
                load_q(sp, 0)
                load_k(sp, 0)
                sp.wait_ge(wo_loaded, G * 16)

            @block.gpsimd
            def _(pool):
                nc.gpsimd.memset(wo[:], 0.0).then_inc(wo_zero, 1)
                nc.gpsimd.memset(head_rows[:], 1.0).then_inc(filled, 1)
                nc.gpsimd.memset(sum_row[:], 0.0).then_inc(filled, 1)
                nc.gpsimd.memset(v_strip[:], 0.0).then_inc(filled, 1)
                pool.wait_ge(filled, 3)
                nc.gpsimd.affine_select(out=head_rows[:], in_=head_rows[:], compare_op=ALU.is_ge, fill=0.0,
                                        base=0, pattern=[[-D, P // NCH]], channel_multiplier=1).then_inc(filled, 1)
                pool.wait_ge(filled, 4)
                nc.gpsimd.affine_select(out=head_rows[:], in_=head_rows[:], compare_op=ALU.is_ge, fill=0.0,
                                        base=D - 1, pattern=[[D, P // NCH]], channel_multiplier=-1)\
                    .then_inc(filled, 1)
                nc.gpsimd.affine_select(out=sum_row[:], in_=sum_row[:], compare_op=ALU.not_equal, fill=1.0,
                                        base=-D, pattern=[[-W, G], [0, W]], channel_multiplier=1)
                nc.gpsimd.memset(v_strip[:, :, :, :, D], 1.0)
                pool.wait_ge(k.a0_loaded, 48)
                nc.gpsimd.tensor_tensor(k.x[:], k.x[:], bo[:].unsqueeze(1).to_broadcast([P, NT, M]), ALU.add)
                pool.wait_ge(most_ready, 1)
                nc.gpsimd.partition_all_reduce(norm[:, 2:4], norm[:, 0:2], P, RMAX).then_inc(reduced, 1)

            @block.scalar
            def _(act):
                def second_part(n):
                    side, cols = columns(n)
                    act.wait_ge(rest_ready, n + 1)
                    nc.scalar.activation(part[:, side, 1, cols], rest[:, side, cols], ACT.Copy)\
                        .then_inc(part_ready[1], 1)

                for n in range(STEPS):
                    side, cols = columns(n)
                    act.wait_ge(projected, n + 1)
                    nc.scalar.activation(part[:, side, 0, cols], ps[:, n, :], ACT.Copy).then_inc(part_ready[0], 1)
                    if n >= 4:
                        act.wait_ge(normed, n - 3)
                    nc.scalar.activation(square[:, n % 4, :], ps[:, n, :], ACT.Square).then_inc(squared, 1)
                    if n >= 1:
                        second_part(n - 1)
                second_part(STEPS - 1)
                for c in range(NCH):
                    act.wait_ge(v_projected, c + 1)
                    nc.scalar.activation(values[:, c * TPC:(c + 1) * TPC, :], ps[:, 2 + c, :], ACT.Copy)

            @block.vector
            def _(dve):
                def third_part(n):
                    side, cols = columns(n)
                    dve.wait_ge(part_ready[1], n + 1)
                    nc.vector.tensor_tensor(part[:, side, 2, cols], rest[:, side, cols], part[:, side, 1, cols],
                                            ALU.subtract).then_inc(part_ready[2], 1)

                for n in range(STEPS):
                    side, cols = columns(n)
                    dve.wait_ge(squared, n + 1)
                    nc.vector.tensor_tensor(rest[:, side, cols], ps[:, n, :], part[:, side, 0, cols],
                                            ALU.subtract).then_inc(rest_ready, 1)
                    if n >= 2:
                        third_part(n - 2)
                third_part(STEPS - 2)
                third_part(STEPS - 1)
                dve.wait_ge(normed, STEPS)
                for side in range(2):
                    last = nc.vector.tensor_reduce(norm[:, side:side + 1], ps[:, side, :], X_AXIS, ALU.max)
                last.then_inc(most_ready, 1)
                dve.wait_ge(reduced, 1)
                nc.vector.tensor_tensor(norm[:, 0:1], norm[:, 2:3], norm[:, 3:4], ALU.mult).then_inc(product, 1)
                dve.wait_ge(product, 1)
                nc.vector.tensor_scalar(safe[:], norm[:, 0:1], 1.0625 * SCALE * SCALE, SAFE_ARGUMENT ** 2,
                                        ALU.mult, ALU.is_le)

            @block.tensor
            def _(pe):
                def head_norms(n):
                    rows = P // NCH
                    c = n % NCH
                    pe.wait_ge(squared, n + 1)
                    nc.tensor.matmul(ps[rows * c:rows * (c + 1), n // NCH, :], head_rows[:], square[:, n % 4, :],
                                     start=True, stop=True).then_inc(normed, 1)

                def project(n):
                    side, cols = columns(n)
                    nc.tensor.matmul(ps[:, n, :], sides[side][:], k.xnT[:, cols], start=True, stop=True)\
                        .then_inc(projected, 1)

                pe.wait_ge(k.a0_loaded, 48)
                for n in range(STEPS):
                    project(n)
                    if n == 4:
                        pe.wait_ge(filled, 5)
                        pe.wait_ge(rest_ready, 2)
                    if n >= 4:
                        head_norms(n - 4)
                for n in range(STEPS - 4, STEPS):
                    head_norms(n)
                for t in range(NT):
                    if t % TPC == 0:
                        pe.wait_ge(rest_ready, 2 + t // TPC + 1)
                    last = nc.tensor.matmul(ps[:, 2 + t // TPC, (t % TPC) * P:(t % TPC + 1) * P],
                                            k.xnT[:, t * P:(t + 1) * P], k.a0_wk[:], start=True, stop=True)
                    if t % TPC == TPC - 1:
                        last.then_inc(v_projected, 1)

        probs = sb("probs", [P, PROBS, 2, CH])
        weighted = sb("weighted", [P, CH])
        inverse = sb("inverse", [P, CH])
        attended = sb("attended", [P, CH])
        running_max = sb("running_max", [P, CH])
        minus_max = sb("minus_max", [P, TPC])
        shift = sb("shift", [P, G, TPC, P])

        v_ready, score_done, exp_done, pv_done = sem("v_ready"), sem("score_done"), sem("exp_done"), sem("pv_done")
        acc_copied, sums_done, inverse_ready, attended_ready, out_done, x_added = (
            sem("acc_copied"), sem("sums_done"), sem("inverse_ready"), sem("attended_ready"), sem("out_done"),
            sem("x_added"))
        max_score, max_taken, max_turned, max_read, shift_ready = (
            sem("max_score"), sem("max_taken"), sem("max_turned"), sem("max_read"), sem("shift_ready"))
        block = ctx.enter_context(nc.Block())

        @block.sync
        def _(sp):
            for g in range(1, NG):
                sp.wait_ge(loaded, g * (LOADS * 16))
                if g >= 2:
                    sp.wait_ge(pv_done, NCH * (g - 1) * JT + PROBS)
                load_k(sp, g)
                load_q(sp, g)

        @block.scalar
        def _(act):
            act.sem_inc(exp_done, RING)
            with act.Fori(0, NG) as g:
                for n in range(NCH * JT):
                    act.wait_ge(score_done, g * (NCH * JT) + (n + 1))
                    act.wait_ge(pv_done, g * (NCH * JT) + (n + 1))
                    bank = 2 * (n % JT % RING)
                    nc.scalar.activation(probs[:, n % PROBS, :, :], ps[:, bank:bank + 2, :],
                                         ACT.Exp, scale=SCALE).then_inc(exp_done, 1)

        def dve_program(dve, guarded):
            def strip_values(g, slot):
                nc.vector.tensor_copy(v_strip[:, slot, :, :, 0:D],
                                      values[:, :, bass.ds(g * (G * D), G * D)].rearrange("p t (h d) -> p t h d", d=D))\
                    .then_inc(v_ready, 1)

            def row_maxima(it):
                for n in range(G * NT):
                    h, kt = n // NT, n % NT
                    dve.wait_ge(max_score, it * (G * NT) + (n + 1))
                    if kt == 0:
                        ins = nc.vector.tensor_copy(running_max[:], ps[:, n % 2, :])
                    else:
                        ins = nc.vector.tensor_tensor(running_max[:], ps[:, n % 2, :], running_max[:], ALU.max)
                    ins.then_inc(max_taken, 1)
                    dve.wait_ge(max_taken, it * (G * NT) + (n + 1 + TURNS))
                    if kt == NT - 1:
                        dve.wait_ge(max_turned, it * G + (h + 1))
                        nc.vector.tensor_reduce(minus_max[:], ps[:, 2, :].rearrange("p (i k) -> p i k", i=TPC),
                                                X_AXIS, ALU.max, negate=True).then_inc(max_read, 1)
                        dve.wait_ge(max_read, it * G + (h + 2))
                        for i in range(TPC):
                            ins = nc.vector.tensor_scalar(shift[:, h, i, :], k.ident[:], minus_max[:, i:i + 1], None,
                                                          ALU.mult)
                        ins.then_inc(shift_ready, 1)

            def epilogue(it, qc):
                dve.wait_ge(pv_done, (it + 1) * JT + PROBS)
                nc.vector.tensor_copy(weighted[:], ps[:, ACC, :]).then_inc(acc_copied, 1)
                dve.wait_ge(sums_done, it + 1)
                nc.vector.reciprocal(inverse[:], ps[:, EPI, :]).then_inc(inverse_ready, 1)
                dve.wait_ge(inverse_ready, it + 1)
                nc.vector.tensor_tensor(attended[:], weighted[:], inverse[:], ALU.mult).then_inc(attended_ready, 1)
                dve.wait_ge(out_done, it + 1)
                rows = k.x[:, bass.ds(qc * TPC, TPC), :]
                nc.vector.tensor_tensor(rows, rows, ps[:, EPI, :].rearrange("p (i m) -> p i m", m=M), ALU.add)\
                    .then_inc(x_added, 1)

            strip_values(0, 0)
            with dve.Fori(0, NG // 2) as gg:
                for par in range(2):
                    g = gg * 2 + par
                    strip_values((g + 1) % NG, 1 - par)
                    with dve.Fori(0, NCH) as qc:
                        if guarded:
                            row_maxima(g * NCH + qc)
                        epilogue(g * NCH + qc, qc)

        @block.vector
        def _(dve):
            dve.sem_inc(max_taken, TURNS)
            is_safe = dve.value_load(safe[0:1, 0:1], min_val=0, max_val=1)
            with dve.If(is_safe == 1):
                dve_program(dve, guarded=False)
            with dve.Else():
                dve_program(dve, guarded=True)

        def pe_program(pe, guarded):
            def score(out, slot, h, kt, q0, last):
                k_flat = k_rows[:].rearrange("r b h t -> r (b h t)")
                q_flat = q_rows[:].rearrange("r b h t -> r (b h t)")
                return nc.tensor.matmul(out, k_flat[:, bass.ds(slot * (G * S) + (h * S + kt * P), P)],
                                        q_flat[:, bass.ds(slot * (G * S) + (h * S + q0), CH)], start=True, stop=last)

            def scores(it, par, qc, j):
                kt, pair = j // 2, j % 2
                before = j - RING if j >= RING else max(t for t in range(JT) if t % RING == j) - JT
                pe.wait_ge(exp_done, it * JT + (before + 1 + RING))
                for hh in range(2):
                    bank = 2 * (j % RING) + hh
                    ins = score(ps[:, bank, :], par, 2 * pair + hh, kt, qc * CH, not guarded)
                    if guarded:
                        ins = nc.tensor.matmul(ps[:, bank, :], k.ones[:], shift[:, 2 * pair + hh, :, :],
                                               start=False, stop=True)
                ins.then_inc(score_done, 1)

            def weigh(it, par, j):
                kt, pair = j // 2, j % 2
                pe.wait_ge(exp_done, it * JT + (j + 1 + RING))
                if j == 0:
                    pe.wait_ge(acc_copied, it + 1)
                for hh in range(2):
                    h = 2 * pair + hh
                    last = nc.tensor.matmul(ps[W * h:W * (h + 1), ACC, :], v_strip[:, par, kt, h, :],
                                            probs[:, j % PROBS, hh, :], start=(kt == 0), stop=(kt == NT - 1))
                last.then_inc(pv_done, 1)

            def sums(n):
                pe.wait_ge(acc_copied, n + 1)
                pe.wait_ge(x_added, n)
                nc.tensor.matmul(ps[:, EPI, :], sum_row[:], weighted[:], start=True, stop=True).then_inc(sums_done, 1)

            def project(n, g):
                pe.wait_ge(attended_ready, n)
                for i in range(TPC):
                    last = nc.tensor.matmul(ps[:, EPI, i * P:(i + 1) * P], attended[:, i * P:(i + 1) * P],
                                            wo[:, :, :].rearrange("p g m -> p (g m)")[:, bass.ds(g * M, M)],
                                            start=True, stop=True)
                last.then_inc(out_done, 1)

            def row_maxima(it, par, qc):
                pe.wait_ge(exp_done, it * JT + RING)
                for n in range(G * NT):
                    h, kt = n // NT, n % NT
                    pe.wait_ge(max_taken, it * (G * NT) + (n + 1))
                    score(ps[:, n % 2, :], par, h, kt, qc * CH, True).then_inc(max_score, 1)
                    if kt == NT - 1:
                        pe.wait_ge(max_taken, it * (G * NT) + (n + 1 + TURNS))
                        pe.wait_ge(max_read, it * G + (h + 1))
                        for i in range(TPC):
                            last = nc.tensor.transpose(ps[:, 2, i * P:(i + 1) * P], running_max[:, i * P:(i + 1) * P],
                                                       k.ident[:])
                        last.then_inc(max_turned, 1)
                pe.wait_ge(shift_ready, it * G + G)

            if not guarded:
                pe.wait_ge(loaded, LOADS * 16)
                for j in range(RING):
                    scores(0, 0, 0, j)
            with pe.Fori(0, NG // 2) as gg:
                for par in range(2):
                    g = gg * 2 + par
                    with pe.Fori(0, NCH) as qc:
                        pe.wait_ge(v_ready, g + 1)
                        it = g * NCH + qc
                        if guarded:
                            pe.wait_ge(loaded, (g + 1) * (LOADS * 16))
                            row_maxima(it, par, qc)
                            for j in range(RING):
                                scores(it, par, qc, j)
                        for j in range(JT):
                            if j + RING < JT:
                                scores(it, par, qc, j + RING)
                            weigh(it, par, j)
                            if not guarded and j + RING >= JT:
                                group = (it + 1) // NCH % NG
                                if j + RING == JT:
                                    pe.wait_ge(loaded, (group + 1) * (LOADS * 16))
                                scores(it + 1, group % 2, (qc + 1) % NCH, j + RING - JT)
                            if not guarded and j == 4:
                                with pe.If(it > 0):
                                    sums(it)
                            if not guarded and j == 10:
                                with pe.If(it > 0):
                                    project(it, (it + NI - 1) // NCH % NG)
                        if guarded:
                            sums(it + 1)
                            project(it + 1, g)
            if not guarded:
                sums(NI)
                project(NI, NG - 1)

        @block.tensor
        def _(pe):
            pe.sem_inc(pv_done, PROBS)
            pe.sem_inc(x_added, 1)
            pe.sem_inc(acc_copied, 1)
            pe.sem_inc(max_read, 1)
            is_safe = pe.value_load(safe[0:1, 0:1], min_val=0, max_val=1)
            with pe.If(is_safe == 1):
                pe_program(pe, guarded=False)
            with pe.Else():
                pe_program(pe, guarded=True)


def attention_wide(k):
    nc, ps, d = k.nc, k.ps, k.dram
    H, D = 16, 64
    NP = H // 2
    SCALE = float(D) ** -0.5
    NI = NP * NCH
    RING, PROBS = 2, 8
    ACC, EPI, QV, KB = 4, 5, 6, 7
    ADDS = NT - 2

    with ExitStack() as ctx:
        def sb(name, shape, dt=F32):
            return ctx.enter_context(nc.sbuf_tensor(f"s_a1_{name}", shape, dt))

        def sem(name):
            return nc.alloc_semaphore(f"a1_{name}")

        safe = sb("safe", [P, 1], I32)
        w_all, wp = k.a1_w, k.a1_wp

        k_rows = sb("k_rows", [P, 2, 2, S], F32R)
        q_rows = sb("q_rows", [P, 2, 2, 2, CH], F32R)
        values = sb("values", [P, 2, NT, P])

        def hi_halves(rows, source, order):
            out = []
            for s in range(2):
                half = s ^ order
                out.append((rows(s, order)[D * half:D * (half + 1)], source[D * s:D * (s + 1)]))
            return out

        def lo_halves(rows, source, order):
            out = []
            for s in range(2):
                half = s ^ order
                out.append((rows(s, order)[D * (1 - half):D * (2 - half)], source[D * s:D * (s + 1)],
                            rows(s, 0)[D * s:D * (s + 1)]))
            return out

        def q_at(slot):
            flat = q_rows[:].rearrange("p i s o c -> p (i s o c)")
            return lambda s, order: flat[:, bass.ds(slot * (4 * CH) + (2 * s + order) * CH, CH)]

        def k_at(par, c0):
            return lambda s, order: k_rows[:, par, s, bass.ds(c0, CH)]

        with ExitStack() as prep:
            def psb(name, shape, dt=F32):
                return prep.enter_context(nc.sbuf_tensor(f"s_a1_{name}", shape, dt))

            xn = psb("xn", [P, NT, M])
            layernorm(k, xn, "a1", has_stats=True)
            w_b = psb("w_b", [M, 2, H, D], BF16)
            gram = psb("gram", [P, 2, 2 * NP, D], BF16)
            fourth = psb("fourth", [P, 2 * NP, D])
            halves_one = psb("halves_one", [P, P])
            norm = psb("norm", [P, 4 * NP])
            bound = psb("bound", [P, 2])
            filled, w_cut, power_done, power_left = sem("filled"), sem("w_cut"), sem("power_done"), sem("power_left")
            summed_rows, summed_all, dve_step = sem("summed_rows"), sem("summed_all"), sem("dve_step")
            most_ready, reduced = sem("most_ready"), sem("reduced")
            piece_done, hi_done, lo_done, v_done = sem("first_piece"), sem("first_hi"), sem("first_lo"), sem("first_v")
            KQ = NCH + 1
            PIECES = KQ + NCH
            POWERS = 3
            limit = (SAFE_ARGUMENT ** 2 / (1.12 * SCALE ** 2 * M ** 2)) ** 8

            def piece_bank(i):
                return (6, 7, 6, 7, 2, 3, 4, 5, 1)[i]

            def power_banks(n):
                return ps[:, 2 * n:2 * n + 2, :]

            def piece_halves(fn, i):
                if i < NCH:
                    return fn(k_at(0, i * CH), ps[:, piece_bank(i), :], 0)
                return fn(q_at(0), ps[:, piece_bank(i), :], 0) + fn(q_at(0), ps[:, piece_bank(i), :], 1)

            block = prep.enter_context(nc.Block())

            @block.gpsimd
            def _(pool):
                nc.gpsimd.memset(halves_one[:], 0.0).then_inc(filled, 1)
                pool.wait_ge(filled, 1)
                for s in range(2):
                    nc.gpsimd.memset(halves_one[D * s:D * (s + 1), D * s:D * (s + 1)], 1.0).then_inc(filled, 1)
                pool.wait_ge(filled, 3)
                pool.wait_ge(k.a1_loaded, 96)
                nc.gpsimd.tensor_tensor(k.x[:], k.x[:], k.a1_bp[:].unsqueeze(1).to_broadcast([P, NT, M]), ALU.add)
                pool.wait_ge(most_ready, 1)
                nc.gpsimd.partition_all_reduce(bound[:, 1:2], bound[:, 0:1], P, RMAX).then_inc(reduced, 1)

            @block.scalar
            def _(act):
                def piece(i):
                    act.wait_ge(piece_done, i + 1)
                    if i < KQ:
                        for dst, src in piece_halves(hi_halves, i):
                            last = nc.scalar.activation(dst, src, ACT.Copy)
                        last.then_inc(hi_done, 1)
                    else:
                        c = i - KQ
                        nc.scalar.activation(values[:, 0, c * TPC:(c + 1) * TPC, :], ps[:, piece_bank(i), :],
                                             ACT.Copy).then_inc(v_done, 1)

                for n in range(POWERS):
                    piece(n)
                    act.wait_ge(power_done, n + 1)
                    if n < POWERS - 1:
                        nc.scalar.activation(gram[:, n, :, :].rearrange("r g e -> r (g e)"), power_banks(n), ACT.Copy)\
                            .then_inc(power_left, 1)
                    else:
                        nc.scalar.activation(fourth[:].rearrange("r g e -> r (g e)"), power_banks(n), ACT.Square)\
                            .then_inc(power_left, 1)
                for i in range(POWERS, PIECES):
                    piece(i)

            @block.vector
            def _(dve):
                done = [0]

                def link(ins):
                    done[0] += 1
                    ins.then_inc(dve_step, 1)
                    dve.wait_ge(dve_step, done[0])

                def piece(i):
                    dve.wait_ge(hi_done, i + 1)
                    for dst, src, hi in piece_halves(lo_halves, i):
                        last = nc.vector.tensor_tensor(dst, src, hi.bitcast(F32), ALU.subtract)
                    last.then_inc(lo_done, 1)

                dve.wait_ge(k.a1_loaded, 96)
                nc.vector.tensor_copy(w_b[:], w_all[:, 0:2, :, :]).then_inc(w_cut, 1)
                for i in range(POWERS):
                    piece(i)
                dve.wait_ge(power_left, POWERS)
                nc.vector.tensor_reduce(norm[:, 0:2 * NP], fourth[:], X_AXIS, ALU.add).then_inc(summed_rows, 1)
                piece(POWERS)
                dve.wait_ge(summed_all, 1)
                link(nc.vector.tensor_copy(norm[:, 2 * NP:4 * NP], ps[:, 0, 0:2 * NP]))
                link(nc.vector.tensor_tensor(norm[:, 0:NP], norm[:, 2 * NP:3 * NP], norm[:, 3 * NP:4 * NP], ALU.mult))
                nc.vector.tensor_reduce(bound[:, 0:1], norm[:, 0:NP], X_AXIS, ALU.max).then_inc(most_ready, 1)
                dve.wait_ge(reduced, 1)
                nc.vector.tensor_scalar(safe[:], bound[:, 1:2], limit, None, ALU.is_le)
                for i in range(POWERS + 1, KQ):
                    piece(i)

            @block.tensor
            def _(pe):
                def power(n):
                    for side in range(2):
                        for h in range(H):
                            p, s = h // 2, h % 2
                            g = side * NP + p
                            half = slice(D * s, D * (s + 1))
                            if n == 0:
                                left = right = w_b[:, side, h, :]
                            else:
                                left = right = gram[half, n - 1, g, :]
                            last = nc.tensor.matmul(ps[half, 2 * n + side, p * D:(p + 1) * D], left, right,
                                                    start=True, stop=True)
                    last.then_inc(power_done, 1)

                def piece(i):
                    bank = piece_bank(i)
                    if 2 <= i < NCH:
                        pe.wait_ge(lo_done, i - 1)
                    if i < NCH:
                        last = nc.tensor.matmul(ps[:, bank, :], w_all[:, 1, 0:2, :], k.xnT[:, i * CH:(i + 1) * CH],
                                                start=True, stop=True)
                    elif i < KQ:
                        last = nc.tensor.matmul(ps[:, bank, :], w_all[:, 0, 0:2, :], k.xnT[:, 0:CH],
                                                start=True, stop=True)
                    else:
                        for t in range(TPC):
                            first = ((i - KQ) * TPC + t) * P
                            last = nc.tensor.matmul(ps[:, bank, t * P:(t + 1) * P], k.xnT[:, first:first + P],
                                                    w_all[:, 2, 0:2, :], start=True, stop=True)
                    last.then_inc(piece_done, 1)

                pe.wait_ge(k.a1_loaded, 96)
                for n in range(POWERS):
                    piece(n)
                    if n == 0:
                        pe.wait_ge(w_cut, 1)
                    else:
                        pe.wait_ge(power_left, n)
                    power(n)
                piece(POWERS)
                pe.wait_ge(filled, 3)
                pe.wait_ge(summed_rows, 1)
                nc.tensor.matmul(ps[:, 0, 0:2 * NP], halves_one[:], norm[:, 0:2 * NP], start=True, stop=True)\
                    .then_inc(summed_all, 1)
                for i in range(POWERS + 1, PIECES):
                    piece(i)

        probs = sb("probs", [P, PROBS, 2, CH])
        part_sum = sb("part_sum", [P, 2, 2, CH])
        weight_sum = sb("weight_sum", [P, 2, CH])
        wq_now, wk_now, wv_now = sb("wq_now", [M, P]), sb("wk_now", [M, P]), sb("wv_now", [M, P])
        x_now = sb("x_now", [M, CH])
        weighted = sb("weighted", [P, CH])
        inverse = sb("inverse", [P, CH])
        attended = sb("attended", [P, CH])
        running_max = sb("running_max", [P, CH])
        minus_max = sb("minus_max", [P, TPC])
        shift = sb("shift", [P, 2, TPC, P])

        v_out, q_hi, k_hi, q_lo, k_lo = sem("v_out"), sem("q_hi"), sem("k_hi"), sem("q_lo"), sem("k_lo")
        q_proj, k_proj, v_proj, staged = sem("q_proj"), sem("k_proj"), sem("v_proj"), sem("staged")
        score_done, exp_done, pv_done, summed = sem("score_done"), sem("exp_done"), sem("pv_done"), sem("summed")
        total_ready, acc_copied, sums_done, inverse_ready = (sem("total_ready"), sem("acc_copied"), sem("sums_done"),
                                                             sem("inverse_ready"))
        attended_ready, out_done, x_added = sem("attended_ready"), sem("out_done"), sem("x_added")
        max_score, max_taken, max_turned, max_read, shift_ready = (
            sem("max_score"), sem("max_taken"), sem("max_turned"), sem("max_read"), sem("shift_ready"))
        block = ctx.enter_context(nc.Block())

        def pairs(eng):
            with eng.Fori(0, NP // 2) as pp:
                for par in range(2):
                    with eng.Fori(0, NCH // 2) as half:
                        for odd in range(2):
                            pair = pp * 2 + par
                            qc = half * 2 + odd
                            yield pair, par, qc, odd, pair * NCH + qc

        def additions_over(t):
            return t + 1 if t < 2 else t - 1

        @block.gpsimd
        def _(pool):
            for pair, par, qc, odd, it in pairs(pool):
                pool.wait_ge(v_proj, it + 1)
                flat = w_all[:].rearrange("m w h e -> m w (h e)")
                nc.gpsimd.tensor_copy(wq_now[:], flat[:, 0, bass.ds((it + 1) // NCH % NP * P, P)])
                nc.gpsimd.tensor_copy(wk_now[:], flat[:, 1, bass.ds((pair + 1) % NP * P, P)])
                nc.gpsimd.tensor_copy(wv_now[:], flat[:, 2, bass.ds((pair + 1) % NP * P, P)])
                nc.gpsimd.tensor_copy(x_now[:], k.xnT[:, bass.ds(qc * CH, CH)]).then_inc(staged, 1)

        @block.scalar
        def _(act):
            act.sem_inc(exp_done, RING)
            for pair, par, qc, odd, it in pairs(act):
                for j in range(NT):
                    act.wait_ge(score_done, it * NT + (j + 1))
                    act.wait_ge(pv_done, it * NT + (j + 1))
                    taken = additions_over(j - PROBS) + ADDS if j >= PROBS else additions_over(NT + j - PROBS)
                    act.wait_ge(summed, it * ADDS + taken)
                    nc.scalar.activation(probs[:, j % PROBS, :, :], ps[:, 2 * (j % RING):2 * (j % RING) + 2, :],
                                         ACT.Exp, scale=SCALE).then_inc(exp_done, 1)
                    if j in (3, 4):
                        if j == 3:
                            act.wait_ge(q_proj, it + 1)
                        for dst, src in hi_halves(q_at(1 - odd), ps[:, QV, :], j - 3):
                            nc.scalar.activation(dst, src, ACT.Copy).then_inc(q_hi, 1)
                    if j in (6, 7):
                        if j == 6:
                            act.wait_ge(k_proj, it + 1)
                        dst, src = hi_halves(k_at(1 - par, qc * CH), ps[:, KB, :], 0)[j - 6]
                        nc.scalar.activation(dst, src, ACT.Copy).then_inc(k_hi, 1)
                    if j == 12:
                        act.wait_ge(v_proj, it + 2)
                        nc.scalar.activation(values[:, 1 - par, bass.ds(qc * TPC, TPC), :], ps[:, QV, :], ACT.Copy)\
                            .then_inc(v_out, 1)

        def dve_program(dve, guarded):
            def row_maxima(it):
                for n in range(2 * NT):
                    s, kt = n // NT, n % NT
                    dve.wait_ge(max_score, it * (2 * NT) + (n + 1))
                    if kt == 0:
                        ins = nc.vector.tensor_copy(running_max[:], ps[:, n % 2, :])
                    else:
                        ins = nc.vector.tensor_tensor(running_max[:], ps[:, n % 2, :], running_max[:], ALU.max)
                    ins.then_inc(max_taken, 1)
                    dve.wait_ge(max_taken, it * (2 * NT) + (n + 1 + RING))
                    if kt == NT - 1:
                        dve.wait_ge(max_turned, it * 2 + (s + 1))
                        nc.vector.tensor_reduce(minus_max[:], ps[:, 2, :].rearrange("p (i k) -> p i k", i=TPC),
                                                X_AXIS, ALU.max, negate=True).then_inc(max_read, 1)
                        dve.wait_ge(max_read, it * 2 + (s + 2))
                        for i in range(TPC):
                            ins = nc.vector.tensor_scalar(shift[:, s, i, :], k.ident[:], minus_max[:, i:i + 1], None,
                                                          ALU.mult)
                        ins.then_inc(shift_ready, 1)

            def take_weighted(n):
                dve.wait_ge(pv_done, n * NT + PROBS)
                nc.vector.tensor_copy(weighted[:], ps[:, ACC, :]).then_inc(acc_copied, 1)

            def divide(n):
                dve.wait_ge(sums_done, n)
                nc.vector.reciprocal(inverse[:], ps[:, EPI, :]).then_inc(inverse_ready, 1)
                dve.wait_ge(inverse_ready, n)
                nc.vector.tensor_tensor(attended[:], weighted[:], inverse[:], ALU.mult).then_inc(attended_ready, 1)

            def add_to_x(n, qc):
                dve.wait_ge(out_done, n)
                rows = k.x[:, bass.ds(qc * TPC, TPC), :]
                nc.vector.tensor_tensor(rows, rows, ps[:, EPI, :].rearrange("p (i m) -> p i m", m=M), ALU.add)\
                    .then_inc(x_added, 1)

            for pair, par, qc, odd, it in pairs(dve):
                if guarded:
                    row_maxima(it)
                dve.wait_ge(total_ready, it + 1)
                for j in range(2, NT):
                    dve.wait_ge(exp_done, it * NT + (j + 1 + RING))
                    if j < 4:
                        other = probs[:, (j - 2) % PROBS, :, :]
                    else:
                        dve.wait_ge(summed, it * ADDS + (ADDS + j - 3))
                        other = part_sum[:, j % 2, :, :]
                    nc.vector.tensor_tensor(part_sum[:, j % 2, :, :], probs[:, j % PROBS, :, :], other, ALU.add)\
                        .then_inc(summed, 1)
                    if j == 3 and not guarded:
                        with dve.If(it > 0):
                            divide(it)
                    if j in (5, 6):
                        dve.wait_ge(q_hi, it * 4 + (2 * j - 8))
                        for dst, src, hi in lo_halves(q_at(1 - odd), ps[:, QV, :], j - 5):
                            last = nc.vector.tensor_tensor(dst, src, hi.bitcast(F32), ALU.subtract)
                        if j == 6:
                            last.then_inc(q_lo, 1)
                    if j in (8, 9):
                        dve.wait_ge(k_hi, it * 2 + (j - 7))
                        dst, src, hi = lo_halves(k_at(1 - par, qc * CH), ps[:, KB, :], 0)[j - 8]
                        last = nc.vector.tensor_tensor(dst, src, hi.bitcast(F32), ALU.subtract)
                        if j == 9:
                            last.then_inc(k_lo, 1)
                    if j == 12 and not guarded:
                        with dve.If(it > 0):
                            add_to_x(it, (qc + NCH - 1) % NCH)
                dve.wait_ge(summed, it * ADDS + 2 * ADDS)
                nc.vector.tensor_tensor(weight_sum[:], part_sum[:, 0, :, :], part_sum[:, 1, :, :], ALU.add)\
                    .then_inc(total_ready, 1)
                take_weighted(it + 1)
                if guarded:
                    divide(it + 1)
                    add_to_x(it + 1, qc)
            if not guarded:
                divide(NI)
                add_to_x(NI, NCH - 1)

        @block.vector
        def _(dve):
            dve.sem_inc(max_taken, RING)
            dve.sem_inc(summed, ADDS)
            dve.sem_inc(total_ready, 1)
            is_safe = dve.value_load(safe[0:1, 0:1], min_val=0, max_val=1)
            with dve.If(is_safe == 1):
                dve_program(dve, guarded=False)
            with dve.Else():
                dve_program(dve, guarded=True)

        def pe_program(pe, guarded):
            def score(out, par, s, kt, odd, last):
                for order in range(2):
                    ins = nc.tensor.matmul(out, k_rows[:, par, s, kt * P:(kt + 1) * P], q_at(odd)(s, order),
                                           start=(order == 0), stop=(order == 1 and last))
                return ins

            def scores(it, par, odd, j):
                pe.wait_ge(exp_done, it * NT + (j + 1))
                for s in range(2):
                    bank = 2 * (j % RING) + s
                    ins = score(ps[:, bank, :], par, s, j, odd, not guarded)
                    if guarded:
                        ins = nc.tensor.matmul(ps[:, bank, :], k.ones[:], shift[:, s, :, :], start=False, stop=True)
                ins.then_inc(score_done, 1)

            def weigh(it, par, j):
                if j + RING >= NT:
                    pe.wait_ge(exp_done, it * NT + (j + 1 + RING))
                if j == 0:
                    pe.wait_ge(acc_copied, it + 1)
                for s in range(2):
                    last = nc.tensor.matmul(ps[D * s:D * (s + 1), ACC, :], values[:, par, j, D * s:D * (s + 1)],
                                            probs[:, j % PROBS, s, :], start=(j == 0), stop=(j == NT - 1))
                last.then_inc(pv_done, 1)

            def sums(n):
                pe.wait_ge(total_ready, n + 1)
                pe.wait_ge(x_added, n)
                for s in range(2):
                    last = nc.tensor.matmul(ps[D * s:D * (s + 1), EPI, :], k.ones[:, 0:D], weight_sum[:, s, :],
                                            start=True, stop=True)
                last.then_inc(sums_done, 1)

            def project(n, pair):
                pe.wait_ge(attended_ready, n)
                for i in range(TPC):
                    last = nc.tensor.matmul(ps[:, EPI, i * P:(i + 1) * P], attended[:, i * P:(i + 1) * P],
                                            wp[:].rearrange("p g m -> p (g m)")[:, bass.ds(pair * M, M)],
                                            start=True, stop=True)
                last.then_inc(out_done, 1)

            def row_maxima(it, par, odd):
                pe.wait_ge(exp_done, it * NT + RING)
                for n in range(2 * NT):
                    s, kt = n // NT, n % NT
                    pe.wait_ge(max_taken, it * (2 * NT) + (n + 1))
                    score(ps[:, n % 2, :], par, s, kt, odd, True).then_inc(max_score, 1)
                    if kt == NT - 1:
                        pe.wait_ge(max_taken, it * (2 * NT) + (n + 1 + RING))
                        pe.wait_ge(max_read, it * 2 + (s + 1))
                        for i in range(TPC):
                            last = nc.tensor.transpose(ps[:, 2, i * P:(i + 1) * P], running_max[:, i * P:(i + 1) * P],
                                                       k.ident[:])
                        last.then_inc(max_turned, 1)
                pe.wait_ge(shift_ready, it * 2 + 2)

            def operands_ready(it):
                pe.wait_ge(q_lo, it + 1)
                pe.wait_ge(k_lo, it + 1)

            if not guarded:
                operands_ready(0)
                for j in range(RING):
                    scores(0, 0, 0, j)
            for pair, par, qc, odd, it in pairs(pe):
                pe.wait_ge(v_out, it + 1)
                if guarded:
                    operands_ready(it)
                    row_maxima(it, par, odd)
                    for j in range(RING):
                        scores(it, par, odd, j)
                for j in range(NT):
                    if j % RING == 0 and j + RING < NT:
                        for ahead in range(RING):
                            scores(it, par, odd, j + RING + ahead)
                    if j + RING == NT and not guarded:
                        operands_ready(it + 1)
                        if odd == 0:
                            for first in range(RING):
                                scores(it + 1, par, 1, first)
                        else:
                            with pe.If(qc < NCH - 1):
                                for first in range(RING):
                                    scores(it + 1, par, 0, first)
                            with pe.Else():
                                for first in range(RING):
                                    scores(it + 1, 1 - par, 0, first)
                    weigh(it, par, j)
                    if j == 1:
                        pe.wait_ge(staged, it + 1)
                        nc.tensor.matmul(ps[:, QV, :], wq_now[:], k.xnT[:, bass.ds((qc + 1) % NCH * CH, CH)],
                                         start=True, stop=True).then_inc(q_proj, 1)
                    if j == 3 and not guarded:
                        with pe.If(it > 0):
                            sums(it)
                    if j == 4:
                        nc.tensor.matmul(ps[:, KB, :], wk_now[:], x_now[:], start=True, stop=True).then_inc(k_proj, 1)
                    if j == 9 and not guarded:
                        with pe.If(it > 0):
                            project(it, (it + NI - 1) // NCH % NP)
                    if j == 10:
                        pe.wait_ge(q_lo, it + 2)
                        for i in range(TPC):
                            last = nc.tensor.matmul(ps[:, QV, i * P:(i + 1) * P], x_now[:, i * P:(i + 1) * P],
                                                    wv_now[:], start=True, stop=True)
                        last.then_inc(v_proj, 1)
                if guarded:
                    sums(it + 1)
                    project(it + 1, pair)
            if not guarded:
                sums(NI)
                project(NI, NP - 1)

        @block.tensor
        def _(pe):
            pe.sem_inc(pv_done, PROBS)
            for ahead in (x_added, acc_copied, max_read, v_proj, q_lo, k_lo, v_out):
                pe.sem_inc(ahead, 1)
            is_safe = pe.value_load(safe[0:1, 0:1], min_val=0, max_val=1)
            with pe.If(is_safe == 1):
                pe_program(pe, guarded=False)
            with pe.Else():
                pe_program(pe, guarded=True)


def macaron(nc, dram):
    with ExitStack() as ctx:
        k = Kernel(nc, ctx, dram)

        def run(*stages):
            for stage in stages:
                with nc.cleanup_on_exit():
                    stage(k)

        run(constants, lambda k: moe_top1(k, "a", load_weights, k.x_loaded), attention_small, lambda k: moe_top1(k, "b"))
        k.top1_weights.close()
        k.place_attention_weights(ctx)
        run(lambda k: moe_top2(k, "c", load_attention_weights, has_stats=True), attention_wide, lambda k: moe_top2(k, "d", store=True))


INPUTS = {
    "x": "L0_attn_x",
    "t1_wg": "L0_ffn_wg", "t1_w1": "L0_ffn_w1", "t1_b1": "L0_ffn_b1", "t1_w2": "L0_ffn_w2", "t1_b2": "L0_ffn_b2",
    "a0_wk": "L0_attn_Wk", "a0_wq": "L0_attn_Wq", "a0_wo": "L0_attn_Wo", "a0_bo": "L0_attn_bo",
    "t2_router": "L1_ffn_router_w", "t2_w1": "L1_ffn_w1", "t2_w2": "L1_ffn_w2",
    "a1_wq": "L1_attn_Wq", "a1_wk": "L1_attn_Wk", "a1_wv": "L1_attn_Wv", "a1_wp": "L1_attn_Wp", "a1_bp": "L1_attn_bp",
}


def kernel(**inputs):
    import numpy as np
    import concourse.bacc as bacc
    from concourse.bass_utils import run_bass_kernel_spmd

    nc = bacc.Bacc("TRN2", target_bir_lowering=False, num_devices=1)
    arrays, dram = {}, {}
    for short, name in INPUTS.items():
        a = np.asarray(inputs[name])
        a = np.ascontiguousarray(a.T if short == "t2_router" else a)
        arrays[f"in_{name}_dram"] = a
        dram[short] = nc.dram_tensor(f"in_{name}_dram", a.shape, mybir.dt.from_np(a.dtype), kind="ExternalInput").ap()
    dram["out"] = nc.dram_tensor("out_0_dram", (1, S, M), F32, kind="ExternalOutput").ap()
    macaron(nc, dram)
    r = run_bass_kernel_spmd(nc, [arrays], core_ids=[0])
    return r.results[0]["out_0_dram"]
```
